# Optimizing a Trainium2 kernel written in Bass

```python
import numpy as np
import jax
import jax.numpy as jnp

def _softmax(x, axis=-1):
    return jax.nn.softmax(x, axis=axis)

def _gelu(x):
    return jax.nn.gelu(x, approximate=True)

def _silu(x):
    return jax.nn.silu(x)

def _sigmoid(x):
    return jax.nn.sigmoid(x)

def _layernorm(x, axis=-1, eps=1e-05):
    m = jnp.mean(x, axis=axis, keepdims=True)
    v = jnp.var(x, axis=axis, keepdims=True)
    return (x - m) / jnp.sqrt(v + eps)

def _scatter_add(tgt, idx, src, axis=0):
    return tgt.at[idx].add(src)

def _segment_sum(src, seg, n):
    return jax.ops.segment_sum(src, seg, n)
kernel_name = 'mk_decoder_postln_d2_seqx_r8_c2570c'

def setup_inputs(seed: int=0):
    np.random.seed(seed)
    _w = jnp.asarray

    def _rec_inputs():
        import jax
        import jax.numpy as jnp
        _rk = jax.random.key(seed)
        x = -1.394e-06 + 0.9999 * jax.random.normal(jax.random.fold_in(_rk, 1), (32, 56, 128), jnp.float32)
        _lenS = 56 - jax.random.randint(jax.random.fold_in(_rk, 7), (32,), 0, max(1, 56 // 4) + 1, jnp.int32)
        _lenS2 = 1500 - jax.random.randint(jax.random.fold_in(_rk, 8), (32,), 0, max(1, 1500 // 4) + 1, jnp.int32)
        _ctx_1024P = jax.random.normal(jax.random.fold_in(_rk, 11), (32, 16, 128), jnp.float32)
        _ctx_1024c = jax.random.dirichlet(jax.random.fold_in(_rk, 511), 0.3 * jnp.ones((16,), jnp.float32), (32, 1500))
        _ctx_1024t = jnp.einsum('bsk,bkd->bsd', _ctx_1024c, _ctx_1024P)
        _ctx_1024t = _ctx_1024t * jax.lax.rsqrt(jnp.mean(jnp.square(_ctx_1024t)) + 1e-12) * 0.953939
        ctx_1024 = -0.000392918 + 0.999932 * (_ctx_1024t + 0.3 * jax.random.normal(jax.random.fold_in(_rk, 611), (32, 1500, 128), jnp.float32))
        _validS = jnp.arange(56)[None, :] < _lenS[:, None]
        _validS2 = jnp.arange(1500)[None, :] < _lenS2[:, None]
        _causal = jnp.tril(jnp.ones((56, 56), dtype=bool))
        mask_BxS2_bk0 = jnp.logical_not(jnp.broadcast_to(_validS2[:, :], (32, 1500)))
        return (x, ctx_1024, mask_BxS2_bk0)
    x, ctx_1024, mask_BxS2_bk0 = _rec_inputs()

    def _L0_attn_setup():
        import jax, jax.numpy as jnp
        import numpy as np
        LN_EPS = 1e-05

        def _ssm_scan(x_ssm, A, Bm, C, reverse):
            Bb, L, di = x_ssm.shape
            ds = Bm.shape[1]

            def step(h, x_t):
                h = jnp.clip(h * A[None] + x_t[:, :, None] * Bm[None], -10.0, 10.0)
                y = jnp.einsum('bid,id->bi', h, C)
                return (h, y)
            h0 = jnp.zeros((Bb, di, ds), x_ssm.dtype)
            _, ys = jax.lax.scan(step, h0, jnp.swapaxes(x_ssm, 0, 1), reverse=reverse)
            return jnp.swapaxes(ys, 0, 1)
        key = jax.random.key(seed)
        ks = jax.random.split(key, 6)
        B, L, D = (4, 256, 128)
        d_state, expand = (16, 2)
        d_inner = D * expand
        x = jax.random.normal(ks[0], (B, L, D), jnp.float32)
        in_proj_w = jax.random.normal(ks[1], (d_inner * 2, D), jnp.float32) * np.float32(1.0 / np.sqrt(D))
        A_log = jax.random.normal(ks[2], (d_inner, d_state), jnp.float32)
        B_mat = jax.random.normal(ks[3], (d_inner, d_state), jnp.float32) * np.float32(1.0 / np.sqrt(d_state))
        C_mat = jnp.full((d_inner, d_state), 0.01, jnp.float32)
        out_proj_w = jax.random.normal(ks[4], (D, d_inner), jnp.float32) * np.float32(1.0 / np.sqrt(d_inner))
        ln_w = jnp.ones((D,), jnp.float32)
        ln_b = jnp.zeros((D,), jnp.float32)
        return {'x': x, 'in_proj_w': in_proj_w, 'A_log': A_log, 'B_mat': B_mat, 'C_mat': C_mat, 'out_proj_w': out_proj_w, 'ln_w': ln_w, 'ln_b': ln_b}
    _L0_attn_all = _L0_attn_setup()
    _L0_attn_in = {k: v for k, v in _L0_attn_all.items() if k in ('in_proj_w', 'A_log', 'B_mat', 'C_mat', 'out_proj_w', 'ln_w', 'ln_b')}
    del _L0_attn_all

    def _L0_xattn_setup():
        import jax, jax.numpy as jnp
        import numpy as np
        DIM = 128
        DIM_LATENT = 128
        DIM_HEAD = 64
        INNER = max(DIM, DIM_LATENT)
        HEADS = INNER // DIM_HEAD
        SCALE = DIM_HEAD ** (-0.5)
        LN_EPS = 1e-05
        RMS_EPS = 1e-08

        def layernorm(x, g, b):
            mu = jnp.mean(x, axis=-1, keepdims=True)
            var = jnp.mean(jnp.square(x - mu), axis=-1, keepdims=True)
            return (x - mu) * jax.lax.rsqrt(var + LN_EPS) * g + b

        def rmsnorm(x, gamma):
            n = jnp.linalg.norm(x, axis=-1, keepdims=True) * x.shape[-1] ** (-0.5)
            return x / jnp.maximum(n, RMS_EPS) * gamma
        key = jax.random.key(seed)
        ks = jax.random.split(key, 8)
        b, n, nl = (8, 256, 64)
        x = jax.random.normal(ks[0], (b, n, DIM), dtype=jnp.float32)
        latents = jax.random.normal(ks[1], (b, nl, DIM_LATENT), dtype=jnp.float32)
        mask = jax.random.randint(ks[2], (b, n), 0, 2).astype(bool)
        init = lambda k, shape, fan_in: jax.random.normal(k, shape, jnp.float32) * fan_in ** (-0.5)
        return {'x': x, 'latents': latents, 'mask': mask, 'ln_x_g': jnp.ones((DIM,), jnp.float32), 'ln_x_b': jnp.zeros((DIM,), jnp.float32), 'ln_l_g': jnp.ones((DIM_LATENT,), jnp.float32), 'ln_l_b': jnp.zeros((DIM_LATENT,), jnp.float32), 'q_gamma': jnp.ones((DIM_HEAD,), jnp.float32), 'k_gamma': jnp.ones((DIM_HEAD,), jnp.float32), 'W_q': init(ks[3], (DIM_LATENT, INNER), DIM_LATENT), 'W_kv': init(ks[4], (DIM, 2 * INNER), DIM), 'W_out': init(ks[5], (INNER, DIM_LATENT), INNER), 'b_out': jnp.zeros((DIM_LATENT,), jnp.float32)}
    _L0_xattn_all = _L0_xattn_setup()
    _L0_xattn_in = {k: v for k, v in _L0_xattn_all.items() if k in ('ln_x_g', 'ln_x_b', 'ln_l_g', 'ln_l_b', 'q_gamma', 'k_gamma', 'W_q', 'W_kv', 'W_out', 'b_out')}
    del _L0_xattn_all

    def _L0_ffn_setup():
        import jax, jax.numpy as jnp
        import numpy as np
        TOP_K = 2
        key = jax.random.key(seed)
        k1, k2, k3, k4 = jax.random.split(key, 4)
        B, S, D = (2, 256, 128)
        E, W = (8, 128)
        x = jax.random.normal(k1, (B, S, D), dtype=jnp.float32)
        router_w = jax.random.normal(k2, (E, D), dtype=jnp.float32) * 0.02
        w1 = jax.random.normal(k3, (D, E * W), dtype=jnp.float32) * 0.02
        w2 = jax.random.normal(k4, (E * W, D), dtype=jnp.float32) * 0.02
        return {'x': x, 'router_w': router_w, 'w1': w1, 'w2': w2}
    _L0_ffn_all = _L0_ffn_setup()
    _L0_ffn_in = {k: v for k, v in _L0_ffn_all.items() if k in ('router_w', 'w1', 'w2')}
    del _L0_ffn_all

    def _L1_attn_setup():
        import jax, jax.numpy as jnp
        import numpy as np
        D_MODEL = 128
        INNER = 256
        D_STATE = 16
        D_CONV = 4
        DT_RANK = 64
        DT_MIN, DT_MAX = (0.001, 0.1)
        RMS_EPS = 1e-06

        def _causal_depthwise_conv1d(x, kernel, bias):
            channels = x.shape[-1]
            rhs = kernel[:, None, :]
            out = jax.lax.conv_general_dilated(lhs=x, rhs=rhs, window_strides=(1,), padding=[(kernel.shape[0] - 1, 0)], dimension_numbers=('NWC', 'WIO', 'NWC'), feature_group_count=channels)
            return out + bias[None, None, :]

        def _selective_scan(u, dt, b, c, a, d):
            da = jnp.exp(dt[..., None] * a)
            db = (dt * u)[..., None] * b[:, :, None, :]

            def step(h, inp):
                da_t, db_t, c_t = inp
                h = da_t * h + db_t
                y = jnp.einsum('bds,bs->bd', h, c_t)
                return (h, y)
            h0 = jnp.zeros((u.shape[0], u.shape[2], a.shape[1]), u.dtype)
            _, ys = jax.lax.scan(step, h0, (da.transpose(1, 0, 2, 3), db.transpose(1, 0, 2, 3), c.transpose(1, 0, 2)))
            return ys.transpose(1, 0, 2) + u * d
        key = jax.random.key(seed)
        ks = jax.random.split(key, 16)

        def lin(k, fan_in, shape):
            return jax.random.normal(k, shape, jnp.float32) / np.sqrt(fan_in)
        a_init = jnp.log(jnp.arange(1, D_STATE + 1, dtype=jnp.float32))
        return {'x': jax.random.normal(ks[0], (2, 256, D_MODEL), jnp.float32), 'norm_scale': jnp.ones((D_MODEL,), jnp.float32), 'in_proj_w': lin(ks[1], D_MODEL, (D_MODEL, 2 * INNER)), 'in_proj_b': jnp.zeros((2 * INNER,), jnp.float32), 'out_proj_w': lin(ks[2], INNER, (INNER, D_MODEL)), 'out_proj_b': jnp.zeros((D_MODEL,), jnp.float32), 'dt_in_w': lin(ks[3], INNER, (INNER, DT_RANK)), 'dt_in_b': jnp.zeros((DT_RANK,), jnp.float32), 'dt_out_w': lin(ks[4], DT_RANK, (DT_RANK, INNER)), 'dt_out_b': jnp.zeros((INNER,), jnp.float32), 'b_proj_w': lin(ks[5], INNER, (INNER, D_STATE)), 'b_proj_b': jnp.zeros((D_STATE,), jnp.float32), 'c_proj_w': lin(ks[6], INNER, (INNER, D_STATE)), 'c_proj_b': jnp.zeros((D_STATE,), jnp.float32), 'conv_kernel': jax.random.normal(ks[7], (D_CONV, INNER), jnp.float32) / np.sqrt(D_CONV), 'conv_bias': jnp.zeros((INNER,), jnp.float32), 'a_log': jnp.tile(a_init[None, :], (INNER, 1)), 'd': jnp.ones((INNER,), jnp.float32), 'dt_bias': jnp.zeros((INNER,), jnp.float32)}
    _L1_attn_all = _L1_attn_setup()
    _L1_attn_in = {k: v for k, v in _L1_attn_all.items() if k in ('norm_scale', 'in_proj_w', 'in_proj_b', 'out_proj_w', 'out_proj_b', 'dt_in_w', 'dt_in_b', 'dt_out_w', 'dt_out_b', 'b_proj_w', 'b_proj_b', 'c_proj_w', 'c_proj_b', 'conv_kernel', 'conv_bias', 'a_log', 'd', 'dt_bias')}
    del _L1_attn_all

    def _L1_xattn_setup():
        import jax, jax.numpy as jnp
        import numpy as np
        N_EMBD = 128
        N_HEAD = 16
        HEAD_DIM = N_EMBD // N_HEAD
        key = jax.random.key(seed)
        ks = jax.random.split(key, 8)
        B, T, T_ctx, C = (2, 256, 256, N_EMBD)
        s = 1.0 / np.sqrt(C)
        return {'x': jax.random.normal(ks[0], (B, T, C), dtype=jnp.float32), 'context': jax.random.normal(ks[1], (B, T_ctx, C), dtype=jnp.float32), 'Wq': jax.random.normal(ks[2], (C, C), dtype=jnp.float32) * s, 'bq': jnp.zeros((C,), dtype=jnp.float32), 'Wkv': jax.random.normal(ks[3], (C, 2 * C), dtype=jnp.float32) * s, 'bkv': jnp.zeros((2 * C,), dtype=jnp.float32), 'Wp': jax.random.normal(ks[4], (C, C), dtype=jnp.float32) * s, 'bp': jnp.zeros((C,), dtype=jnp.float32)}
    _L1_xattn_all = _L1_xattn_setup()
    _L1_xattn_in = {k: v for k, v in _L1_xattn_all.items() if k in ('Wq', 'bq', 'Wkv', 'bkv', 'Wp', 'bp')}
    del _L1_xattn_all

    def _L1_ffn_setup():
        import jax, jax.numpy as jnp
        import numpy as np
        H = 128
        I = 64
        E = 8
        TOPK = 2
        NGROUP = 4
        TOPKG = 2
        SCALE = 1.0
        B, S = (4, 128)

        def _gate(xf, gate_weight, bias):
            T = xf.shape[0]
            logits = xf @ gate_weight.T
            scores = jax.nn.sigmoid(logits)
            scores_for_choice = scores + bias[None, :]
            gsz = E // NGROUP
            grp = scores_for_choice.reshape(T, NGROUP, gsz)
            group_scores = jax.lax.top_k(grp, 2)[0].sum(-1)
            _, group_idx = jax.lax.top_k(group_scores, TOPKG)
            rows = jnp.arange(T)[:, None]
            group_mask = jnp.zeros((T, NGROUP), xf.dtype).at[rows, group_idx].set(1.0)
            score_mask = jnp.broadcast_to(group_mask[:, :, None], (T, NGROUP, gsz)).reshape(T, E)
            tmp_scores = jnp.where(score_mask > 0, scores_for_choice, 0.0)
            _, topk_idx = jax.lax.top_k(tmp_scores, TOPK)
            topk_weight = jnp.take_along_axis(scores, topk_idx, axis=1)
            if TOPK > 1:
                topk_weight = topk_weight / (topk_weight.sum(-1, keepdims=True) + 1e-20)
            topk_weight = topk_weight * SCALE
            return (topk_idx, topk_weight)
        key = jax.random.key(seed)
        k0, k1, k2, k3, k4 = jax.random.split(key, 5)
        return {'hidden_states': jax.random.normal(k0, (B, S, H), jnp.float32), 'gate_weight': jax.random.normal(k1, (E, H), jnp.float32) * (1.0 / np.sqrt(H)), 'e_score_correction_bias': jnp.zeros((E,), jnp.float32), 'gate_proj': jax.random.normal(k2, (E, I, H), jnp.float32) * 0.02, 'up_proj': jax.random.normal(k3, (E, I, H), jnp.float32) * 0.02, 'down_proj': jax.random.normal(k4, (E, H, I), jnp.float32) * 0.02}
    _L1_ffn_all = _L1_ffn_setup()
    _L1_ffn_in = {k: v for k, v in _L1_ffn_all.items() if k in ('gate_weight', 'e_score_correction_bias', 'gate_proj', 'up_proj', 'down_proj')}
    del _L1_ffn_all
    return {'x': x, 'ctx_1024': ctx_1024, 'mask_BxS2_bk0': mask_BxS2_bk0, 'L0_attn_in_proj_w': _L0_attn_in['in_proj_w'], 'L0_attn_A_log': _L0_attn_in['A_log'], 'L0_attn_B_mat': _L0_attn_in['B_mat'], 'L0_attn_C_mat': _L0_attn_in['C_mat'], 'L0_attn_out_proj_w': _L0_attn_in['out_proj_w'], 'L0_attn_ln_w': _L0_attn_in['ln_w'], 'L0_attn_ln_b': _L0_attn_in['ln_b'], 'L0_xattn_ln_x_g': _L0_xattn_in['ln_x_g'], 'L0_xattn_ln_x_b': _L0_xattn_in['ln_x_b'], 'L0_xattn_ln_l_g': _L0_xattn_in['ln_l_g'], 'L0_xattn_ln_l_b': _L0_xattn_in['ln_l_b'], 'L0_xattn_q_gamma': _L0_xattn_in['q_gamma'], 'L0_xattn_k_gamma': _L0_xattn_in['k_gamma'], 'L0_xattn_W_q': _L0_xattn_in['W_q'], 'L0_xattn_W_kv': _L0_xattn_in['W_kv'], 'L0_xattn_W_out': _L0_xattn_in['W_out'], 'L0_xattn_b_out': _L0_xattn_in['b_out'], 'L0_ffn_router_w': _L0_ffn_in['router_w'], 'L0_ffn_w1': _L0_ffn_in['w1'], 'L0_ffn_w2': _L0_ffn_in['w2'], 'L1_attn_norm_scale': _L1_attn_in['norm_scale'], 'L1_attn_in_proj_w': _L1_attn_in['in_proj_w'], 'L1_attn_in_proj_b': _L1_attn_in['in_proj_b'], 'L1_attn_out_proj_w': _L1_attn_in['out_proj_w'], 'L1_attn_out_proj_b': _L1_attn_in['out_proj_b'], 'L1_attn_dt_in_w': _L1_attn_in['dt_in_w'], 'L1_attn_dt_in_b': _L1_attn_in['dt_in_b'], 'L1_attn_dt_out_w': _L1_attn_in['dt_out_w'], 'L1_attn_dt_out_b': _L1_attn_in['dt_out_b'], 'L1_attn_b_proj_w': _L1_attn_in['b_proj_w'], 'L1_attn_b_proj_b': _L1_attn_in['b_proj_b'], 'L1_attn_c_proj_w': _L1_attn_in['c_proj_w'], 'L1_attn_c_proj_b': _L1_attn_in['c_proj_b'], 'L1_attn_conv_kernel': _L1_attn_in['conv_kernel'], 'L1_attn_conv_bias': _L1_attn_in['conv_bias'], 'L1_attn_a_log': _L1_attn_in['a_log'], 'L1_attn_d': _L1_attn_in['d'], 'L1_attn_dt_bias': _L1_attn_in['dt_bias'], 'L1_xattn_Wq': _L1_xattn_in['Wq'], 'L1_xattn_bq': _L1_xattn_in['bq'], 'L1_xattn_Wkv': _L1_xattn_in['Wkv'], 'L1_xattn_bkv': _L1_xattn_in['bkv'], 'L1_xattn_Wp': _L1_xattn_in['Wp'], 'L1_xattn_bp': _L1_xattn_in['bp'], 'L1_ffn_gate_weight': _L1_ffn_in['gate_weight'], 'L1_ffn_e_score_correction_bias': _L1_ffn_in['e_score_correction_bias'], 'L1_ffn_gate_proj': _L1_ffn_in['gate_proj'], 'L1_ffn_up_proj': _L1_ffn_in['up_proj'], 'L1_ffn_down_proj': _L1_ffn_in['down_proj']}

def reference(x, ctx_1024, mask_BxS2_bk0, L0_attn_in_proj_w, L0_attn_A_log, L0_attn_B_mat, L0_attn_C_mat, L0_attn_out_proj_w, L0_attn_ln_w, L0_attn_ln_b, L0_xattn_ln_x_g, L0_xattn_ln_x_b, L0_xattn_ln_l_g, L0_xattn_ln_l_b, L0_xattn_q_gamma, L0_xattn_k_gamma, L0_xattn_W_q, L0_xattn_W_kv, L0_xattn_W_out, L0_xattn_b_out, L0_ffn_router_w, L0_ffn_w1, L0_ffn_w2, L1_attn_norm_scale, L1_attn_in_proj_w, L1_attn_in_proj_b, L1_attn_out_proj_w, L1_attn_out_proj_b, L1_attn_dt_in_w, L1_attn_dt_in_b, L1_attn_dt_out_w, L1_attn_dt_out_b, L1_attn_b_proj_w, L1_attn_b_proj_b, L1_attn_c_proj_w, L1_attn_c_proj_b, L1_attn_conv_kernel, L1_attn_conv_bias, L1_attn_a_log, L1_attn_d, L1_attn_dt_bias, L1_xattn_Wq, L1_xattn_bq, L1_xattn_Wkv, L1_xattn_bkv, L1_xattn_Wp, L1_xattn_bp, L1_ffn_gate_weight, L1_ffn_e_score_correction_bias, L1_ffn_gate_proj, L1_ffn_up_proj, L1_ffn_down_proj):
    import jax
    import jax.numpy as jnp

    def _L0_attn_ref(x, in_proj_w, A_log, B_mat, C_mat, out_proj_w, ln_w, ln_b):
        import jax, jax.numpy as jnp
        import numpy as np
        LN_EPS = 1e-05

        def _ssm_scan(x_ssm, A, Bm, C, reverse):
            Bb, L, di = x_ssm.shape
            ds = Bm.shape[1]

            def step(h, x_t):
                h = jnp.clip(h * A[None] + x_t[:, :, None] * Bm[None], -10.0, 10.0)
                y = jnp.einsum('bid,id->bi', h, C)
                return (h, y)
            h0 = jnp.zeros((Bb, di, ds), x_ssm.dtype)
            _, ys = jax.lax.scan(step, h0, jnp.swapaxes(x_ssm, 0, 1), reverse=reverse)
            return jnp.swapaxes(ys, 0, 1)
        mu = jnp.mean(x, axis=-1, keepdims=True)
        var = jnp.mean((x - mu) ** 2, axis=-1, keepdims=True)
        xn = (x - mu) * jax.lax.rsqrt(var + LN_EPS) * ln_w + ln_b
        x_proj = jnp.einsum('bld,ed->ble', xn, in_proj_w)
        x_ssm, gate = jnp.split(x_proj, 2, axis=-1)
        A = -jnp.clip(jnp.exp(A_log), -10.0, -0.01)
        out_f = _ssm_scan(x_ssm, A, B_mat, C_mat, reverse=False)
        out_b = _ssm_scan(x_ssm, A, B_mat, C_mat, reverse=True)
        out = (out_f + out_b) * 0.5 * jax.nn.silu(gate)
        return jnp.einsum('bli,di->bld', out, out_proj_w)

    def _L0_xattn_ref(x, latents, mask, ln_x_g, ln_x_b, ln_l_g, ln_l_b, q_gamma, k_gamma, W_q, W_kv, W_out, b_out):
        import jax, jax.numpy as jnp
        import numpy as np
        DIM = 128
        DIM_LATENT = 128
        DIM_HEAD = 64
        INNER = max(DIM, DIM_LATENT)
        HEADS = INNER // DIM_HEAD
        SCALE = DIM_HEAD ** (-0.5)
        LN_EPS = 1e-05
        RMS_EPS = 1e-08

        def layernorm(x, g, b):
            mu = jnp.mean(x, axis=-1, keepdims=True)
            var = jnp.mean(jnp.square(x - mu), axis=-1, keepdims=True)
            return (x - mu) * jax.lax.rsqrt(var + LN_EPS) * g + b

        def rmsnorm(x, gamma):
            n = jnp.linalg.norm(x, axis=-1, keepdims=True) * x.shape[-1] ** (-0.5)
            return x / jnp.maximum(n, RMS_EPS) * gamma
        b, n, _ = x.shape
        nl = latents.shape[1]
        xn = layernorm(x, ln_x_g, ln_x_b)
        ln = layernorm(latents, ln_l_g, ln_l_b)
        q = ln @ W_q
        kv = jnp.concatenate([xn @ W_kv, ln @ W_kv], axis=1)
        k, v = (kv[..., :INNER], kv[..., INNER:])
        to_heads = lambda t: t.reshape(t.shape[0], t.shape[1], HEADS, DIM_HEAD).transpose(0, 2, 1, 3)
        q, k, v = (to_heads(q), to_heads(k), to_heads(v))
        qn = rmsnorm(q, q_gamma) * SCALE
        kn = rmsnorm(k, k_gamma)
        sim = jnp.einsum('bhid,bhjd->bhij', qn, kn)
        full_mask = jnp.pad(mask, ((0, 0), (0, nl)), constant_values=True)
        neg = -jnp.finfo(sim.dtype).max
        sim = jnp.where(full_mask[:, None, None, :], sim, neg)
        attn = jax.nn.softmax(sim.astype(jnp.float32), axis=-1).astype(sim.dtype)
        out = jnp.einsum('bhij,bhjd->bhid', attn, v)
        out = out.transpose(0, 2, 1, 3).reshape(b, nl, INNER)
        return out @ W_out + b_out

    def _L0_ffn_ref(x, router_w, w1, w2):
        import jax, jax.numpy as jnp
        import numpy as np
        TOP_K = 2
        B, S, D = x.shape
        E = router_w.shape[0]
        W = w1.shape[1] // E
        T = B * S
        xf = x.reshape(T, D)
        router_logits = jnp.einsum('td,ed->te', xf, router_w)
        router_probs = jax.nn.sigmoid(router_logits.astype(jnp.float32))
        top_w, sel = jax.lax.top_k(router_probs, TOP_K)
        top_w = top_w / (top_w.sum(axis=-1, keepdims=True) + 1e-20)
        top_w = top_w.astype(x.dtype)
        W1e = w1.reshape(D, E, W).transpose(1, 0, 2)
        W2e = w2.reshape(E, W, D)
        h = jnp.einsum('td,edw->etw', xf, W1e)
        a = jnp.square(jax.nn.relu(h))
        y = jnp.einsum('etw,ewd->etd', a, W2e)
        cw = jnp.zeros((T, E), dtype=x.dtype).at[jnp.arange(T)[:, None], sel].set(top_w)
        out = jnp.einsum('etd,te->td', y, cw)
        return out.reshape(B, S, D)

    def _L1_attn_ref(x, norm_scale, in_proj_w, in_proj_b, out_proj_w, out_proj_b, dt_in_w, dt_in_b, dt_out_w, dt_out_b, b_proj_w, b_proj_b, c_proj_w, c_proj_b, conv_kernel, conv_bias, a_log, d, dt_bias):
        import jax, jax.numpy as jnp
        import numpy as np
        D_MODEL = 128
        INNER = 256
        D_STATE = 16
        D_CONV = 4
        DT_RANK = 64
        DT_MIN, DT_MAX = (0.001, 0.1)
        RMS_EPS = 1e-06

        def _causal_depthwise_conv1d(x, kernel, bias):
            channels = x.shape[-1]
            rhs = kernel[:, None, :]
            out = jax.lax.conv_general_dilated(lhs=x, rhs=rhs, window_strides=(1,), padding=[(kernel.shape[0] - 1, 0)], dimension_numbers=('NWC', 'WIO', 'NWC'), feature_group_count=channels)
            return out + bias[None, None, :]

        def _selective_scan(u, dt, b, c, a, d):
            da = jnp.exp(dt[..., None] * a)
            db = (dt * u)[..., None] * b[:, :, None, :]

            def step(h, inp):
                da_t, db_t, c_t = inp
                h = da_t * h + db_t
                y = jnp.einsum('bds,bs->bd', h, c_t)
                return (h, y)
            h0 = jnp.zeros((u.shape[0], u.shape[2], a.shape[1]), u.dtype)
            _, ys = jax.lax.scan(step, h0, (da.transpose(1, 0, 2, 3), db.transpose(1, 0, 2, 3), c.transpose(1, 0, 2)))
            return ys.transpose(1, 0, 2) + u * d
        residual = x
        var = jnp.mean(jnp.square(x), axis=-1, keepdims=True)
        xn = x * jax.lax.rsqrt(var + RMS_EPS) * norm_scale
        uz = xn @ in_proj_w + in_proj_b
        u, z = jnp.split(uz, 2, axis=-1)
        u = _causal_depthwise_conv1d(u, conv_kernel, conv_bias)
        u = jax.nn.silu(u)
        dt = (u @ dt_in_w + dt_in_b) @ dt_out_w + dt_out_b + dt_bias
        dt = jnp.clip(jax.nn.softplus(dt), DT_MIN, DT_MAX)
        b = jnp.tanh(u @ b_proj_w + b_proj_b)
        c = jnp.tanh(u @ c_proj_w + c_proj_b)
        a = -jnp.exp(a_log)
        y = _selective_scan(u, dt, b, c, a, d)
        y = y * jax.nn.silu(z)
        y = y @ out_proj_w + out_proj_b
        return residual + y

    def _L1_xattn_ref(x, context, Wq, bq, Wkv, bkv, Wp, bp):
        import jax, jax.numpy as jnp
        import numpy as np
        N_EMBD = 128
        N_HEAD = 16
        HEAD_DIM = N_EMBD // N_HEAD
        B, T, C = x.shape
        T_ctx = context.shape[1]
        H, D = (N_HEAD, C // N_HEAD)
        q = (x @ Wq + bq).reshape(B, T, H, D).transpose(0, 2, 1, 3)
        kv = context @ Wkv + bkv
        k, v = jnp.split(kv, 2, axis=-1)
        k = k.reshape(B, T_ctx, H, D).transpose(0, 2, 1, 3)
        v = v.reshape(B, T_ctx, H, D).transpose(0, 2, 1, 3)
        att = jnp.einsum('bhtd,bhsd->bhts', q, k) * (1.0 / jnp.sqrt(jnp.asarray(D, q.dtype)))
        causal = jnp.arange(T)[:, None] >= jnp.arange(T_ctx)[None, :]
        att = jnp.where(causal[None, None], att, jnp.asarray(-jnp.inf, att.dtype))
        att = jax.nn.softmax(att, axis=-1)
        y = jnp.einsum('bhts,bhsd->bhtd', att, v)
        y = y.transpose(0, 2, 1, 3).reshape(B, T, C)
        return y @ Wp + bp

    def _L1_ffn_ref(hidden_states, gate_weight, e_score_correction_bias, gate_proj, up_proj, down_proj):
        import jax, jax.numpy as jnp
        import numpy as np
        H = 128
        I = 64
        E = 8
        TOPK = 2
        NGROUP = 4
        TOPKG = 2
        SCALE = 1.0
        B, S = (4, 128)

        def _gate(xf, gate_weight, bias):
            T = xf.shape[0]
            logits = xf @ gate_weight.T
            scores = jax.nn.sigmoid(logits)
            scores_for_choice = scores + bias[None, :]
            gsz = E // NGROUP
            grp = scores_for_choice.reshape(T, NGROUP, gsz)
            group_scores = jax.lax.top_k(grp, 2)[0].sum(-1)
            _, group_idx = jax.lax.top_k(group_scores, TOPKG)
            rows = jnp.arange(T)[:, None]
            group_mask = jnp.zeros((T, NGROUP), xf.dtype).at[rows, group_idx].set(1.0)
            score_mask = jnp.broadcast_to(group_mask[:, :, None], (T, NGROUP, gsz)).reshape(T, E)
            tmp_scores = jnp.where(score_mask > 0, scores_for_choice, 0.0)
            _, topk_idx = jax.lax.top_k(tmp_scores, TOPK)
            topk_weight = jnp.take_along_axis(scores, topk_idx, axis=1)
            if TOPK > 1:
                topk_weight = topk_weight / (topk_weight.sum(-1, keepdims=True) + 1e-20)
            topk_weight = topk_weight * SCALE
            return (topk_idx, topk_weight)
        Bv, Sv, Hv = hidden_states.shape
        xf = hidden_states.reshape(-1, Hv).astype(jnp.float32)
        topk_idx, topk_weight = _gate(xf, gate_weight.astype(jnp.float32), e_score_correction_bias.astype(jnp.float32))
        y = jnp.zeros_like(xf)
        for e in range(E):
            combine_w = jnp.where(topk_idx == e, topk_weight, 0.0).sum(-1)
            g = xf @ gate_proj[e].T
            u = xf @ up_proj[e].T
            o = jax.nn.silu(g) * u @ down_proj[e].T
            y = y + combine_w[:, None] * o
        return y.reshape(Bv, Sv, Hv)
    x = _layernorm(x + _L0_attn_ref(x, L0_attn_in_proj_w, L0_attn_A_log, L0_attn_B_mat, L0_attn_C_mat, L0_attn_out_proj_w, L0_attn_ln_w, L0_attn_ln_b), axis=-1)
    x = _layernorm(x + _L0_xattn_ref(ctx_1024, x, mask_BxS2_bk0, L0_xattn_ln_x_g, L0_xattn_ln_x_b, L0_xattn_ln_l_g, L0_xattn_ln_l_b, L0_xattn_q_gamma, L0_xattn_k_gamma, L0_xattn_W_q, L0_xattn_W_kv, L0_xattn_W_out, L0_xattn_b_out), axis=-1)
    x = _layernorm(x + _L0_ffn_ref(x, L0_ffn_router_w, L0_ffn_w1, L0_ffn_w2), axis=-1)
    x = _layernorm(x + _L1_attn_ref(x, L1_attn_norm_scale, L1_attn_in_proj_w, L1_attn_in_proj_b, L1_attn_out_proj_w, L1_attn_out_proj_b, L1_attn_dt_in_w, L1_attn_dt_in_b, L1_attn_dt_out_w, L1_attn_dt_out_b, L1_attn_b_proj_w, L1_attn_b_proj_b, L1_attn_c_proj_w, L1_attn_c_proj_b, L1_attn_conv_kernel, L1_attn_conv_bias, L1_attn_a_log, L1_attn_d, L1_attn_dt_bias), axis=-1)
    x = _layernorm(x + _L1_xattn_ref(x, ctx_1024, L1_xattn_Wq, L1_xattn_bq, L1_xattn_Wkv, L1_xattn_bkv, L1_xattn_Wp, L1_xattn_bp), axis=-1)
    x = _layernorm(x + _L1_ffn_ref(x, L1_ffn_gate_weight, L1_ffn_e_score_correction_bias, L1_ffn_gate_proj, L1_ffn_up_proj, L1_ffn_down_proj), axis=-1)
    return x

_drawn_inputs = setup_inputs


def setup_inputs(seed=0):
    import zlib

    import numpy as np

    out = dict(_drawn_inputs(seed))
    spreads = {'L0_attn_C_mat': (0.009999999776482582, 0.6),
     'L0_attn_ln_w': (1.0, 0.6),
     'L0_attn_ln_b': (0.0, 0.8),
     'L0_xattn_ln_x_g': (1.0, 0.2),
     'L0_xattn_ln_x_b': (0.0, 0.1),
     'L0_xattn_ln_l_g': (1.0, 0.2),
     'L0_xattn_ln_l_b': (0.0, 0.1),
     'L0_xattn_q_gamma': (1.0, 0.2),
     'L0_xattn_k_gamma': (1.0, 0.2),
     'L0_xattn_b_out': (0.0, 0.1),
     'L1_attn_norm_scale': (1.0, 0.2),
     'L1_attn_in_proj_b': (0.0, 0.316),
     'L1_attn_out_proj_b': (0.0, 0.1),
     'L1_attn_dt_in_b': (0.0, 0.8),
     'L1_attn_dt_out_b': (0.0, 2.0),
     'L1_attn_b_proj_b': (0.0, 0.8),
     'L1_attn_c_proj_b': (0.0, 0.8),
     'L1_attn_conv_bias': (0.0, 0.447),
     'L1_attn_d': (1.0, 0.2),
     'L1_attn_dt_bias': (0.0, 2.0),
     'L1_xattn_bq': (0.0, 0.37),
     'L1_xattn_bkv': (0.0, 0.1),
     'L1_xattn_bp': (0.0, 0.1),
     'L1_ffn_e_score_correction_bias': (0.0, 0.8)}
    factors = {'L0_attn_in_proj_w': 8.0,
     'L0_attn_B_mat': 8.0,
     'L0_attn_out_proj_w': 8.0,
     'L0_ffn_router_w': 7.373,
     'L0_ffn_w1': 7.018,
     'L0_ffn_w2': 6.464,
     'L1_attn_dt_in_w': 8.0,
     'L1_attn_dt_out_w': 8.0,
     'L1_attn_a_log': 4.168,
     'L1_ffn_gate_weight': 8.0,
     'L1_ffn_gate_proj': 8.0,
     'L1_ffn_up_proj': 8.0,
     'L1_ffn_down_proj': 8.0}
    for name, (base, spread) in spreads.items():
        noise = np.random.default_rng([zlib.crc32(name.encode()), seed]).standard_normal(out[name].shape)
        drawn = base * np.exp(spread * noise) if base else spread * noise
        out[name] = jnp.asarray(drawn.astype(out[name].dtype))
    for name, factor in factors.items():
        out[name] = (out[name] * factor).astype(out[name].dtype)
    return out
```

```python
from contextlib import ExitStack, contextmanager

import numpy as np

import concourse.bass as bass
from concourse import mybir

ALU = mybir.AluOpType
ACT = mybir.ActivationFunctionType
F32 = mybir.dt.float32
BF16 = mybir.dt.bfloat16
U8 = mybir.dt.uint8
AX = mybir.AxisListType.X
RMAX = bass.bass_isa.ReduceOp.max

P = 128
B, L, D = 32, 56, 128
T = B * L
T2 = 2 * L
NT = T // T2
NC = 4
CH = T // NC
BC = B // NC
TPC = NT // NC
INNER = 256
DS = 16
S2 = 1500
KP = 125
KT = S2 // KP
E = 8
NEG = -(2.0 ** 100)
LN_EPS = 1e-5


class Counted:

    def __init__(self, sem):
        self.sem, self.base = sem, 0

    def __call__(self, count):
        return self.base + count


def wait_apart(eng, sem, count, spare):
    eng.wait_ge(sem, count)
    eng.sem_inc(spare)


class Core:

    def __init__(self, nc, dram, out, ctx):
        self.nc, self.dram, self.out, self.ctx = nc, dram, out, ctx
        self.counted = {}

    def sb(self, name, shape, dt=F32):
        return self.ctx.enter_context(self.nc.sbuf_tensor(name, shape, dt))

    def sem(self, name):
        return self.ctx.enter_context(self.nc.semaphore(name))

    def shared(self, name):
        if name not in self.counted:
            self.counted[name] = Counted(self.sem(name))
        return self.counted[name]


@contextmanager
def scope(core, stage):
    with ExitStack() as ctx:
        def sb(name, shape, dt=F32):
            return ctx.enter_context(core.nc.sbuf_tensor(f"{stage}_{name}", shape, dt))

        def psum(name, shape, dt=F32):
            return ctx.enter_context(core.nc.psum_tensor(f"{stage}_{name}", shape, dt))

        yield sb, psum


LN_EXP_TABLES = 6


def load_tables(nc, act, tables):
    act.add_instruction(mybir.InstLoadActFuncSet(act_func_set_id=tables, name=nc.get_next_instruction_name()))


def over(ap, shape):
    return ap.broadcast_to(shape)


def stage_constants(core):
    nc = core.nc
    core.ident = core.sb("ident", [P, P])
    core.ones = core.sb("ones", [P, P])
    core.eps_ln = core.sb("eps_ln", [P, 1])
    core.eps_rms = core.sb("eps_rms", [P, 1])
    core.selector = core.sb("selector", [96, 32, P], BF16)
    core.x_tm = core.sb("x_tm", [T2, NT, D])
    core.xT = core.sb("xT", [D, T])
    zeroed, loaded = core.sem("const_zeroed"), core.sem("const_loaded")
    with nc.Block() as block:
        @block.gpsimd
        def _(pool):
            pool.memset(core.ident[:, :], 0.0).then_inc(zeroed, 1)
            pool.memset(core.selector[:, :, :], 0.0).then_inc(zeroed, 1)
            pool.memset(core.ones[:, :], 1.0)
            pool.memset(core.eps_ln[:, :], LN_EPS)
            pool.memset(core.eps_rms[:, :], 1e-6)
            pool.wait_ge(zeroed, 1)
            pool.affine_select(out=core.ident[:, :], in_=core.ident[:, :], compare_op=ALU.not_equal,
                               fill=1.0, base=0, pattern=[[-1, P]], channel_multiplier=1)
            pool.wait_ge(zeroed, 2)
            for part in range(3):
                pool.affine_select(out=core.selector[:, :, :], in_=core.selector[:, :, :],
                                   compare_op=ALU.not_equal, fill=1.0, base=-32 * part,
                                   pattern=[[-1, 32], [0, P]], channel_multiplier=1).then_inc(zeroed, 1)
                pool.wait_ge(zeroed, 3 + part)

        @block.sync
        def _(sp):
            sp.dma_start(core.x_tm[:, :, :], core.dram["x"].rearrange("b t d -> (b t) d")
                         .rearrange("(n p) d -> p n d", p=T2)).then_inc(loaded, 16)
            sp.wait_ge(loaded, 16)


def stage_norm(core, name, project=None, factor=1.0, rms=False, gain=None, shift=None,
               residual=True, outT=None, final=False):
    nc = core.nc
    projected, added, stats, moments = (core.shared(s) for s in ("n_proj", "n_add", "n_stats", "n_moments"))
    roots, scales, normed, turned, kept = (core.shared(s) for s in ("n_roots", "n_scales", "n_normed", "n_turned", "n_kept"))
    squared = core.shared("n_squared")
    with scope(core, name) as (sb, psum):
        y = psum("y", [P, NC, 512]) if project else None
        xt = psum("xt", [P, NC, 512]) if outT else None
        z = sb("z", [T2, NT, D]) if project else core.x_tm
        keep = core.x_tm if residual else sb("keep", [T2, NT, D])
        raw = sb("raw", [T2, NT, 6])
        mv = sb("mv", [T2, NT, 2])
        std = sb("std", [T2, NT])
        rstd = sb("rstd", [T2, NT])
        offset = sb("offset", [T2, NT])
        with nc.Block() as block:
            @block.tensor
            def _(pe):
                if project:
                    for c in range(NC):
                        for n in range(c * TPC, (c + 1) * TPC):
                            r = n % TPC
                            last = project(pe, n, y[0:T2, c, r * D:(r + 1) * D])
                        last.then_inc(projected.sem, 1)
                if outT:
                    for c in range(NC):
                        pe.wait_ge(normed.sem, normed(c + 1))
                        for r in range(TPC):
                            last = pe.transpose(xt[:, c, r * T2:(r + 1) * T2], keep[:, c * TPC + r, :],
                                                core.ident[0:T2, 0:T2])
                        last.then_inc(turned.sem, 1)

            @block.vector
            def _(ve):
                for c in range(NC):
                    tiles = slice(c * TPC, (c + 1) * TPC)
                    if project:
                        ve.wait_ge(projected.sem, projected(c + 1))
                        ve.scalar_tensor_tensor(z[:, tiles, :], core.x_tm[:, tiles, :], factor,
                                                y[0:T2, c, :].rearrange("p (r d) -> p r d", d=D),
                                                ALU.mult, ALU.add).then_inc(added.sem, 1)
                        ve.wait_ge(added.sem, added(c + 1))
                    for n in range(c * TPC, (c + 1) * TPC):
                        last = ve.bn_stats(raw[:, n, :], z[:, n, :])
                    last.then_inc(stats.sem, 1)
                    ve.wait_ge(stats.sem, stats(c + 1))
                    for n in range(c * TPC, (c + 1) * TPC):
                        last = ve.bn_aggr(mv[:, n, :], raw[:, n, :])
                    last.then_inc(moments.sem, 1)
                if rms:
                    ve.wait_ge(moments.sem, moments(NC))
                    ve.tensor_tensor(offset[:, :], mv[:, :, 0], mv[:, :, 0], ALU.mult).then_inc(squared.sem, 1)
                    ve.wait_ge(squared.sem, squared(1))
                    ve.tensor_tensor(mv[:, :, 1], mv[:, :, 1], offset[:, :], ALU.add).then_inc(squared.sem, 1)
                for c in range(NC):
                    tiles = slice(c * TPC, (c + 1) * TPC)
                    ve.wait_ge(roots.sem, roots(c + 1))
                    ve.reciprocal(rstd[:, tiles], std[:, tiles]).then_inc(scales.sem, 1)
                    ve.wait_ge(scales.sem, scales(2 * c + 1))
                    ve.scalar_tensor_tensor(offset[:, tiles], mv[:, tiles, 0], 0.0 if rms else -1.0,
                                            rstd[:, tiles], ALU.mult, ALU.mult).then_inc(scales.sem, 1)
                if outT:
                    for c in range(NC):
                        ve.wait_ge(turned.sem, turned(c + 1))
                        if gain is None:
                            ve.tensor_copy(outT(c)[0], outT(c)[1](xt[:, c, 0:CH]))
                        elif shift is None:
                            ve.tensor_scalar(outT(c)[0], outT(c)[1](xt[:, c, 0:CH]), gain, None, ALU.mult)
                        else:
                            ve.tensor_scalar(outT(c)[0], outT(c)[1](xt[:, c, 0:CH]), gain, shift, ALU.mult, ALU.add)

            @block.scalar
            def _(act):
                eps = core.eps_rms if rms else core.eps_ln
                for c in range(NC):
                    tiles = slice(c * TPC, (c + 1) * TPC)
                    if rms:
                        act.wait_ge(squared.sem, squared(2))
                    else:
                        act.wait_ge(moments.sem, moments(c + 1))
                    act.activation(std[:, tiles], mv[:, tiles, 1], ACT.Sqrt, bias=eps[0:T2, :]).then_inc(roots.sem, 1)
                for c in range(NC):
                    act.wait_ge(scales.sem, scales(2 * c + 2))
                    for n in range(c * TPC, (c + 1) * TPC):
                        last = act.activation(keep[:, n, :], z[:, n, :], ACT.Identity,
                                              bias=offset[:, n:n + 1], scale=rstd[:, n:n + 1])
                    last.then_inc(normed.sem, 1)

            if final:
                @block.sync
                def _(sp):
                    rows = core.out.rearrange("b t d -> (b t) d").rearrange("(n p) d -> p n d", p=T2)
                    for c in range(NC):
                        tiles = slice(c * TPC, (c + 1) * TPC)
                        sp.wait_ge(normed.sem, normed(c + 1))
                        sp.dma_start(rows[:, tiles, :], keep[:, tiles, :]).then_inc(kept.sem, 16)
                    sp.wait_ge(kept.sem, kept(16 * NC))
        projected.base += NC if project else 0
        added.base += NC if project else 0
        stats.base += NC
        moments.base += NC
        squared.base += 2 if rms else 0
        roots.base += NC
        scales.base += 2 * NC
        normed.base += NC
        turned.base += NC if outT else 0


def by_batch(xT):
    return lambda c: (xT[:, c * CH:(c + 1) * CH], lambda ap: ap)


GB = 4
NB = INNER * DS // P // GB


def stage_scan(core):
    nc, d = core.nc, core.dram
    NG = INNER * DS // P
    CPG = P // DS
    with scope(core, "l0s") as (sb, psum):
        xnT = sb("xnT", [D, L, B])
        yT = sb("yT", [P, 2, L, B])
        win = sb("win", [D, 2 * INNER])
        lnw = sb("lnw", [D, 2])
        loads = core.sem("l0s_loads")
        with nc.Block() as block:
            @block.sync
            def _(sp):
                sp.dma_start(win[:, :], d["L0_attn_in_proj_wT"]).then_inc(loads, 16)
                sp.dma_start(lnw[:, :], d["L0_attn_ln"]).then_inc(loads, 16)
                sp.wait_ge(loads, 32)
        stage_norm(core, "l0n", residual=False, gain=lnw[:, 0:1], shift=lnw[:, 1:2],
                   outT=lambda c: (xnT[:, :, c * BC:(c + 1) * BC].rearrange("p t b -> p b t"),
                                   lambda ap: ap.rearrange("p (b t) -> p b t", t=L)))
        with scope(core, "l0r") as (sb2, psum2):
            u = sb2("u", [P, 2, L, 2, GB * B])
            wexp = sb2("wexp", [D, NG, P])
            cexp = sb2("cexp", [P, NG, P])
            brow = u[:, 1].rearrange("p t r x -> p (t r x)")[:, 0:NG * P]
            c_gp = sb2("c_gp", [NG, 2, P])
            cA = sb2("cA", [P, 2, NG])
            mine = sb2("mine", [P, CPG])
            a_col = sb2("a_col", [P, 1])
            pu = psum2("pu", [P, 4, 512])
            py = psum2("py", [P, 4, 512])
            loads2, built, turned, got = (core.sem(f"l0r_{s}") for s in ("loads", "built", "turned", "got"))
            step_done, u_made, u_taken = (core.sem(f"l0r_{s}") for s in ("step", "u_made", "u_taken"))
            y_read, y_taken, apart = (core.sem(f"l0r_{s}") for s in ("y_read", "y_taken", "apart"))
            with nc.Block() as block:
                @block.sync
                def _(sp):
                    sp.dma_start(brow, d["L0_attn_B_mat"].rearrange("i s -> (i s)")
                                 .partition_broadcast(P)).then_inc(loads2, 16)
                    sp.dma_start(c_gp[:, 0, :], d["L0_attn_C_mat"].rearrange("(g i) s -> g (i s)", i=CPG)).then_inc(loads2, 16)
                    sp.dma_start(c_gp[:, 1, :], d["L0_attn_A_log"].rearrange("(g i) s -> g (i s)", i=CPG)).then_inc(loads2, 16)

                @block.gpsimd
                def _(pool):
                    pool.memset(mine[:, :], 1.0).then_inc(built, 1)
                    pool.memset(cexp[:, :, :], 0.0).then_inc(built, 1)
                    pool.wait_ge(built, 1)
                    pool.affine_select(out=mine[:, :], in_=mine[:, :], compare_op=ALU.is_ge, fill=0.0,
                                       base=0, pattern=[[-DS, CPG]], channel_multiplier=1).then_inc(built, 1)
                    pool.wait_ge(built, 3)
                    pool.affine_select(out=mine[:, :], in_=mine[:, :], compare_op=ALU.is_ge, fill=0.0,
                                       base=DS - 1, pattern=[[DS, CPG]], channel_multiplier=-1).then_inc(built, 1)

                @block.tensor
                def _(pe):
                    pe.wait_ge(loads2, 48)
                    for k in range(2):
                        pe.transpose(pu[:, 0, k * NG:(k + 1) * NG], c_gp[:, k, :], core.ident[0:NG, 0:NG]).then_inc(turned, 1)

                @block.scalar
                def _(act):
                    act.wait_ge(turned, 2)
                    act.activation(cA[:, 0, :], pu[:, 0, 0:NG], ACT.Copy).then_inc(got, 1)
                    act.activation(cA[:, 1, :], pu[:, 0, NG:2 * NG], ACT.Exp).then_inc(got, 1)

                @block.vector
                def _(ve):
                    ve.wait_ge(loads2, 48)
                    ve.tensor_tensor(wexp[:, :, :].rearrange("p g (i s) -> p (g i) s", s=DS),
                                     over(win[:, 0:INNER].unsqueeze(2), [D, INNER, DS]),
                                     brow.rearrange("p (i s) -> p i s", s=DS), ALU.mult)
                    ve.wait_ge(got, 2)
                    ve.tensor_scalar(cA[:, 1, :], cA[:, 1, :], -0.01, -10.0, ALU.min, ALU.max).then_inc(got, 1)
                    ve.wait_ge(got, 3)
                    ve.tensor_reduce(a_col[:, :], cA[:, 1, :], AX, ALU.min, negate=True)
                    ve.wait_ge(built, 4)
                    for g in range(NG):
                        at = (g % (P // CPG)) * CPG
                        ve.tensor_scalar(cexp[:, g, at:at + CPG], mine[:, :], cA[:, 0, g:g + 1], None, ALU.mult)

            per_block = 2 * 2 * (L - 1) + 2
            QT = L // NC
            middle, outer = (1, 2), (0, 3)

            def scanned(k, step):
                return k * per_block + 2 + 4 * step

            def half_done(k):
                return k % (NB // 2) == NB // 2 - 1

            with nc.Block() as block:
                @block.tensor
                def _(pe):
                    def inputs_of(k, quarters, n):
                        for gl in range(GB):
                            for c in quarters:
                                if n >= 4:
                                    pe.wait_ge(u_taken, 2 * (n - 3))
                                pe.matmul(pu[:, n % 4, 0:CH], wexp[:, k * GB + gl, :],
                                          xnT[:, c * QT:(c + 1) * QT, :], start=True, stop=True).then_inc(u_made, 1)
                                n += 1
                        return n

                    def sums_of(k, c):
                        pe.wait_ge(step_done, scanned(k, (c + 1) * QT - 1))
                        for r in range(2):
                            bank = NC - 1 - c if r else c
                            for gl in range(GB):
                                h = u[:, k % 2, c * QT:(c + 1) * QT, r, gl * B:(gl + 1) * B]
                                last = pe.matmul(py[:, bank, 0:CH], cexp[:, k * GB + gl, :], h[:, ::-1, :] if r else h,
                                                 start=(k % (NB // 2) == 0 and gl == 0 and c < 2),
                                                 stop=(half_done(k) and gl == GB - 1 and c >= 2))
                        return last

                    n_u = 0
                    for k in range(2):
                        n_u = inputs_of(k, middle, n_u)
                        n_u = inputs_of(k, outer, n_u)
                    for k in range(NB):
                        if k == NB // 2:
                            pe.wait_ge(y_taken, NC)
                        sums_of(k, 0)
                        sums_of(k, 1)
                        sums_of(k, 2).then_inc(y_read, 1)
                        if k + 2 < NB:
                            n_u = inputs_of(k + 2, middle, n_u)
                        sums_of(k, 3).then_inc(y_read, 1)
                        if k + 2 < NB:
                            n_u = inputs_of(k + 2, outer, n_u)

                @block.scalar
                def _(act):
                    def fill(k, quarters, n):
                        for gl in range(GB):
                            for c in quarters:
                                act.wait_ge(u_made, n + 1)
                                src = pu[:, n % 4, 0:CH].rearrange("p (t b) -> p t b", b=B)
                                at = slice(gl * B, (gl + 1) * B)
                                t0 = c * QT
                                act.activation(u[:, k % 2, t0:t0 + QT, 0, at], src, ACT.Copy).then_inc(u_taken, 1)
                                back = u[:, k % 2, L - t0 - QT:L - t0, 1, at][:, ::-1, :]
                                act.activation(back, src, ACT.Copy).then_inc(u_taken, 1)
                                n += 1
                        return n

                    def keep_sums(half, quarters):
                        for c in quarters:
                            act.activation(yT[:, half, c * QT:(c + 1) * QT, :],
                                           py[:, c, 0:CH].rearrange("p (t b) -> p t b", b=B),
                                           ACT.Copy, scale=0.5).then_inc(y_taken, 1)

                    n = 0
                    for k in range(2):
                        n = fill(k, middle, n)
                        n = fill(k, outer, n)
                    for k in range(NB):
                        for m, quarters in enumerate((middle, outer)):
                            act.wait_ge(y_read, 2 * k + m + 1)
                            if half_done(k):
                                keep_sums(k // (NB // 2), quarters)
                            if k + 2 < NB:
                                if m == 0:
                                    act.wait_ge(step_done, scanned(k, 3 * QT))
                                n = fill(k + 2, quarters, n)

                @block.vector
                def _(ve):
                    w = GB * B
                    filled = 2 * GB * NC
                    with ve.Fori(0, NB // 2) as pair:
                        for m in range(2):
                            wait_apart(ve, u_taken, pair * (2 * filled) + (m + 1) * filled, apart)
                            x = u[:, m].rearrange("p t r x -> p t (r x)")
                            for r in range(2):
                                first = x[:, 0, r * w:(r + 1) * w]
                                ve.tensor_scalar(first, first, 10.0, -10.0, ALU.min, ALU.max).then_inc(step_done, 1)
                            base = scanned(m, 0)
                            for t in range(1, L):
                                for r in range(2):
                                    prev, cur = (x[:, t - 1 + i, r * w:(r + 1) * w] for i in range(2))
                                    ve.wait_ge(step_done, pair * (2 * per_block) + (base + 4 * (t - 1) + r - 1))
                                    ve.scalar_tensor_tensor(cur, prev, a_col[:, :], cur, ALU.mult,
                                                            ALU.add).then_inc(step_done, 1)
                                for r in range(2):
                                    cur = x[:, t, r * w:(r + 1) * w]
                                    ve.wait_ge(step_done, pair * (2 * per_block) + (base + 4 * (t - 1) + r + 1))
                                    ve.tensor_scalar(cur, cur, 10.0, -10.0, ALU.min, ALU.max).then_inc(step_done, 1)

        with scope(core, "l0g") as (sb2, psum2):
            gate = sb2("gate", [P, 2, T])
            gT = sb2("gT", [P, 2, T])
            wout = sb2("wout", [P, 2, D])
            made, opened, wl = (core.sem(f"l0g_{s}") for s in ("made", "opened", "loads"))
            with scope(core, "l0gp") as (_, psum3), nc.Block() as block:
                pg = psum3("pg", [P, 8, 512])

                @block.sync
                def _(sp):
                    sp.dma_start(wout[:, :, :], d["L0_attn_out_proj_wT"].rearrange("(h p) d -> p h d", p=P)).then_inc(wl, 16)
                    sp.wait_ge(wl, 16)

                @block.tensor
                def _(pe):
                    for h in range(2):
                        for c in range(NC):
                            pe.matmul(pg[:, h * NC + c, 0:CH], win[:, INNER + h * P:INNER + (h + 1) * P],
                                      xnT[:, c * 14:(c + 1) * 14, :], start=True, stop=True).then_inc(made, 1)

                @block.scalar
                def _(act):
                    for k in range(2 * NC):
                        act.wait_ge(made, k + 1)
                        act.activation(gate[:, k // NC, (k % NC) * CH:(k % NC + 1) * CH], pg[:, k, 0:CH],
                                       ACT.Silu).then_inc(opened, 1)

                @block.vector
                def _(ve):
                    for k in range(2 * NC):
                        h, c = k // NC, k % NC
                        ve.wait_ge(opened, k + 1)
                        ve.tensor_tensor(gT[:, h, :].rearrange("p (b t) -> p t b", t=L)[:, c * 14:(c + 1) * 14, :],
                                         yT[:, h, c * 14:(c + 1) * 14, :],
                                         gate[:, h, c * CH:(c + 1) * CH].rearrange("p (t b) -> p t b", b=B), ALU.mult)

            def project(pe, n, out):
                for h in range(2):
                    last = pe.matmul(out, gT[:, h, n * T2:(n + 1) * T2], wout[:, h, :], start=(h == 0), stop=(h == 1))
                return last

            stage_norm(core, "l0p", project=project, outT=by_batch(core.xT))


HB, DH = 2, 64
QR = HB * L
QP = HB * DH
VW = DH + 1
HINV = 1.0 / D


def stage_attention(core):
    nc, d = core.nc, core.dram
    with scope(core, "b") as (sb, psum):
        mk = sb("mk", [D, D])
        mv_ext = sb("mv_ext", [D, HB, VW])
        qw = sb("qw", [D, B, QR])
        qblk = sb("qblk", [P, B, HB, L])
        klT = sb("klT", [P, T])
        vl = sb("vl", [L, B, HB, VW])
        aT = sb("aT", [DH, HB, T])
        wout = sb("wout", [DH, HB, D])
        bout = sb("bout", [1, D])
        negmask = sb("negmask", [B, S2], BF16)
        onehot = sb("onehot", [B, B, QR], BF16)
        stage_latents(core, mk, mv_ext, qw, qblk, klT, vl, wout, bout, negmask, onehot)
        with scope(core, "bm") as (sb2, _):
            att = sb2("att", [P, B, DH])
            with scope(core, "bl") as (sb3, psum3):
                stage_context(core, sb3, psum3, mk, mv_ext, qw, qblk, klT, vl, att, negmask, onehot)
            heads_to_features(core, "bh", att, aT, None)

        def project(pe, n, out):
            for h in range(HB):
                pe.matmul(out, aT[:, h, n * T2:(n + 1) * T2], wout[:, h, :], start=(h == 0), stop=False)
            return pe.matmul(out, core.ones[0:1, 0:T2], bout[:, :], start=False, stop=True)

        stage_norm(core, "bn", project=project, outT=by_batch(core.xT))


def stage_latents(core, mk, mv_ext, qw, qblk, klT, vl, wout, bout, negmask, onehot):
    nc, d = core.nc, core.dram
    with scope(core, "bq") as (sb, psum):
        w = sb("w", [D, 3, D])
        lng = sb("lng", [D, 4])
        gam = sb("gam", [L, 2, DH])
        lT = sb("lT", [D, T])
        mask8 = sb("mask8", [B, S2], U8)
        loads, done = core.sem("bq_loads"), core.sem("bq_done")
        with nc.Block() as block:
            @block.sync
            def _(sp):
                sp.dma_start(w[:, 0, :], d["L0_xattn_W_q"]).then_inc(loads, 16)
                sp.dma_start(w[:, 1:3, :], d["L0_xattn_W_kv"].rearrange("i (k o) -> i k o", k=2)).then_inc(loads, 16)
                sp.dma_start(lng[:, :], d["L0_xattn_ln"]).then_inc(loads, 16)
                sp.dma_start(gam[:, 0, :], d["L0_xattn_q_gamma"].partition_broadcast(L)).then_inc(loads, 16)
                sp.dma_start(gam[:, 1, :], d["L0_xattn_k_gamma"].partition_broadcast(L)).then_inc(loads, 16)
                sp.dma_start(wout[:, :, :], d["L0_xattn_W_out"].rearrange("(h i) o -> i h o", h=HB)).then_inc(loads, 16)
                sp.dma_start(bout[:, :], d["L0_xattn_b_out"].rearrange("(a o) -> a o", a=1)).then_inc(loads, 16)
                sp.dma_start(mask8[:, :], d["mask_BxS2_bk0"]).then_inc(loads, 16)
                sp.wait_ge(loads, 8 * 16)

            @block.vector
            def _(ve):
                ve.memset(qblk[:, :, :, :], 0.0)
                ve.memset(vl[:, :, :, DH:VW], 1.0)
                ve.memset(mv_ext[:, :, DH:VW], HINV)
                ve.tensor_copy(onehot[:, :, :], over(core.ident[0:B, 0:B].unsqueeze(2), [B, B, QR]))
                ve.wait_ge(loads, 8 * 16)
                ve.tensor_scalar(negmask[:, :], mask8[:, :], 1.0, -NEG, ALU.subtract, ALU.mult)

        stage_norm(core, "bln", residual=False, gain=lng[:, 2:3], shift=lng[:, 3:4], outT=by_batch(lT))

        with scope(core, "bw") as (sb2, psum2):
            gw = sb2("gw", [D, 2, D])
            bias = sb2("bias", [D, D])
            negmean = sb2("negmean", [D, D])
            mkT = sb2("mkT", [P, D])
            qk = sb2("qk", [L, B, 4, DH])
            sq = sb2("sq", [L, B, 4, DH])
            ss = sb2("ss", [L, B, 4])
            inv = sb2("inv", [L, B, 4])
            qT = sb2("qT", [P, T])
            ps = psum2("ps", [P, 8, 512])
            g = {s: core.sem(f"bw_{s}") for s in ("fold", "mean", "m", "qkv", "taken", "sq", "ss", "root", "inv", "unit",
                                                  "turned", "copied", "wide", "kept", "mkt", "mktc")}
            with nc.Block() as block:
                @block.tensor
                def _(pe):
                    pe.wait_ge(g["fold"], 3)
                    out = ps[:, 0, 0:2 * D]
                    pe.matmul(out, negmean[:, :], gw[:, :, :], start=True, stop=False)
                    pe.matmul(out, bias[:, :], w[:, 1:3, :], start=False, stop=True).then_inc(g["mean"], 1)
                    for b in range(B):
                        if b >= 4:
                            pe.wait_ge(g["taken"], 2 * (b - 3))
                        pe.matmul(ps[0:L, 1 + b % 4, 0:3 * D], lT[:, b * L:(b + 1) * L], w[:, :, :],
                                  start=True, stop=True).then_inc(g["qkv"], 1)
                    pe.wait_ge(g["m"], 2)
                    pe.transpose(ps[:, 5, 0:D], mk[:, :], core.ident[:, :]).then_inc(g["mkt"], 1)
                    pe.wait_ge(g["unit"], 3)
                    for n in range(2 * NC):
                        which, c = n // NC, n % NC
                        if n >= 2:
                            pe.wait_ge(g["copied"], n - 1)
                        for r in range(BC):
                            last = pe.transpose(ps[:, 6 + n % 2, r * L:(r + 1) * L],
                                                qk[:, c * BC + r, 2 * which:2 * which + 2, :].rearrange("p h d -> p (h d)"),
                                                core.ident[0:L, 0:L])
                        last.then_inc(g["turned"], 1)
                    pe.wait_ge(g["copied"], 2 * NC)
                    pe.wait_ge(g["mktc"], 1)
                    for n in range(HB * NC):
                        c, h = n // HB, n % HB
                        if n >= 4:
                            pe.wait_ge(g["kept"], n - 3)
                        pe.matmul(ps[:, 1 + n % 4, 0:CH], mkT[h * DH:(h + 1) * DH, :],
                                  qT[h * DH:(h + 1) * DH, c * CH:(c + 1) * CH], start=True, stop=True).then_inc(g["wide"], 1)

                @block.scalar
                def _(act):
                    for b in range(B):
                        act.wait_ge(g["qkv"], b + 1)
                        act.activation(qk[:, b, :, :], ps[0:L, 1 + b % 4, 0:2 * D].rearrange("p (k d) -> p k d", d=DH),
                                       ACT.Copy).then_inc(g["taken"], 1)
                        act.activation(vl[:, b, :, 0:DH], ps[0:L, 1 + b % 4, 2 * D:3 * D].rearrange("p (h d) -> p h d", d=DH),
                                       ACT.Copy).then_inc(g["taken"], 1)
                    act.wait_ge(g["taken"], 2 * B)
                    act.activation(sq[:, :, :, :], qk[:, :, :, :], ACT.Square).then_inc(g["sq"], 1)
                    act.wait_ge(g["mkt"], 1)
                    act.activation(mkT[:, :], ps[:, 5, 0:D], ACT.Copy).then_inc(g["mktc"], 1)
                    act.wait_ge(g["ss"], 1)
                    act.activation(inv[:, :, :], ss[:, :, :], ACT.Sqrt, scale=1.0 / DH).then_inc(g["root"], 1)
                    for n in range(HB * NC):
                        c, h = n // HB, n % HB
                        act.wait_ge(g["wide"], n + 1)
                        act.activation(qw[:, c * BC:(c + 1) * BC, h * L:(h + 1) * L],
                                       ps[:, 1 + n % 4, 0:CH].rearrange("p (b t) -> p b t", t=L), ACT.Copy).then_inc(g["kept"], 1)

                @block.vector
                def _(ve):
                    ve.memset(negmean[:, :], -HINV).then_inc(g["fold"], 1)
                    ve.tensor_scalar(gw[:, :, :], w[:, 1:3, :], lng[:, 0:1], None, ALU.mult).then_inc(g["fold"], 1)
                    ve.tensor_scalar(bias[:, :], core.ones[:, :], lng[:, 1:2], HINV, ALU.mult, ALU.mult).then_inc(g["fold"], 1)
                    ve.wait_ge(g["mean"], 1)
                    ve.wait_ge(g["fold"], 3)
                    ve.tensor_tensor(mk[:, :], gw[:, 0, :], ps[:, 0, 0:D], ALU.add).then_inc(g["m"], 1)
                    ve.tensor_tensor(mv_ext[:, :, 0:DH], gw[:, 1, :].rearrange("p (h d) -> p h d", h=HB),
                                     ps[:, 0, D:2 * D].rearrange("p (h d) -> p h d", h=HB), ALU.add).then_inc(g["m"], 1)
                    ve.wait_ge(g["sq"], 1)
                    ve.tensor_reduce(ss[:, :, :], sq[:, :, :, :], AX, ALU.add).then_inc(g["ss"], 1)
                    ve.wait_ge(g["root"], 1)
                    ve.tensor_scalar(inv[:, :, :], inv[:, :, :], 1e-8, None, ALU.max).then_inc(g["inv"], 1)
                    ve.wait_ge(g["inv"], 1)
                    ve.reciprocal(inv[:, :, :], inv[:, :, :]).then_inc(g["inv"], 1)
                    ve.wait_ge(g["inv"], 2)
                    ve.tensor_tensor(qk[:, :, :, :], qk[:, :, :, :], over(inv[:, :, :].unsqueeze(3), [L, B, 4, DH]),
                                     ALU.mult).then_inc(g["unit"], 1)
                    ve.scalar_tensor_tensor(gam[:, 0, :], gam[:, 0, :], float(DH) ** -0.5, gam[:, 1, :],
                                            ALU.mult, ALU.mult).then_inc(g["unit"], 1)
                    ve.wait_ge(g["unit"], 2)
                    ve.tensor_tensor(qk[:, :, 0:2, :], qk[:, :, 0:2, :],
                                     over(gam[:, 0, :].unsqueeze(1).unsqueeze(1), [L, B, 2, DH]), ALU.mult).then_inc(g["unit"], 1)
                    for n in range(2 * NC):
                        which, c = n // NC, n % NC
                        ve.wait_ge(g["turned"], n + 1)
                        src = ps[:, 6 + n % 2, 0:CH]
                        if which:
                            ve.tensor_copy(klT[:, c * CH:(c + 1) * CH], src).then_inc(g["copied"], 1)
                        else:
                            ve.tensor_copy(qT[:, c * CH:(c + 1) * CH], src)
                            for h in range(HB):
                                rows = slice(h * DH, (h + 1) * DH)
                                last = ve.tensor_copy(qblk[rows, c * BC:(c + 1) * BC, h, :],
                                                      src[rows, :].rearrange("p (b t) -> p b t", t=L))
                            last.then_inc(g["copied"], 1)


def stage_context(core, sb, psum, mk, mv_ext, qw, qblk, klT, vl, att, negmask, onehot):
    nc = core.nc
    ctx_dram = core.dram["ctx_1024"].rearrange("b (p k) f -> b p k f", k=KT)
    SUB = 3
    KS = KT // SUB
    NX = 4
    xc = sb("xc", [KP, NX, KT, D])
    stats = sb("stats", [KP, 2, KT, 6])
    moments = sb("moments", [KP, 2, KT, 2])
    rstd = sb("rstd", [KP, 2, KT])
    shift = sb("shift", [KP, 2, KT])
    xcT = sb("xcT", [D, 2, KT * KP])
    sq = sb("sq", [KP, 2, KS, HB, DH])
    ss = sb("ss", [KP, 2, KT, HB])
    inv = sb("inv", [KP, 2, KT, HB])
    sc = sb("sc", [P, 2, KT + 1, QR])
    top = sb("top", [P, 2, QR])
    topall = sb("topall", [P, 2, QR])
    plat = sb("plat", [L, QP])
    mixT = sb("mixT", [D, QP])
    rden = sb("rden", [P, HB])
    kl = sb("kl", [P, 2, L])
    pX = psum("pX", [P, 2, 512])
    pK = psum("pK", [P, 2, 512])
    pS = psum("pS", [P, SUB, 512])
    pO = psum("pO", [P, 512])
    lats_at, mix_at, val_at = slice(0, QR), slice(128, 128 + QR), slice(256, 256 + HB * VW)
    names = ("kl apart load0 load1 load2 load3 const stats moments lnv rstd shift xc turned xcT keys sq ss floor lninv inv raw lat scaled lats "
             "top topall subbed probs plat mix mixT val rden att").split()
    s = {n: core.sem(f"bl_{n}") for n in names}

    STEPS = B + 2
    PEEL, UN = 4, 4

    def run(eng, step, steps=STEPS):
        for n in range(PEEL):
            step(n, n)
        with eng.Fori(0, (B - PEEL) // UN) as i:
            for j in range(UN):
                step(i * UN + (PEEL + j), PEEL + j)
        for n in range(B, steps):
            step(n, n)

    def a_part(k):
        return k < B

    def b_part(k):
        return 1 <= k < B + 1

    def c_part(k):
        return 2 <= k < B + 2

    def d_part(k):
        return 3 <= k

    with nc.Block() as block:
        @block.sync
        def _(sp):
            def load(n, k, wait):
                if wait:
                    sp.wait_ge(s["mix"], n - NX + 1)
                sp.dma_start(xc[:, k % NX, :, :], ctx_dram[bass.ds(n, 1)].rearrange("a p k f -> p (a k) f")
                             if not isinstance(n, int) else ctx_dram[n]).then_inc(s[f"load{k % NX}"], 16)
            for n in range(NX):
                load(n, n, False)
            with sp.Fori(0, (B - NX) // NX) as i:
                for j in range(NX):
                    load(i * NX + (NX + j), j, True)

        @block.gpsimd
        def _(pool):
            fills = ((sc[:, 0, KT, :], NEG), (top[96:P, 0, :], NEG), (sc[:, 1, KT, :], NEG),
                     (top[96:P, 1, :], NEG), (plat[:, :], 0.0), (mixT[:, :], 0.0), (att[:, :, :], 0.0))
            for m, (tile, value) in enumerate(fills):
                if m:
                    pool.wait_ge(s["const"], m)
                pool.memset(tile, value).then_inc(s["const"], 1)
            pool.wait_ge(s["const"], len(fills))

            def step(n, k):
                if c_part(k):
                    buf = k % 2
                    pool.wait_ge(s["topall"], n - 1)
                    pool.tensor_tensor(sc[0:KP, buf, :, :], sc[0:KP, buf, :, :],
                                       over(topall[0:KP, buf, :].unsqueeze(1), [KP, KT + 1, QR]),
                                       ALU.subtract).then_inc(s["subbed"], 1)
                if a_part(k):
                    wait_apart(pool, s["shift"], 2 * n + 2, s["apart"])
                    for t in range(KT):
                        last = pool.tensor_scalar(xc[:, k % NX, t, :], xc[:, k % NX, t, :],
                                                  rstd[:, k % 2, t:t + 1], shift[:, k % 2, t:t + 1], ALU.mult, ALU.add)
                    last.then_inc(s["xc"], 1)
                if b_part(k):
                    buf = (k - 1) % 2
                    if k > 2:
                        pool.wait_ge(s["subbed"], n - 2)
                    wait_apart(pool, s["top"], n, s["apart"])
                    pool.partition_all_reduce(topall[:, buf, :], top[:, buf, :], P, RMAX).then_inc(s["topall"], 1)
            run(pool, step)

        @block.vector
        def _(ve):
            ve.wait_ge(s["const"], 7)

            def shifts(n, buf):
                ve.wait_ge(s["rstd"], n + 1)
                ve.tensor_tensor(shift[:, buf, :], moments[:, buf, :, 0], rstd[:, buf, :], ALU.mult).then_inc(s["shift"], 1)
                ve.wait_ge(s["shift"], 2 * n + 1)
                ve.tensor_scalar(shift[:, buf, :], shift[:, buf, :], -1.0, 1.0, ALU.mult, ALU.add).then_inc(s["shift"], 1)

            def step(n, k):
                if a_part(k):
                    buf = k % 2
                    ve.wait_ge(s[f"load{k % NX}"], (n - k % NX) * (16 // NX) + 16)
                    for t in range(KT):
                        last = ve.bn_stats(stats[:, buf, t, :], xc[:, k % NX, t, :])
                    last.then_inc(s["stats"], 1)
                if d_part(k):
                    ve.wait_ge(s["val"], n - 2)
                    val = pO[:, val_at].rearrange("p (h v) -> p h v", v=VW)
                    ve.reciprocal(rden[:, :], val[:, :, DH]).then_inc(s["rden"], 1)
                if a_part(k):
                    wait_apart(ve, s["stats"], n + 1, s["apart"])
                    for t in range(KT):
                        last = ve.bn_aggr(moments[:, buf, t, :], stats[:, buf, t, :])
                    last.then_inc(s["moments"], 1)
                if d_part(k):
                    ve.wait_ge(s["rden"], n - 2)
                    for h in range(HB):
                        rows = slice(h * DH, h * DH + L)
                        last = ve.tensor_scalar(att[rows, bass.ds(n - 3, 1), :].rearrange("p a d -> p (a d)"),
                                                val[rows, h, 0:DH], rden[rows, h:h + 1], None, ALU.mult)
                    last.then_inc(s["att"], 1)
                if b_part(k):
                    buf = (k - 1) % 2
                    for u in range(SUB):
                        if u == SUB - 1 and a_part(k):
                            shifts(n, k % 2)
                        ve.wait_ge(s["sq"], n * SUB - SUB + u + 1)
                        ve.tensor_reduce(ss[:, buf, u * KS:(u + 1) * KS, :], sq[:, (k - 1 + u) % 2, :, :, :], AX,
                                         ALU.add).then_inc(s["ss"], 1)
                elif a_part(k):
                    shifts(n, k % 2)
                if b_part(k):
                    buf = (k - 1) % 2
                    ve.wait_ge(s["ss"], SUB * n)
                    ve.tensor_scalar(ss[:, buf, :, :], ss[:, buf, :, :], 1e-16 * DH, None, ALU.max).then_inc(s["floor"], 1)
                    if k > 2:
                        ve.wait_ge(s["mix"], n - 2)
                    ve.wait_ge(s["lat"], n)
                    ve.tensor_copy(sc[0:L, buf, KT, :], pO[0:L, lats_at]).then_inc(s["lats"], 1)
                    ve.wait_ge(s["inv"], n)
                    for u in range(SUB):
                        tiles = slice(u * KS, (u + 1) * KS)
                        ve.wait_ge(s["raw"], n * SUB - SUB + u + 1)
                        ve.tensor_tensor(sc[0:KP, buf, tiles, :].rearrange("p k (h q) -> p k h q", h=HB),
                                         pS[0:KP, u, 0:KS * QR].rearrange("p (k h q) -> p k h q", k=KS, h=HB),
                                         over(inv[:, buf, tiles, :].unsqueeze(3), [KP, KS, HB, L]),
                                         ALU.mult).then_inc(s["scaled"], 1)
                    ve.wait_ge(s["scaled"], SUB * n)
                    ve.wait_ge(s["lats"], n)
                    if k > 2:
                        ve.wait_ge(s["topall"], n - 2)
                    ve.tensor_reduce(top[0:KP, buf, :], sc[0:KP, buf, :, :].rearrange("p k q -> p q k"), AX,
                                     ALU.max).then_inc(s["top"], 1)
            run(ve, step, STEPS + 1)

        @block.scalar
        def _(act):
            load_tables(nc, act, LN_EXP_TABLES)

            def roots(n, buf):
                act.wait_ge(s["moments"], n + 1)
                act.activation(rstd[:, buf, :], moments[:, buf, :, 1], ACT.Ln, bias=core.eps_ln[0:KP, :]).then_inc(s["lnv"], 1)
                act.wait_ge(s["lnv"], n + 1)
                act.activation(rstd[:, buf, :], rstd[:, buf, :], ACT.Exp, scale=-0.5).then_inc(s["rstd"], 1)

            def step(n, k):
                if a_part(k) and k == 0:
                    act.wait_ge(s["const"], 7)
                if b_part(k):
                    buf = (k - 1) % 2
                    act.activation(kl[:, buf, :], klT[:, bass.ds((n - 1) * L, L)], ACT.Copy).then_inc(s["kl"], 1)
                    for u in range(SUB + 1):
                        if u < SUB:
                            act.wait_ge(s["turned"], n * SUB - SUB + u + 1)
                            act.activation(xcT[:, buf, u * KS * KP:(u + 1) * KS * KP], pX[:, (k - 1 + u) % 2, 0:KS * KP],
                                           ACT.Copy).then_inc(s["xcT"], 1)
                        if u:
                            act.wait_ge(s["keys"], n * SUB - SUB + u)
                            if k > 1 or u > 2:
                                act.wait_ge(s["ss"], n * SUB - SUB + u - 2)
                            act.activation(sq[:, (k - 2 + u) % 2, :, :, :],
                                           pK[0:KP, (k - 2 + u) % 2, :].rearrange("p (k h d) -> p k h d", k=KS, h=HB),
                                           ACT.Square).then_inc(s["sq"], 1)
                        if u == 2 and a_part(k):
                            roots(n, k % 2)
                elif a_part(k):
                    roots(n, k % 2)
                if c_part(k):
                    act.wait_ge(s["subbed"], n - 1)
                    act.activation(sc[0:KP, k % 2, 0:KT, :], sc[0:KP, k % 2, 0:KT, :], ACT.Exp).then_inc(s["probs"], 1)
                if b_part(k):
                    act.wait_ge(s["floor"], n)
                    act.activation(inv[:, buf, :, :], ss[:, buf, :, :], ACT.Ln, scale=1.0 / DH).then_inc(s["lninv"], 1)
                    act.wait_ge(s["lninv"], n)
                    act.activation(inv[:, buf, :, :], inv[:, buf, :, :], ACT.Exp, scale=-0.5).then_inc(s["inv"], 1)
                if c_part(k):
                    if k > 2:
                        act.wait_ge(s["val"], n - 2)
                    act.activation(plat[:, :].rearrange("p (h q) -> p h q", h=HB)[:, :, 0:L],
                                   sc[0:L, k % 2, KT, :].rearrange("p (h q) -> p h q", h=HB), ACT.Exp).then_inc(s["probs"], 1)
                    act.wait_ge(s["mix"], n - 1)
                    act.activation(mixT[:, :].rearrange("p (h q) -> p h q", h=HB)[:, :, 0:L],
                                   pO[:, mix_at].rearrange("p (h q) -> p h q", h=HB), ACT.Copy).then_inc(s["mixT"], 1)
            run(act, step)

        @block.tensor
        def _(pe):
            pe.wait_ge(s["const"], 7)

            def values(n, k):
                pe.wait_ge(s["mixT"], n - 2)
                pe.matmul(pO[:, val_at], mixT[:, :], mv_ext[:, :, :], start=True, stop=False)
                pe.matmul(pO[:, val_at], plat[:, :], vl[:, bass.ds(n - 3, 1), :, :], start=False,
                          stop=True).then_inc(s["val"], 1)

            def step(n, k):
                if b_part(k):
                    buf, x = (k - 1) % 2, (k - 1) % NX
                    bq = n - 1
                    pe.wait_ge(s["xc"], n)
                    def turn(u):
                        if k > 1 or u > 1:
                            pe.wait_ge(s["xcT"], n * SUB - SUB + u - 1)
                        for r in range(KS):
                            last = pe.transpose(pX[:, (k - 1 + u) % 2, r * KP:(r + 1) * KP], xc[:, x, u * KS + r, :],
                                                core.ident[0:KP, 0:KP])
                        last.then_inc(s["turned"], 1)

                    def keys(u):
                        pe.wait_ge(s["xcT"], n * SUB - SUB + u + 1)
                        if k > 1 or u > 1:
                            pe.wait_ge(s["sq"], n * SUB - SUB + u - 1)
                        for r in range(KS):
                            at = slice((u * KS + r) * KP, (u * KS + r + 1) * KP)
                            last = pe.matmul(pK[0:KP, (k - 1 + u) % 2, r * D:(r + 1) * D], xcT[:, buf, at], mk[:, :],
                                             start=True, stop=True)
                        last.then_inc(s["keys"], 1)

                    turn(0)
                    turn(1)
                    if d_part(k):
                        values(n, k)
                    keys(0)
                    turn(2)
                    keys(1)
                    keys(2)
                    if d_part(k):
                        pe.wait_ge(s["att"], n - 2)
                    elif k == 2:
                        pe.wait_ge(s["lats"], n - 1)
                    pe.wait_ge(s["kl"], n)
                    pe.matmul(pO[0:L, lats_at], kl[:, buf, :],
                              qblk[:, bass.ds(bq, 1), :, :], start=True, stop=True).then_inc(s["lat"], 1)
                    for u in range(SUB):
                        if k > 1:
                            pe.wait_ge(s["scaled"], n * SUB - 2 * SUB + u + 1)
                        for r in range(KS):
                            t = u * KS + r
                            out = pS[0:KP, u, r * QR:(r + 1) * QR]
                            pe.matmul(out, xcT[:, buf, t * KP:(t + 1) * KP], qw[:, bass.ds(bq, 1), :],
                                      start=True, stop=False)
                            last = pe.matmul(out, negmask[:, t:S2:KT], onehot[:, bass.ds(bq, 1), :], start=False, stop=True)
                        last.then_inc(s["raw"], 1)
                elif d_part(k):
                    values(n, k)
                if c_part(k):
                    buf, x = k % 2, (k - 2) % NX
                    pe.wait_ge(s["probs"], 2 * n - 2)
                    if b_part(k):
                        pe.wait_ge(s["lats"], n)
                    else:
                        pe.wait_ge(s["att"], n - 2)
                    for t in range(KT):
                        last = pe.matmul(pO[:, mix_at], xc[:, x, t, :], sc[0:KP, buf, t, :],
                                         start=(t == 0), stop=(t == KT - 1))
                    last.then_inc(s["mix"], 1)
            run(pe, step, STEPS + 1)


def rank_below(ve, s, values, earlier, lots, rank, n, limit, out):
    shape = [T2, NT, n, n]
    other, own = over(values.unsqueeze(2), shape), over(values.unsqueeze(3), shape)
    ve.tensor_tensor(lots[0], other, own, ALU.is_gt).then_inc(s.sem, 1)
    ve.tensor_tensor(lots[1], other, own, ALU.is_equal).then_inc(s.sem, 1)
    ve.wait_ge(s.sem, s(2))
    ve.tensor_tensor(lots[1], lots[1], over(earlier.unsqueeze(1), shape), ALU.mult).then_inc(s.sem, 1)
    ve.wait_ge(s.sem, s(3))
    ve.tensor_tensor(lots[0], lots[0], lots[1], ALU.add).then_inc(s.sem, 1)
    ve.wait_ge(s.sem, s(4))
    ve.tensor_reduce(rank, lots[0], AX, ALU.add).then_inc(s.sem, 1)
    ve.wait_ge(s.sem, s(5))
    ve.tensor_scalar(out, rank, limit - 0.5, None, ALU.is_lt).then_inc(s.sem, 1)
    ve.wait_ge(s.sem, s(6))
    s.base += 6


def stage_router(core, name, weights_T, bias, groups, parts):
    nc = core.nc
    with scope(core, name) as (sb, psum):
        wr = sb("wr", [D, E])
        bias_row = sb("bias_row", [T2, E])
        prob = sb("prob", [T2, NT, E])
        choice = sb("choice", [T2, NT, E])
        pairs = sb("pairs", [T2, NT, E // 2])
        best = sb("best", [T2, NT, E // 2])
        lot0, lot1 = sb("lot0", [T2, NT, E, E]), sb("lot1", [T2, NT, E, E])
        earlier = sb("earlier", [T2, E, E])
        rank = sb("rank", [T2, NT, E])
        used = sb("used", [T2, NT, E])
        total = sb("total", [T2, NT])
        low = sb("low", [T2, NT, E], BF16)
        split = sb("split", [T2, NT, 96])
        ps = psum("ps", [P, 5, 512])
        loads, built, logits, probs, cut, turned = (core.sem(f"{name}_{x}") for x in ("loads", "built", "logits", "probs", "cut", "turned"))
        chain = core.shared("router_chain")
        with nc.Block() as block:
            @block.sync
            def _(sp):
                sp.dma_start(wr[:, :], weights_T).then_inc(loads, 16)
                if bias is not None:
                    sp.dma_start(bias_row[:, :], bias.partition_broadcast(T2)).then_inc(loads, 16)

            @block.gpsimd
            def _(pool):
                pool.memset(earlier[:, :, :], 1.0).then_inc(built, 1)
                pool.wait_ge(built, 1)
                pool.affine_select(out=earlier[:, :, :], in_=earlier[:, :, :], compare_op=ALU.is_ge, fill=0.0,
                                   base=-1, pattern=[[1, E], [-1, E]], channel_multiplier=0).then_inc(built, 1)
                pool.wait_ge(built, 2)
                pool.memset(split[:, :, :], 0.0).then_inc(built, 1)

            @block.tensor
            def _(pe):
                pe.wait_ge(loads, 16 if bias is None else 32)
                for n in range(NT):
                    last = pe.matmul(ps[0:T2, 4, n * E:(n + 1) * E], core.xT[:, n * T2:(n + 1) * T2], wr[:, :],
                                     start=True, stop=True)
                last.then_inc(logits, 1)
                pe.wait_ge(cut, 1)
                for c in range(NC):
                    for r in range(TPC):
                        last = pe.transpose(ps[0:96, c, r * T2:(r + 1) * T2], split[:, c * TPC + r, :],
                                            core.ident[0:T2, 0:T2])
                    last.then_inc(turned, 1)

            @block.scalar
            def _(act):
                act.wait_ge(logits, 1)
                act.activation(prob[:, :, :], ps[0:T2, 4, 0:NT * E].rearrange("p (n e) -> p n e", e=E),
                               ACT.Sigmoid).then_inc(probs, 1)
                for c in range(NC):
                    act.wait_ge(turned, c + 1)
                    act.activation(parts[:, c * CH:(c + 1) * CH], ps[0:96, c, 0:CH], ACT.Copy)

            @block.vector
            def _(ve):
                ve.wait_ge(probs, 1)
                ve.wait_ge(built, 3)
                ranked = prob[:, :, :]
                if bias is not None:
                    ranked = choice[:, :, :]
                    ve.tensor_tensor(ranked, prob[:, :, :], over(bias_row[:, :].unsqueeze(1), [T2, NT, E]),
                                     ALU.add).then_inc(chain.sem, 1)
                    ve.wait_ge(chain.sem, chain(1))
                    two = ranked.rearrange("p n (g k) -> p n g k", k=2)
                    ve.tensor_tensor(pairs[:, :, :], two[:, :, :, 0], two[:, :, :, 1], ALU.add).then_inc(chain.sem, 1)
                    ve.wait_ge(chain.sem, chain(2))
                    chain.base += 2
                    h = E // 2
                    rank_below(ve, chain, pairs[:, :, :], earlier[:, 0:h, 0:h],
                               [x[:, :, 0:h, 0:h] for x in (lot0, lot1)], rank[:, :, 0:h], h, 2, best[:, :, :])
                    ve.tensor_tensor(ranked.rearrange("p n (g k) -> p n g k", k=2), two,
                                     over(best[:, :, :].unsqueeze(3), [T2, NT, h, 2]), ALU.mult).then_inc(chain.sem, 1)
                    ve.wait_ge(chain.sem, chain(1))
                    ve.tensor_scalar(ranked, ranked, 0.0, None, ALU.add).then_inc(chain.sem, 1)
                    ve.wait_ge(chain.sem, chain(2))
                    chain.base += 2
                rank_below(ve, chain, ranked, earlier[:, :, :], [lot0[:, :, :, :], lot1[:, :, :, :]], rank[:, :, :],
                           E, 2, used[:, :, :])
                ve.tensor_tensor(used[:, :, :], used[:, :, :], prob[:, :, :], ALU.mult).then_inc(chain.sem, 1)
                ve.wait_ge(chain.sem, chain(1))
                ve.tensor_reduce(total[:, :], used[:, :, :], AX, ALU.add).then_inc(chain.sem, 1)
                ve.wait_ge(chain.sem, chain(2))
                ve.tensor_scalar(total[:, :], total[:, :], 1e-20, None, ALU.add).then_inc(chain.sem, 1)
                ve.wait_ge(chain.sem, chain(3))
                ve.reciprocal(total[:, :], total[:, :]).then_inc(chain.sem, 1)
                ve.wait_ge(chain.sem, chain(4))
                ve.tensor_tensor(used[:, :, :], used[:, :, :], over(total[:, :].unsqueeze(2), [T2, NT, E]),
                                 ALU.mult).then_inc(chain.sem, 1)
                ve.wait_ge(chain.sem, chain(5))
                chain.base += 5
                split_exactly(ve, chain, used[:, :, :], low[:, :, :], [split[:, :, 32 * p:32 * p + E] for p in range(3)])
                ve.tensor_scalar(total[:, :], total[:, :], 1.0, None, ALU.mult).then_inc(cut, 1)


def split_exactly(ve, s, value, low, parts):
    for p, part in enumerate(parts):
        ve.tensor_copy(low, value).then_inc(s.sem, 1)
        ve.wait_ge(s.sem, s(1))
        ve.tensor_copy(part, low).then_inc(s.sem, 1)
        if p < 2:
            ve.tensor_tensor(value, value, low, ALU.subtract).then_inc(s.sem, 1)
        ve.wait_ge(s.sem, s(3 if p < 2 else 2))
        s.base += 3 if p < 2 else 2


def stage_experts0(core):
    nc, d = core.nc, core.dram
    with scope(core, "f0") as (sb, psum):
        parts = sb("parts", [96, T], BF16)
        stage_router(core, "f0r", d["L0_ffn_router_wT"], None, False, parts)
        w1 = sb("w1", [D, E, P])
        w2 = sb("w2", [P, E, D])
        hidden = sb("hidden", [P, E, T])
        rect = sb("rect", [P, 4, CH])
        part = sb("part", [P, 4, CH])
        loads, up, wide, rects, some, all_ = (core.sem(f"f0_{x}") for x in ("loads", "up", "wide", "rects", "some", "all"))
        with scope(core, "f0p") as (_, psum2), nc.Block() as block:
            ph = psum2("ph", [P, 4, 512])
            pw = psum2("pw", [P, 4, 512])

            @block.sync
            def _(sp):
                sp.dma_start(w1[:, :, :], d["L0_ffn_w1"].rearrange("i (e w) -> i e w", e=E)).then_inc(loads, 16)
                sp.dma_start(w2[:, :, :], d["L0_ffn_w2"].rearrange("(e w) o -> w e o", e=E)).then_inc(loads, 16)

            @block.tensor
            def _(pe):
                pe.wait_ge(loads, 32)
                for n in range(NC * E):
                    c, e = n // E, n % E
                    cols = slice(c * CH, (c + 1) * CH)
                    if n >= 4:
                        pe.wait_ge(rects, n - 3)
                    pe.matmul(ph[:, n % 4, 0:CH], w1[:, e, :], core.xT[:, cols], start=True, stop=True).then_inc(up, 1)
                    if n >= 4:
                        pe.wait_ge(some, n - 3)
                    pe.matmul(pw[:, n % 4, 0:CH], core.selector[:, e, :], parts[:, cols], start=True, stop=True).then_inc(wide, 1)

            @block.scalar
            def _(act):
                for n in range(NC * E):
                    act.wait_ge(up, n + 1)
                    if n >= 4:
                        act.wait_ge(all_, n - 3)
                    act.activation(rect[:, n % 4, :], ph[:, n % 4, 0:CH], ACT.Relu).then_inc(rects, 1)

            @block.vector
            def _(ve):
                for n in range(NC * E + 1):
                    if n < NC * E:
                        ve.wait_ge(wide, n + 1)
                        ve.wait_ge(rects, n + 1)
                        ve.tensor_tensor(part[:, n % 4, :], rect[:, n % 4, :], pw[:, n % 4, 0:CH], ALU.mult).then_inc(some, 1)
                    if n:
                        m = n - 1
                        ve.wait_ge(some, m + 1)
                        ve.tensor_tensor(hidden[:, m % E, (m // E) * CH:(m // E + 1) * CH], part[:, m % 4, :],
                                         rect[:, m % 4, :], ALU.mult).then_inc(all_, 1)

        def project(pe, n, out):
            for e in range(E):
                last = pe.matmul(out, hidden[:, e, n * T2:(n + 1) * T2], w2[:, e, :], start=(e == 0), stop=(e == E - 1))
            return last

        stage_norm(core, "f0n", project=project, outT=None)


def stage_experts1(core):
    nc, d = core.nc, core.dram
    PR = E // 2
    half = P // 2

    def both(r):
        return core.selector[:, :, :].rearrange("k r m -> k (r m)")[:, r * P + half:(r + 1) * P + half]

    with scope(core, "f1") as (sb, psum):
        parts = sb("parts", [96, T], BF16)
        stage_router(core, "f1r", d["L1_ffn_gate_weightT"], d["L1_ffn_e_score_correction_bias"], True, parts)
        wg = sb("wg", [D, PR, P])
        wu = sb("wu", [D, PR, P])
        wd = sb("wd", [P, PR, D])
        hidden = sb("hidden", [P, PR, T])
        gate = sb("gate", [P, 2, CH])
        part = sb("part", [P, 2, CH])
        loads, gates, ups, wide, opened, some, all_ = (core.sem(f"f1_{x}") for x in ("loads", "gates", "ups", "wide", "opened", "some", "all"))
        with scope(core, "f1p") as (_, psum2), nc.Block() as block:
            pg, pu, pw = (psum2(x, [P, 2, 512]) for x in ("pg", "pu", "pw"))

            @block.sync
            def _(sp):
                sp.dma_start(wg[:, :, :], d["L1_ffn_gate_projT"].rearrange("i (e w) -> i e w", e=PR)).then_inc(loads, 16)
                sp.dma_start(wu[:, :, :], d["L1_ffn_up_projT"].rearrange("i (e w) -> i e w", e=PR)).then_inc(loads, 16)
                sp.dma_start(wd[:, :, :], d["L1_ffn_down_projT"].rearrange("(e w) o -> w e o", e=PR)).then_inc(loads, 16)

            @block.tensor
            def _(pe):
                pe.wait_ge(loads, 48)
                for n in range(NC * PR):
                    c, e = n // PR, n % PR
                    cols = slice(c * CH, (c + 1) * CH)
                    if n >= 2:
                        pe.wait_ge(opened, n - 1)
                    pe.matmul(pg[:, n % 2, 0:CH], wg[:, e, :], core.xT[:, cols], start=True, stop=True).then_inc(gates, 1)
                    if n >= 2:
                        pe.wait_ge(some, n - 1)
                    pe.matmul(pu[:, n % 2, 0:CH], wu[:, e, :], core.xT[:, cols], start=True, stop=True).then_inc(ups, 1)
                    if n >= 2:
                        pe.wait_ge(all_, n - 1)
                    pe.matmul(pw[:, n % 2, 0:CH], both(2 * e), parts[:, cols],
                              start=True, stop=True).then_inc(wide, 1)

            @block.scalar
            def _(act):
                for n in range(NC * PR):
                    act.wait_ge(gates, n + 1)
                    if n >= 2:
                        act.wait_ge(some, n - 1)
                    act.activation(gate[:, n % 2, :], pg[:, n % 2, 0:CH], ACT.Silu).then_inc(opened, 1)

            @block.vector
            def _(ve):
                for n in range(NC * PR + 1):
                    if n < NC * PR:
                        ve.wait_ge(ups, n + 1)
                        ve.wait_ge(opened, n + 1)
                        if n >= 2:
                            ve.wait_ge(all_, n - 1)
                        ve.tensor_tensor(part[:, n % 2, :], gate[:, n % 2, :], pu[:, n % 2, 0:CH], ALU.mult).then_inc(some, 1)
                    if n:
                        m = n - 1
                        ve.wait_ge(some, m + 1)
                        ve.wait_ge(wide, m + 1)
                        ve.tensor_tensor(hidden[:, m % PR, (m // PR) * CH:(m // PR + 1) * CH], part[:, m % 2, :],
                                         pw[:, m % 2, 0:CH], ALU.mult).then_inc(all_, 1)

        def project(pe, n, out):
            for e in range(PR):
                last = pe.matmul(out, hidden[:, e, n * T2:(n + 1) * T2], wd[:, e, :], start=(e == 0), stop=(e == PR - 1))
            return last

        stage_norm(core, "f1n", project=project, final=True)


def stage_mamba(core):
    nc, d = core.nc, core.dram
    R = 64
    H2 = INNER // P
    with scope(core, "m") as (sb, psum):
        col = sb("col", [P, H2, 12])
        alog = sb("alog", [P, H2, DS])
        sz = sb("sz", [P, H2, T])
        u = sb("u", [P, H2, T])
        dt = sb("dt", [P, H2, T])
        bc3 = sb("bc3", [96, T], BF16)
        wout = sb("wout", [P, H2, D])
        bout = sb("bout", [1, D])
        BIAS_U, BIAS_Z, CONV_B, DT_B, DT_B2, SKIP, TAP = 0, 1, 2, 3, 4, 5, 6
        with scope(core, "mi") as (sb2, _):
            xnT = sb2("xnT", [D, T])
            scale = sb2("scale", [D, 1])
            win = sb2("win", [D, 2 * INNER])
            wdt_in = sb2("wdt_in", [P, H2, R])
            wdt_out = sb2("wdt_out", [R, INNER])
            dtb = sb2("dtb", [R, 1])
            wbc = sb2("wbc", [P, H2, 96])
            bcb = sb2("bcb", [96, 1])
            loads = core.sem("mi_loads")
            with nc.Block() as block:
                @block.vector
                def _(ve):
                    ve.memset(wbc[:, :, :], 0.0)

                @block.sync
                def _(sp):
                    for dst, src in ((col[:, :, :], d["L1_attn_channels"].rearrange("(h p) k -> p h k", p=P)),
                                     (alog[:, :, :], d["L1_attn_a_log"].rearrange("(h p) s -> p h s", p=P)),
                                     (scale[:, :], d["L1_attn_norm_scale"].rearrange("(p a) -> p a", a=1)),
                                     (win[:, :], d["L1_attn_in_proj_w"]),
                                     (wdt_in[:, :, :], d["L1_attn_dt_in_w"].rearrange("(h p) r -> p h r", p=P)),
                                     (wdt_out[:, :], d["L1_attn_dt_out_w"]),
                                     (dtb[:, :], d["L1_attn_dt_in_b"].rearrange("(p a) -> p a", a=1)),
                                     (wout[:, :, :], d["L1_attn_out_proj_w"].rearrange("(h p) o -> p h o", p=P)),
                                     (bout[:, :], d["L1_attn_out_proj_b"].rearrange("(a o) -> a o", a=1))):
                        sp.dma_start(dst, src).then_inc(loads, 16)
                    sp.wait_ge(loads, 9 * 16)
            with nc.Block() as block:
                @block.sync
                def _(sp):
                    for p in range(3):
                        for k, w in enumerate(("b", "c")):
                            at = slice(32 * p + DS * k, 32 * p + DS * (k + 1))
                            sp.dma_start(wbc[:, :, at], d[f"L1_attn_{w}_proj_w"].rearrange("(h p) s -> p h s", p=P)).then_inc(loads, 16)
                            sp.dma_start(bcb[at, :], d[f"L1_attn_{w}_proj_b"].rearrange("(p a) -> p a", a=1)).then_inc(loads, 16)
                    sp.wait_ge(loads, 21 * 16)
            stage_norm(core, "min", rms=True, residual=False, gain=scale[:, 0:1], outT=by_batch(xnT))
            TP = L + 3
            pre = sb2("pre", [P, H2, B, TP])
            dtr = sb2("dtr", [R, T])
            ubias = sb2("ubias", [P, H2])
            bc = sb2("bc", [96, T])
            low = sb2("low", [96, T], BF16)
            e1 = sb2("e1", [P, H2, T])
            names = "neg zero pu pz ur uz conv u pr r pd e pbc bc done".split()
            s = {n: core.sem(f"mi_{n}") for n in names}
            chain = core.shared("mi_chain")
            with scope(core, "mip") as (_, psum2), nc.Block() as block:
                ps = psum2("ps", [P, 8, 512])

                @block.tensor
                def _(pe):
                    for k in range(2 * H2 * NC):
                        if k >= 8:
                            pe.wait_ge(s["ur"], k - 7)
                        pe.matmul(ps[:, k % 8, 0:CH], win[:, (k // NC) * P:(k // NC + 1) * P],
                                  xnT[:, (k % NC) * CH:(k % NC + 1) * CH], start=True, stop=True).then_inc(s["pu"], 1)
                    pe.wait_ge(s["ur"], 4 * NC)
                    for c in range(NC):
                        cols = slice(c * CH, (c + 1) * CH)
                        pe.wait_ge(s["u"], 2)
                        for h in range(H2):
                            last = pe.matmul(ps[0:R, c, 0:CH], wdt_in[:, h, :], u[:, h, cols], start=(h == 0), stop=(h == 1))
                        last.then_inc(s["pr"], 1)
                        for h in range(H2):
                            last = pe.matmul(ps[0:96, 4 + c, 0:CH], wbc[:, h, :], u[:, h, cols], start=(h == 0), stop=(h == 1))
                        last.then_inc(s["pbc"], 1)
                    for k in range(H2 * NC):
                        h, c = k // NC, k % NC
                        pe.wait_ge(s["r"], NC)
                        pe.wait_ge(s["bc"], NC)
                        pe.matmul(ps[:, k, 0:CH], wdt_out[:, h * P:(h + 1) * P], dtr[:, c * CH:(c + 1) * CH],
                                  start=True, stop=True).then_inc(s["pd"], 1)

                @block.scalar
                def _(act):
                    act.wait_ge(s["zero"], 1)
                    for k in range(4 * NC):
                        h, c = (k // NC) % H2, k % NC
                        cols = slice(c * CH, (c + 1) * CH)
                        act.wait_ge(s["pu"], k + 1)
                        if k < 2 * NC:
                            act.activation(pre[:, h, c * BC:(c + 1) * BC, 3:TP],
                                           ps[:, k % 8, 0:CH].rearrange("p (b t) -> p b t", t=L), ACT.Identity,
                                           bias=col[:, h, BIAS_U:BIAS_U + 1]).then_inc(s["ur"], 1)
                        else:
                            act.activation(sz[:, h, cols], ps[:, k % 8, 0:CH], ACT.Silu,
                                           bias=col[:, h, BIAS_Z:BIAS_Z + 1]).then_inc(s["ur"], 1)
                    for h in range(H2):
                        act.wait_ge(s["conv"], 4 * (h + 1))
                        act.activation(u[:, h, :], e1[:, h, :], ACT.Silu, bias=col[:, h, CONV_B:CONV_B + 1]).then_inc(s["u"], 1)
                    for c in range(NC):
                        act.wait_ge(s["pr"], c + 1)
                        act.activation(dtr[:, c * CH:(c + 1) * CH], ps[0:R, c, 0:CH], ACT.Identity, bias=dtb[:, :]).then_inc(s["r"], 1)
                    for c in range(NC):
                        act.wait_ge(s["pbc"], c + 1)
                        act.activation(bc[:, c * CH:(c + 1) * CH], ps[0:96, 4 + c, 0:CH], ACT.Tanh, bias=bcb[:, :]).then_inc(s["bc"], 1)
                    for k in range(H2 * NC):
                        h, c = k // NC, k % NC
                        act.wait_ge(s["neg"], k + 1)
                        act.activation(e1[:, h, c * CH:(c + 1) * CH], e1[:, h, c * CH:(c + 1) * CH],
                                       ACT.Exp).then_inc(s["e"], 1)
                    act.activation(alog[:, :, :], alog[:, :, :], ACT.Exp).then_inc(s["e"], 1)

                @block.vector
                def _(ve):
                    ve.memset(pre[:, :, :, 0:3], 0.0).then_inc(s["zero"], 1)
                    ve.tensor_tensor(ubias[:, :], col[:, :, DT_B], col[:, :, DT_B2], ALU.add).then_inc(s["zero"], 1)
                    for h in range(H2):
                        out = e1[:, h, :].rearrange("p (b t) -> p b t", t=L)
                        ve.wait_ge(s["ur"], (h + 1) * NC)
                        ve.tensor_scalar(out, pre[:, h, :, 0:L], col[:, h, TAP:TAP + 1], None, ALU.mult).then_inc(s["conv"], 1)
                        for k in range(1, 4):
                            ve.wait_ge(s["conv"], 4 * h + k)
                            ve.scalar_tensor_tensor(out, pre[:, h, :, k:k + L], col[:, h, TAP + k:TAP + k + 1], out,
                                                    ALU.mult, ALU.add).then_inc(s["conv"], 1)
                    ve.wait_ge(s["bc"], NC)
                    for p in range(3):
                        ve.tensor_copy(low[:, :], bc[:, :]).then_inc(chain.sem, 1)
                        ve.wait_ge(chain.sem, chain(1))
                        ve.tensor_copy(bc3[32 * p:32 * p + 32, :], low[32 * p:32 * p + 32, :])
                        chain.base += 1
                        if p < 2:
                            for q in range(p + 1, 3):
                                one = slice(32 * q, 32 * q + 32)
                                ve.tensor_tensor(bc[one, :], bc[one, :], low[one, :], ALU.subtract).then_inc(chain.sem, 1)
                            chain.base += 2 - p
                            ve.wait_ge(chain.sem, chain(0))
                    coef = log1p_coefficients(0.11)
                    ve.wait_ge(s["zero"], 2)
                    ve.wait_ge(s["u"], 2)
                    for k in range(H2 * NC):
                        h, c = k // NC, k % NC
                        ve.wait_ge(s["pd"], k + 1)
                        ve.tensor_scalar(e1[:, h, c * CH:(c + 1) * CH], ps[:, k, 0:CH], ubias[:, h:h + 1], 0.0,
                                         ALU.add, ALU.min).then_inc(s["neg"], 1)
                    ve.wait_ge(s["e"], H2 * NC)
                    ve.tensor_scalar(e1[:, :, :], e1[:, :, :], 0.11, None, ALU.min).then_inc(chain.sem, 1)
                    ve.wait_ge(chain.sem, chain(1))
                    ve.tensor_scalar(dt[:, :, :], e1[:, :, :], coef[-1], None, ALU.mult).then_inc(chain.sem, 1)
                    for j, c in enumerate(coef[-2::-1]):
                        ve.wait_ge(chain.sem, chain(2 + j))
                        ve.scalar_tensor_tensor(dt[:, :, :], dt[:, :, :], c, e1[:, :, :], ALU.add, ALU.mult).then_inc(chain.sem, 1)
                    n = len(coef) + 1
                    ve.wait_ge(chain.sem, chain(n))
                    ve.tensor_scalar(dt[:, :, :], dt[:, :, :], 0.001, 0.1, ALU.max, ALU.min).then_inc(chain.sem, 1)
                    ve.wait_ge(s["e"], H2 * NC + 1)
                    ve.tensor_scalar(alog[:, :, :], alog[:, :, :], -1.0, None, ALU.mult)
                    chain.base += n + 1

        gT = sb("gT", [P, H2, T])
        dtu = sb("dtu", [P, H2, T])
        NU = 4
        da = sb("da", [P, NU, CH])
        h_in = sb("h_in", [P, NU, CH])
        hs = sb("hs", [P, NU, CH])
        hc = sb("hc", [P, NU, CH])
        names = "apart dtu decay zeroed wideb widec db scan hc summed out skip".split()
        s = {n: core.sem(f"ms_{n}") for n in names}
        with scope(core, "msp") as (_, psum2), nc.Block() as block:
            pb, pc = psum2("pb", [P, 2, 512]), psum2("pc", [P, 2, 512])
            py = psum2("py", [P, NC, 512])

            def over_states(eng, step):
                for half in range(H2):
                    n0 = half * DS * NC
                    step(half, 0, n0, 0)
                    with eng.Fori(1, DS - 1) as st:
                        step(half, st, st * NC + n0, None)
                    step(half, DS - 1, n0 + (DS - 1) * NC, DS - 1)

            @block.tensor
            def _(pe):
                def wide(half, st, n, k, known):
                    cols = slice(k * CH, (k + 1) * CH)
                    row = (lambda r: core.selector[:, r, :]) if isinstance(st, int) else (
                        lambda r: core.selector[:, bass.ds(r, 1), :].rearrange("p a m -> p (a m)"))
                    if not (half == 0 and known == 0 and k < 2):
                        pe.wait_ge(s["db"], n + k - 1)
                    pe.matmul(pb[:, k % 2, 0:CH], row(st), bc3[:, cols], start=True, stop=True).then_inc(s["wideb"], 1)
                    if not (half == 0 and known == 0 and k < 2):
                        pe.wait_ge(s["hc"], n + k - 1)
                    pe.matmul(pc[:, k % 2, 0:CH], row(st + DS), bc3[:, cols], start=True, stop=True).then_inc(s["widec"], 1)

                def add(half, n, k, known):
                    pe.wait_ge(s["hc"], n + k + 1)
                    if known == 0 and half:
                        pe.wait_ge(s["out"], half * NC)
                    pe.matmul(py[:, k, 0:CH], core.ident[:, :], hc[:, k, :], start=(known == 0),
                              stop=(known == DS - 1)).then_inc(s["summed"], 1)

                pe.sem_inc(s["summed"])
                wide(0, 0, 0, 0, 0)
                wide(0, 0, 0, 1, 0)

                def step(half, st, n, known):
                    after = None if (half == H2 - 1 and known == DS - 1) else (
                        (half + 1, 0, n + NC) if known == DS - 1 else (half, st + 1, n + NC))
                    wide(half, st, n, 2, known)
                    add(half, n, 0, known)
                    wide(half, st, n, 3, known)
                    add(half, n, 1, known)
                    if after:
                        wide(*after, 0, None)
                    add(half, n, 2, known)
                    if after:
                        wide(*after, 1, None)
                    add(half, n, 3, known)
                over_states(pe, step)

            @block.scalar
            def _(act):
                act.wait_ge(s["zeroed"], 1)

                def step(half, st, n, known):
                    for k in range(NC):
                        if not (half == 0 and known == 0):
                            wait_apart(act, s["scan"], n + k - NC + 1, s["apart"])
                        a = alog[:, half, st:st + 1] if isinstance(st, int) else alog[:, half, bass.ds(st, 1)]
                        act.activation(da[:, k, :].rearrange("p (b t) -> p b t", t=L)[:, :, 1:L],
                                       dt[:, half, k * CH:(k + 1) * CH].rearrange("p (b t) -> p b t", t=L)[:, :, 1:L],
                                       ACT.Exp, scale=a).then_inc(s["decay"], 1)
                over_states(act, step)

            @block.vector
            def _(ve):
                ve.memset(da[:, :, 0:CH:L], 0.0).then_inc(s["zeroed"], 1)
                ve.tensor_tensor(dtu[:, :, :], dt[:, :, :], u[:, :, :], ALU.mult).then_inc(s["dtu"], 1)
                ve.wait_ge(s["dtu"], 1)

                def readout(n, k, known, half):
                    ve.wait_ge(s["scan"], n + 1)
                    if not (known == 0 and half == 0):
                        ve.wait_ge(s["summed"], n - NC + 2)
                    ve.tensor_tensor(hc[:, k, :], hs[:, k, :], pc[:, k % 2, 0:CH], ALU.mult).then_inc(s["hc"], 1)

                def step(half, st, n, known):
                    for k in range(NC):
                        ve.wait_ge(s["wideb"], n + k + 1)
                        ve.tensor_tensor(h_in[:, k, :], dtu[:, half, k * CH:(k + 1) * CH], pb[:, k % 2, 0:CH],
                                         ALU.mult).then_inc(s["db"], 1)
                        if k:
                            ve.wait_ge(s["widec"], n + k)
                            readout(n + k - 1, k - 1, known, half)
                        elif known != 0:
                            ve.wait_ge(s["widec"], n)
                            readout(n - 1, NC - 1, None, half)
                        ve.wait_ge(s["decay"], n + k + 1)
                        ve.wait_ge(s["db"], n + k + 1)
                        ve.tensor_tensor_scan(hs[:, k, :], da[:, k, :], h_in[:, k, :], 0.0, ALU.mult,
                                              ALU.add).then_inc(s["scan"], 1)
                    if known == DS - 1:
                        ve.wait_ge(s["widec"], n + NC)
                        readout(n + NC - 1, NC - 1, known, half)
                        for k in range(NC):
                            cols = slice(k * CH, (k + 1) * CH)
                            ve.wait_ge(s["summed"], n + k + 2)
                            ve.scalar_tensor_tensor(gT[:, half, cols], u[:, half, cols], col[:, half, SKIP:SKIP + 1],
                                                    py[:, k, 0:CH], ALU.mult, ALU.add).then_inc(s["out"], 1)
                            ve.wait_ge(s["out"], half * NC + k + 1)
                            ve.tensor_tensor(gT[:, half, cols], gT[:, half, cols], sz[:, half, cols], ALU.mult)
                over_states(ve, step)

        def project(pe, n, out):
            for h in range(H2):
                pe.matmul(out, gT[:, h, n * T2:(n + 1) * T2], wout[:, h, :], start=(h == 0), stop=False)
            return pe.matmul(out, core.ones[0:1, 0:T2], bout[:, :], start=False, stop=True)

        stage_norm(core, "mn", project=project, factor=2.0, outT=by_batch(core.xT))


def log1p_coefficients(top):
    e = top * (0.5 - 0.5 * np.cos(np.pi * (np.arange(400) + 0.5) / 400))
    c = np.polynomial.polynomial.polyfit(e, np.log1p(e) / e, 5)
    return [float(x) for x in c]


H1, DH1 = 16, 8
HP = H1 // 2
LP = 64


def heads_to_features(core, name, att, aT, bias):
    nc = core.nc
    moved, took = core.sem(f"{name}_moved"), core.sem(f"{name}_took")
    with scope(core, name) as (_, psum), nc.Block() as block:
        ps = psum("ps", [P, 2, 512])

        @block.tensor
        def _(pe):
            for b in range(B):
                g, r = b // 4, b % 4
                if g >= 2 and r == 0:
                    pe.wait_ge(took, 2 * (g - 1))
                last = pe.transpose(ps[0:64, g % 2, r * P:(r + 1) * P], att[:, b, :], core.ident[:, :])
                if r == 3:
                    last.then_inc(moved, 1)

        @block.vector
        def _(ve):
            for g in range(B // 4):
                ve.wait_ge(moved, g + 1)
                for h in range(2):
                    dst = aT[:, h, g * 4 * L:(g + 1) * 4 * L].rearrange("p (b t) -> p b t", t=L)
                    src = ps[0:64, g % 2, :].rearrange("p (b h t) -> p h b t", b=4, h=2)[:, h, :, 0:L]
                    if bias is None:
                        ve.tensor_copy(dst, src).then_inc(took, 1)
                    else:
                        ve.tensor_scalar(dst, src, bias[:, h:h + 1], None, ALU.add).then_inc(took, 1)


def stage_causal(core):
    nc, d = core.nc, core.dram
    with scope(core, "c") as (sb, psum):
        wp = sb("wp", [64, 2, D])
        bp = sb("bp", [1, D])
        bv = sb("bv", [64, 2])
        att = sb("att", [P, B, 64])
        aT = sb("aT", [64, 2, T])
        with scope(core, "cl") as (sb2, psum2):
            wqkv = sb2("wqkv", [D, 3, D])
            bqk = sb2("bqk", [D, 2])
            cT = sb2("cT", [D, T])
            qT, kT = sb2("qT", [D, T]), sb2("kT", [D, T])
            v1 = sb2("v1", [P, B, H1, DH1 + 1])
            head = sb2("head", [D, H1])
            causal = sb2("causal", [P, L])
            qblk = sb2("qblk", [D, 2, H1, LP])
            sc = sb2("sc", [P, 2, HP, L])
            top = sb2("top", [P, 2, HP])
            pT = sb2("pT", [P, HP, P])
            rden = sb2("rden", [P, HP, 2])
            own = sb2("own", [P, HP, 2, DH1 + 1])
            loads, built, pre, got = (core.sem(f"cl_{x}") for x in ("loads", "built", "pre", "got"))
            with scope(core, "cq") as (_, psum3), nc.Block() as block:
                ps = psum3("ps", [P, 8, 512])

                @block.sync
                def _(sp):
                    for dst, src in ((wqkv[:, 0, :], d["L1_xattn_Wq"]), (wqkv[:, 1:3, :], d["L1_xattn_Wkv"].rearrange("i (k o) -> i k o", k=2)),
                                     (bqk[:, :], d["L1_xattn_bqk"]), (cT[:, :], d["ctx_headT"]),
                                     (wp[:, :, :], d["L1_xattn_Wp_split"]), (bv[:, :], d["L1_xattn_bv_split"]),
                                     (bp[:, :], d["L1_xattn_bp"].rearrange("(a o) -> a o", a=1))):
                        sp.dma_start(dst, src).then_inc(loads, 16)
                    sp.wait_ge(loads, 7 * 16)

                @block.gpsimd
                def _(pool):
                    cz = causal[:, :]
                    steps = (lambda: pool.memset(head[:, :], 1.0),
                             lambda: pool.affine_select(out=head[:, :], in_=head[:, :], compare_op=ALU.is_ge, fill=0.0, base=0,
                                                        pattern=[[-DH1, H1]], channel_multiplier=1),
                             lambda: pool.affine_select(out=head[:, :], in_=head[:, :], compare_op=ALU.is_ge, fill=0.0, base=DH1 - 1,
                                                        pattern=[[DH1, H1]], channel_multiplier=-1),
                             lambda: pool.memset(qblk[:, :, :, :], 0.0),
                             lambda: pool.memset(att[:, :, :], 0.0),
                             lambda: pool.memset(v1[:, :, :, :], 0.0),
                             lambda: pool.memset(v1[0:L, :, :, DH1:DH1 + 1], 1.0),
                             lambda: pool.memset(pT[:, :, :], 0.0),
                             lambda: pool.memset(cz, 0.0),
                             lambda: pool.affine_select(out=causal[0:LP, :], in_=causal[0:LP, :], compare_op=ALU.is_ge, fill=NEG,
                                                        base=0, pattern=[[-1, L]], channel_multiplier=1),
                             lambda: pool.affine_select(out=causal[LP:P, :], in_=causal[LP:P, :], compare_op=ALU.is_ge, fill=NEG,
                                                        base=0, pattern=[[-1, L]], channel_multiplier=1))
                    for n, make in enumerate(steps):
                        make().then_inc(built, 1)
                        pool.wait_ge(built, n + 1)

                @block.tensor
                def _(pe):
                    pe.wait_ge(loads, 7 * 16)
                    for k in range(2 * NC):
                        c = k % NC
                        if k >= 4:
                            pe.wait_ge(got, k - 3)
                        pe.matmul(ps[:, k % 4, 0:CH], wqkv[:, k // NC, :], (core.xT, cT)[k // NC][:, c * CH:(c + 1) * CH],
                                  start=True, stop=True).then_inc(pre, 1)
                    for g in range(B // 4):
                        if g >= 4:
                            pe.wait_ge(got, 2 * NC + g - 3)
                        for r in range(4):
                            b = 4 * g + r
                            last = pe.matmul(ps[0:L, 4 + g % 4, r * D:(r + 1) * D], cT[:, b * L:(b + 1) * L], wqkv[:, 2, :],
                                             start=True, stop=True)
                        last.then_inc(pre, 1)

                @block.vector
                def _(ve):
                    ve.wait_ge(loads, 7 * 16)
                    ve.wait_ge(built, 8)
                    for k in range(2 * NC):
                        ve.wait_ge(pre, k + 1)
                        dst = (qT, kT)[k // NC][:, (k % NC) * CH:(k % NC + 1) * CH]
                        ve.tensor_scalar(dst, ps[:, k % 4, 0:CH], bqk[:, k // NC:k // NC + 1], None, ALU.add).then_inc(got, 1)
                    for g in range(B // 4):
                        ve.wait_ge(pre, 2 * NC + g + 1)
                        ve.tensor_copy(v1[0:L, 4 * g:4 * g + 4, :, 0:DH1],
                                       ps[0:L, 4 + g % 4, :].rearrange("p (b h e) -> p b h e", b=4, h=H1)).then_inc(got, 1)

            names = "apart q raw masked top less probs turned pT val own rden att".split()
            s = {n: core.sem(f"cl_{n}") for n in names}
            SCALE = 1.0 / float(np.sqrt(DH1))
            with scope(core, "clp") as (_, psum3), nc.Block() as block:
                pA, pT2 = psum3("pA", [P, 2, 512]), psum3("pT2", [P, 2, 512])
                VA = H1 * (DH1 + 1)
                pV = psum3("pV", [P, 3, 512])

                def values_at(hp):
                    return hp // 3, slice((hp % 3) * VA, (hp % 3 + 1) * VA)

                def run(eng, step):
                    for n in range(4):
                        step(n, n, n // 2)
                    with eng.Fori(2, B // 2) as i:
                        for j in range(2):
                            step(i * 2 + j, 4 + j, i)
                    for n in range(B, B + 2):
                        step(n, n, n // 2)

                @block.gpsimd
                def _(pool):
                    def step(n, k, pair):
                        if k < B:
                            if k > 1:
                                pool.wait_ge(s["raw"], n - 1)
                            pool.tensor_tensor(qblk[:, k % 2, :, 0:L], over(qT[:, bass.ds(n * L, L)].unsqueeze(1), [D, H1, L]),
                                               over(head[:, :].unsqueeze(2), [D, H1, L]), ALU.mult).then_inc(s["q"], 1)
                    run(pool, step)

                @block.tensor
                def _(pe):
                    def step(n, k, pair):
                        if k < B:
                            pe.wait_ge(s["q"], n + 1)
                            if k:
                                pe.wait_ge(s["masked"], n)
                            for hp in range(HP):
                                last = pe.matmul(pA[:, hp // 4, (hp % 4) * T2:(hp % 4 + 1) * T2],
                                                 qblk[:, k % 2, 2 * hp:2 * hp + 2, :], kT[:, bass.ds(pair * T2, T2)],
                                                 start=True, stop=True)
                            last.then_inc(s["raw"], 1)
                        if k > 1:
                            pe.wait_ge(s["pT"], n - 1)
                            if k > 2:
                                pe.wait_ge(s["att"], n - 2)
                            for hp in range(HP):
                                bank, cols = values_at(hp)
                                last = pe.matmul(pV[:, bank, cols], pT[:, hp, :], v1[:, bass.ds(n - 2, 1), :, :],
                                                 start=True, stop=True)
                            last.then_inc(s["val"], 1)
                        if 1 <= k < B + 1:
                            wait_apart(pe, s["probs"], n, s["apart"])
                            for hp in range(HP):
                                last = pe.transpose(pT2[0:L, hp // 4, (hp % 4) * P:(hp % 4 + 1) * P], sc[:, (k - 1) % 2, hp, :],
                                                    core.ident[:, :])
                            last.then_inc(s["turned"], 1)
                    run(pe, step)

                @block.scalar
                def _(act):
                    def step(n, k, pair):
                        if 1 <= k < B + 1:
                            act.wait_ge(s["turned"], n)
                            if k > 1:
                                act.wait_ge(s["val"], n - 1)
                            act.activation(pT[0:L, :, :].rearrange("p (g h) q -> p g (h q)", g=2), pT2[0:L, :, :],
                                           ACT.Copy).then_inc(s["pT"], 1)
                        if k < B:
                            act.wait_ge(s["less"], n + 1)
                            act.activation(sc[:, k % 2, :, :], sc[:, k % 2, :, :], ACT.Exp, scale=SCALE).then_inc(s["probs"], 1)
                    run(act, step)

                @block.vector
                def _(ve):
                    def step(n, k, pair):
                        if k < B:
                            buf = k % 2
                            ve.wait_ge(s["raw"], n + 1)
                            if k > 1:
                                ve.wait_ge(s["turned"], n - 1)
                            for g in range(2):
                                last = ve.tensor_tensor(sc[:, buf, 4 * g:4 * g + 4, :],
                                                        pA[:, g, 0:4 * T2].rearrange("p (h j t) -> p h j t", h=4, j=2)[:, :, k % 2, :],
                                                        over(causal[:, :].unsqueeze(1), [P, 4, L]), ALU.add)
                            last.then_inc(s["masked"], 1)
                            ve.wait_ge(s["masked"], n + 1)
                            ve.tensor_reduce(top[:, buf, :], sc[:, buf, :, :], AX, ALU.max).then_inc(s["top"], 1)
                        if k > 1:
                            ve.wait_ge(s["val"], n - 1)
                            for hp in range(HP):
                                bank, cols = values_at(hp)
                                pair_of = pV[:, bank, cols].rearrange("p (h k e) -> p h k e", k=2, e=DH1 + 1)[:, hp]
                                last = ve.tensor_copy(own[:, hp, :, :], pair_of)
                            last.then_inc(s["own"], 1)
                            ve.wait_ge(s["own"], n - 1)
                            ve.reciprocal(rden[:, :, :], own[:, :, :, DH1]).then_inc(s["rden"], 1)
                        if k < B:
                            ve.wait_ge(s["top"], n + 1)
                            ve.tensor_tensor(sc[:, buf, :, :], sc[:, buf, :, :], over(top[:, buf, :].unsqueeze(2), [P, HP, L]),
                                             ALU.subtract).then_inc(s["less"], 1)
                        if k > 1:
                            ve.wait_ge(s["rden"], n - 1)
                            for par in range(2):
                                rows = slice(par * LP, par * LP + L)
                                last = ve.tensor_tensor(att[rows, bass.ds(n - 2, 1), :].rearrange("p a (h e) -> p (a h) e", e=DH1),
                                                        own[rows, :, par, 0:DH1], over(rden[rows, :, par].unsqueeze(2), [L, HP, DH1]),
                                                        ALU.mult)
                            last.then_inc(s["att"], 1)
                    run(ve, step)

        heads_to_features(core, "ch", att, aT, bv)

        def project(pe, n, out):
            for h in range(2):
                pe.matmul(out, aT[:, h, n * T2:(n + 1) * T2], wp[:, h, :], start=(h == 0), stop=False)
            return pe.matmul(out, core.ones[0:1, 0:T2], bp[:, :], start=False, stop=True)

        stage_norm(core, "cn", project=project, outT=by_batch(core.xT))



def program(nc, dram, out):
    with ExitStack() as ctx:
        core = Core(nc, dram, out, ctx)
        stage_constants(core)
        for stage in (stage_scan, stage_attention, stage_experts0, stage_mamba, stage_causal, stage_experts1):
            stage(core)


_HOST = {
    "L0_ffn_router_wT": lambda i: i["L0_ffn_router_w"].T,
    "L1_ffn_gate_weightT": lambda i: i["L1_ffn_gate_weight"].T,
    "L1_ffn_gate_projT": lambda i: i["L1_ffn_gate_proj"].reshape(-1, D).T,
    "L1_ffn_up_projT": lambda i: i["L1_ffn_up_proj"].reshape(-1, D).T,
    "L1_ffn_down_projT": lambda i: i["L1_ffn_down_proj"].transpose(0, 2, 1).reshape(-1, D),
    "L1_attn_channels": lambda i: np.concatenate([_channels(i), i["L1_attn_conv_kernel"].T,
                                                  np.zeros((INNER, 2), np.float32)], axis=1),
    "L1_xattn_bqk": lambda i: np.stack([i["L1_xattn_bq"], i["L1_xattn_bkv"][:D]], axis=1),
    "L1_xattn_Wp_split": lambda i: i["L1_xattn_Wp"].reshape(8, 2, 8, D).transpose(0, 2, 1, 3).reshape(64, 2, D),
    "L1_xattn_bv_split": lambda i: i["L1_xattn_bkv"][D:].reshape(8, 2, 8).transpose(0, 2, 1).reshape(64, 2),
    "ctx_headT": lambda i: i["ctx_1024"][:, :L].transpose(2, 0, 1).reshape(D, T),
    "L0_xattn_ln": lambda i: _stack(i, "L0_xattn_ln_x_g", "L0_xattn_ln_x_b", "L0_xattn_ln_l_g", "L0_xattn_ln_l_b"),
    "L0_attn_in_proj_wT": lambda i: i["L0_attn_in_proj_w"].T,
    "L0_attn_ln": lambda i: _stack(i, "L0_attn_ln_w", "L0_attn_ln_b"),
    "L0_attn_out_proj_wT": lambda i: i["L0_attn_out_proj_w"].T,
}
_PLAIN = ["mask_BxS2_bk0", "L0_ffn_w1", "L0_ffn_w2", "L1_ffn_e_score_correction_bias", "L1_attn_a_log", "L1_attn_norm_scale",
          "L1_attn_in_proj_w", "L1_attn_dt_in_w", "L1_attn_dt_out_w", "L1_attn_dt_in_b", "L1_attn_out_proj_w",
          "L1_attn_out_proj_b", "L1_attn_b_proj_w", "L1_attn_c_proj_w", "L1_attn_b_proj_b", "L1_attn_c_proj_b",
          "L1_xattn_Wq", "L1_xattn_Wkv", "L1_xattn_bp",
          "ctx_1024", "L0_xattn_q_gamma", "L0_xattn_k_gamma", "L0_xattn_W_q", "L0_xattn_W_kv", "L0_xattn_W_out",
          "L0_xattn_b_out",
          "x", "L0_attn_A_log", "L0_attn_B_mat", "L0_attn_C_mat"]


def _channels(i):
    b = i["L1_attn_in_proj_b"]
    return np.stack([b[:INNER], b[INNER:], i["L1_attn_conv_bias"], i["L1_attn_dt_out_b"], i["L1_attn_dt_bias"],
                     i["L1_attn_d"]], axis=1)


def _stack(i, *names):
    return np.stack([np.asarray(i[n]) for n in names], axis=1)


def kernel(**inputs):
    import concourse.bacc as _bacc
    from concourse.bass_utils import run_bass_kernel_spmd as _run

    inputs = {k: np.asarray(v) for k, v in inputs.items()}
    laid = {n: inputs[n] for n in _PLAIN} | {n: f(inputs) for n, f in _HOST.items()}
    nc = _bacc.Bacc("TRN2", target_bir_lowering=False, num_devices=1)
    arrays, dram = {}, {}
    for name, a in laid.items():
        a = np.ascontiguousarray(a)
        arrays[f"in_{name}"] = a
        dram[name] = nc.dram_tensor(f"in_{name}", a.shape, mybir.dt.from_np(a.dtype), kind="ExternalInput").ap()
    out = nc.dram_tensor("out_dram", (B, L, D), F32, kind="ExternalOutput").ap()
    program(nc, dram, out)
    r = _run(nc, [arrays], core_ids=[0])
    return r.results[0]["out_dram"]
```

```python
from contextlib import ExitStack, contextmanager

import numpy as np

import concourse.bass as bass
from concourse import mybir

ALU = mybir.AluOpType
ACT = mybir.ActivationFunctionType
F32 = mybir.dt.float32
BF16 = mybir.dt.bfloat16
U8 = mybir.dt.uint8
AX = mybir.AxisListType.X
RMAX = bass.bass_isa.ReduceOp.max

P = 128
B, L, D = 32, 56, 128
T = B * L
T2 = 2 * L
NT = T // T2
NC = 4
CH = T // NC
BC = B // NC
TPC = NT // NC
INNER = 256
DS = 16
S2 = 1500
KP = 125
KT = S2 // KP
NX = 4
E = 8
NEG = -(2.0 ** 100)
LN_EPS = 1e-5
DT_TOP = 0.11


class Counted:

    def __init__(self, sem):
        self.sem, self.base = sem, 0

    def __call__(self, count):
        return self.base + count


def wait_apart(eng, sem, count, spare):
    eng.wait_ge(sem, count)
    eng.sem_inc(spare)


class Core:

    def __init__(self, nc, dram, out, ctx):
        self.nc, self.dram, self.out, self.ctx = nc, dram, out, ctx
        self.counted = {}
        self.apart = self.sem("apart")

    def sb(self, name, shape, dt=F32):
        return self.ctx.enter_context(self.nc.sbuf_tensor(name, shape, dt))

    def sem(self, name):
        return self.ctx.enter_context(self.nc.semaphore(name))

    def shared(self, name):
        if name not in self.counted:
            self.counted[name] = Counted(self.sem(name))
        return self.counted[name]


@contextmanager
def scope(core, stage):
    with ExitStack() as ctx:
        def sb(name, shape, dt=F32):
            return ctx.enter_context(core.nc.sbuf_tensor(f"{stage}_{name}", shape, dt))

        def psum(name, shape, dt=F32):
            return ctx.enter_context(core.nc.psum_tensor(f"{stage}_{name}", shape, dt))

        yield sb, psum


LN_EXP_TABLES = 6


def load_tables(nc, act, tables):
    act.add_instruction(mybir.InstLoadActFuncSet(act_func_set_id=tables, name=nc.get_next_instruction_name()))


def over(ap, shape):
    return ap.broadcast_to(shape)


def stage_constants(core):
    nc = core.nc
    core.ident = core.sb("ident", [P, P])
    core.ones = core.sb("ones", [P, P])
    core.eps_ln = core.sb("eps_ln", [P, 1])
    core.eps_rms = core.sb("eps_rms", [P, 1])
    core.selector = core.sb("selector", [96, 32, P], BF16)
    core.x_tm = core.sb("x_tm", [T2, NT, D])
    core.xT = core.sb("xT", [D, T])
    zeroed, loaded = core.sem("const_zeroed"), core.sem("const_loaded")
    with nc.Block() as block:
        @block.gpsimd
        def _(pool):
            pool.memset(core.ident[:, :], 0.0).then_inc(zeroed, 1)
            pool.memset(core.ones[:, :], 1.0)
            pool.memset(core.eps_ln[:, :], LN_EPS)
            pool.memset(core.eps_rms[:, :], 1e-6)
            pool.wait_ge(zeroed, 1)
            pool.affine_select(out=core.ident[:, :], in_=core.ident[:, :], compare_op=ALU.not_equal,
                               fill=1.0, base=0, pattern=[[-1, P]], channel_multiplier=1)
        @block.sync
        def _(sp):
            sp.dma_start(core.x_tm[:, :, :], core.dram["x"].rearrange("b t d -> (b t) d")
                         .rearrange("(n p) d -> p n d", p=T2)).then_inc(loaded, 16)
            sp.wait_ge(loaded, 16)


def stage_norm(core, name, project=None, factor=1.0, rms=False, gain=None, shift=None,
               residual=True, outT=None, final=False):
    nc = core.nc
    projected, added, stats, moments = (core.shared(s) for s in ("n_proj", "n_add", "n_stats", "n_moments"))
    roots, scales, normed, turned, kept = (core.shared(s) for s in ("n_roots", "n_scales", "n_normed", "n_turned", "n_kept"))
    squared = core.shared("n_squared")
    with scope(core, name) as (sb, psum):
        y = psum("y", [P, NC, 512]) if project else None
        xt = psum("xt", [P, NC, 512]) if outT else None
        z = sb("z", [T2, NT, D]) if project else core.x_tm
        keep = core.x_tm if residual else sb("keep", [T2, NT, D])
        raw = sb("raw", [T2, NT, 6])
        mv = sb("mv", [T2, NT, 2])
        std = sb("std", [T2, NT])
        rstd = sb("rstd", [T2, NT])
        offset = sb("offset", [T2, NT])
        with nc.Block() as block:
            @block.tensor
            def _(pe):
                for c in range(NC + 2):
                    if c < NC and project:
                        for n in range(c * TPC, (c + 1) * TPC):
                            r = n % TPC
                            last = project(pe, n, y[0:T2, c, r * D:(r + 1) * D])
                        last.then_inc(projected.sem, 1)
                    if c >= 2 and outT:
                        pe.wait_ge(normed.sem, normed(c - 1))
                        for r in range(TPC):
                            last = pe.transpose(xt[:, c - 2, r * T2:(r + 1) * T2], keep[:, (c - 2) * TPC + r, :],
                                                core.ident[0:T2, 0:T2])
                        last.then_inc(turned.sem, 1)

            @block.vector
            def _(ve):
                def statistics(c):
                    tiles = slice(c * TPC, (c + 1) * TPC)
                    if project:
                        ve.wait_ge(projected.sem, projected(c + 1))
                        ve.scalar_tensor_tensor(z[:, tiles, :], core.x_tm[:, tiles, :], factor,
                                                y[0:T2, c, :].rearrange("p (r d) -> p r d", d=D),
                                                ALU.mult, ALU.add).then_inc(added.sem, 1)
                        ve.wait_ge(added.sem, added(c + 1))
                    for n in range(c * TPC, (c + 1) * TPC):
                        last = ve.bn_stats(raw[:, n, :], z[:, n, :])
                    last.then_inc(stats.sem, 1)
                    ve.wait_ge(stats.sem, stats(c + 1))
                    for n in range(c * TPC, (c + 1) * TPC):
                        last = ve.bn_aggr(mv[:, n, :], raw[:, n, :])
                    last.then_inc(moments.sem, 1)
                    if rms:
                        ve.wait_ge(moments.sem, moments(c + 1))
                        ve.tensor_tensor(offset[:, tiles], mv[:, tiles, 0], mv[:, tiles, 0], ALU.mult).then_inc(squared.sem, 1)
                        ve.wait_ge(squared.sem, squared(2 * c + 1))
                        ve.tensor_tensor(mv[:, tiles, 1], mv[:, tiles, 1], offset[:, tiles], ALU.add).then_inc(squared.sem, 1)

                def scale_and_offset(c):
                    tiles = slice(c * TPC, (c + 1) * TPC)
                    ve.wait_ge(roots.sem, roots(c + 1))
                    ve.reciprocal(rstd[:, tiles], std[:, tiles]).then_inc(scales.sem, 1)
                    ve.wait_ge(scales.sem, scales(2 * c + 1))
                    ve.scalar_tensor_tensor(offset[:, tiles], mv[:, tiles, 0], 0.0 if rms else -1.0,
                                            rstd[:, tiles], ALU.mult, ALU.mult).then_inc(scales.sem, 1)

                def take(c):
                    ve.wait_ge(turned.sem, turned(c + 1))
                    if gain is None:
                        ve.tensor_copy(outT(c)[0], outT(c)[1](xt[:, c, 0:CH]))
                    elif shift is None:
                        ve.tensor_scalar(outT(c)[0], outT(c)[1](xt[:, c, 0:CH]), gain, None, ALU.mult)
                    else:
                        ve.tensor_scalar(outT(c)[0], outT(c)[1](xt[:, c, 0:CH]), gain, shift, ALU.mult, ALU.add)

                for c in range(NC + 3):
                    if c < NC:
                        statistics(c)
                    if 1 <= c < NC + 1:
                        scale_and_offset(c - 1)
                    if c >= 3 and outT:
                        take(c - 3)

            @block.scalar
            def _(act):
                eps = core.eps_rms if rms else core.eps_ln
                for c in range(NC + 1):
                    if c < NC:
                        tiles = slice(c * TPC, (c + 1) * TPC)
                        if rms:
                            act.wait_ge(squared.sem, squared(2 * c + 2))
                        else:
                            act.wait_ge(moments.sem, moments(c + 1))
                        act.activation(std[:, tiles], mv[:, tiles, 1], ACT.Sqrt, bias=eps[0:T2, :]).then_inc(roots.sem, 1)
                    if c:
                        act.wait_ge(scales.sem, scales(2 * c))
                        for n in range((c - 1) * TPC, c * TPC):
                            last = act.activation(keep[:, n, :], z[:, n, :], ACT.Identity,
                                                  bias=offset[:, n:n + 1], scale=rstd[:, n:n + 1])
                        last.then_inc(normed.sem, 1)

            if final:
                @block.sync
                def _(sp):
                    rows = core.out.rearrange("b t d -> (b t) d").rearrange("(n p) d -> p n d", p=T2)
                    for c in range(NC):
                        tiles = slice(c * TPC, (c + 1) * TPC)
                        sp.wait_ge(normed.sem, normed(c + 1))
                        sp.dma_start(rows[:, tiles, :], keep[:, tiles, :]).then_inc(kept.sem, 16)
                    sp.wait_ge(kept.sem, kept(16 * NC))
        projected.base += NC if project else 0
        added.base += NC if project else 0
        stats.base += NC
        moments.base += NC
        squared.base += 2 * NC if rms else 0
        roots.base += NC
        scales.base += 2 * NC
        normed.base += NC
        turned.base += NC if outT else 0


def by_batch(xT):
    return lambda c: (xT[:, c * CH:(c + 1) * CH], lambda ap: ap)


GB = 4
NB = INNER * DS // P // GB


def stage_scan(core):
    nc, d = core.nc, core.dram
    NG = INNER * DS // P
    CPG = P // DS
    with scope(core, "l0s") as (sb, psum):
        xnT = sb("xnT", [D, L, B])
        yT = sb("yT", [P, 2, L, B])
        win = sb("win", [D, 2 * INNER])
        lnw = sb("lnw", [D, 2])
        loads, loads2 = core.sem("l0s_loads"), core.sem("l0r_loads")
        scan_scope = ExitStack()
        sb2, _ = scan_scope.enter_context(scope(core, "l0r"))
        u = sb2("u", [P, 2, L, 2, GB * B])
        wexp = sb2("wexp", [D, NG, P])
        cexp = sb2("cexp", [P, NG, P])
        brow = u[:, 1].rearrange("p t r x -> p (t r x)")[:, 0:NG * P]
        c_gp = sb2("c_gp", [NG, 2, P])
        cA = sb2("cA", [P, 2, NG])
        mine = sb2("mine", [P, CPG])
        a_col = sb2("a_col", [P, 1])
        with nc.Block() as block:
            @block.sync
            def _(sp):
                sp.dma_start(win[:, :], d["L0_attn_in_proj_wT"]).then_inc(loads, 16)
                sp.dma_start(lnw[:, :], d["L0_attn_ln"]).then_inc(loads, 16)
                sp.dma_start(brow, d["L0_attn_B_mat"].rearrange("i s -> (i s)")
                             .partition_broadcast(P)).then_inc(loads2, 16)
                sp.dma_start(c_gp[:, 0, :], d["L0_attn_C_mat"].rearrange("(g i) s -> g (i s)", i=CPG)).then_inc(loads2, 16)
                sp.dma_start(c_gp[:, 1, :], d["L0_attn_A_log"].rearrange("(g i) s -> g (i s)", i=CPG)).then_inc(loads2, 16)
                sp.wait_ge(loads, 32)
        stage_norm(core, "l0n", residual=False, gain=lnw[:, 0:1], shift=lnw[:, 1:2],
                   outT=lambda c: (xnT[:, :, c * BC:(c + 1) * BC].rearrange("p t b -> p b t"),
                                   lambda ap: ap.rearrange("p (b t) -> p b t", t=L)))
        with scan_scope, scope(core, "l0rp") as (_, psum2):
            pu = psum2("pu", [P, 4, 512])
            py = psum2("py", [P, 4, 512])
            built, turned, got = (core.sem(f"l0r_{s}") for s in ("built", "turned", "got"))
            step_done, u_made, filled_outer, filled_middle = (core.sem(f"l0r_{s}") for s in ("step", "u_made", "outer", "middle"))
            y_read, y_taken = (core.sem(f"l0r_{s}") for s in ("y_read", "y_taken"))
            with nc.Block() as block:
                @block.gpsimd
                def _(pool):
                    pool.memset(mine[:, :], 1.0).then_inc(built, 1)
                    pool.memset(cexp[:, :, :], 0.0).then_inc(built, 1)
                    pool.wait_ge(built, 1)
                    pool.affine_select(out=mine[:, :], in_=mine[:, :], compare_op=ALU.is_ge, fill=0.0,
                                       base=0, pattern=[[-DS, CPG]], channel_multiplier=1).then_inc(built, 1)
                    pool.wait_ge(built, 3)
                    pool.affine_select(out=mine[:, :], in_=mine[:, :], compare_op=ALU.is_ge, fill=0.0,
                                       base=DS - 1, pattern=[[DS, CPG]], channel_multiplier=-1).then_inc(built, 1)

                @block.tensor
                def _(pe):
                    pe.wait_ge(loads2, 48)
                    for k in range(2):
                        pe.transpose(pu[:, 0, k * NG:(k + 1) * NG], c_gp[:, k, :], core.ident[0:NG, 0:NG]).then_inc(turned, 1)

                @block.scalar
                def _(act):
                    act.wait_ge(turned, 2)
                    act.activation(cA[:, 0, :], pu[:, 0, 0:NG], ACT.Copy).then_inc(got, 1)
                    act.activation(cA[:, 1, :], pu[:, 0, NG:2 * NG], ACT.Exp).then_inc(got, 1)

                @block.vector
                def _(ve):
                    ve.wait_ge(loads2, 48)
                    ve.tensor_tensor(wexp[:, :, :].rearrange("p g (i s) -> p (g i) s", s=DS),
                                     over(win[:, 0:INNER].unsqueeze(2), [D, INNER, DS]),
                                     brow.rearrange("p (i s) -> p i s", s=DS), ALU.mult)
                    ve.wait_ge(got, 2)
                    ve.tensor_scalar(cA[:, 1, :], cA[:, 1, :], -0.01, -10.0, ALU.min, ALU.max).then_inc(got, 1)
                    ve.wait_ge(got, 3)
                    ve.tensor_reduce(a_col[:, :], cA[:, 1, :], AX, ALU.min, negate=True)

            selector = core.selector
            made_selector, made_cexp = core.sem("l0r_selector"), core.sem("l0r_cexp")
            per_block = 2 * 2 * (L - 1) + 2
            QT = L // NC
            middle, outer = (1, 2), (0, 3)
            filled = {middle: filled_middle, outer: filled_outer}
            copies = 2 * 2 * GB

            def fill_order(k):
                return (outer, middle) if k == 0 else (middle, outer)

            read_of = [(filled[quarters], k * copies + 2 * (i + 1))
                       for k in range(NB) for quarters in fill_order(k) for i in range(2 * GB)]

            def scanned(k, step):
                return k * per_block + 2 + 4 * step

            def half_done(k):
                return k % (NB // 2) == NB // 2 - 1

            with nc.Block() as block:
                @block.tensor
                def _(pe):
                    def inputs_of(k, quarters, n):
                        for gl in range(GB):
                            for c in quarters:
                                if n >= 4:
                                    pe.wait_ge(*read_of[n - 4])
                                pe.matmul(pu[:, n % 4, 0:CH], wexp[:, k * GB + gl, :],
                                          xnT[:, c * QT:(c + 1) * QT, :], start=True, stop=True).then_inc(u_made, 1)
                                n += 1
                        return n

                    def sums_of(k, c):
                        pe.wait_ge(step_done, scanned(k, (c + 1) * QT - 1))
                        for r in range(2):
                            bank = NC - 1 - c if r else c
                            for gl in range(GB):
                                h = u[:, k % 2, c * QT:(c + 1) * QT, r, gl * B:(gl + 1) * B]
                                last = pe.matmul(py[:, bank, 0:CH], cexp[:, k * GB + gl, :], h[:, ::-1, :] if r else h,
                                                 start=(k % (NB // 2) == 0 and gl == 0 and c < 2),
                                                 stop=(half_done(k) and gl == GB - 1 and c >= 2))
                        return last

                    n_u = 0
                    for k in range(2):
                        for quarters in fill_order(k):
                            n_u = inputs_of(k, quarters, n_u)
                    for k in range(NB):
                        if k == 0:
                            pe.wait_ge(made_cexp, 1)
                        if k == NB // 2:
                            pe.wait_ge(y_taken, NC)
                        sums_of(k, 0)
                        sums_of(k, 1)
                        sums_of(k, 2).then_inc(y_read, 1)
                        if k + 2 < NB:
                            n_u = inputs_of(k + 2, middle, n_u)
                        sums_of(k, 3).then_inc(y_read, 1)
                        if k + 2 < NB:
                            n_u = inputs_of(k + 2, outer, n_u)

                @block.gpsimd
                def _(pool):
                    for g in range(NG):
                        at = (g % (P // CPG)) * CPG
                        last = pool.tensor_scalar(cexp[:, g, at:at + CPG], mine[:, :], cA[:, 0, g:g + 1], None, ALU.mult)
                    last.then_inc(made_cexp, 1)
                    pool.memset(selector[:, :, :], 0.0).then_inc(made_selector, 1)
                    for part in range(3):
                        pool.wait_ge(made_selector, 1 + part)
                        pool.affine_select(out=selector[:, :, :], in_=selector[:, :, :], compare_op=ALU.not_equal,
                                           fill=1.0, base=-32 * part, pattern=[[-1, 32], [0, P]],
                                           channel_multiplier=1).then_inc(made_selector, 1)

                @block.scalar
                def _(act):
                    def fill(k, quarters, n):
                        for gl in range(GB):
                            for c in quarters:
                                act.wait_ge(u_made, n + 1)
                                src = pu[:, n % 4, 0:CH].rearrange("p (t b) -> p t b", b=B)
                                at = slice(gl * B, (gl + 1) * B)
                                t0 = c * QT
                                act.activation(u[:, k % 2, t0:t0 + QT, 0, at], src, ACT.Copy).then_inc(filled[quarters], 1)
                                back = u[:, k % 2, L - t0 - QT:L - t0, 1, at][:, ::-1, :]
                                act.activation(back, src, ACT.Copy).then_inc(filled[quarters], 1)
                                n += 1
                        return n

                    def keep_sums(half, quarters):
                        for c in quarters:
                            act.activation(yT[:, half, c * QT:(c + 1) * QT, :],
                                           py[:, c, 0:CH].rearrange("p (t b) -> p t b", b=B),
                                           ACT.Copy, scale=0.5).then_inc(y_taken, 1)

                    n = 0
                    for k in range(2):
                        for quarters in fill_order(k):
                            n = fill(k, quarters, n)
                    for k in range(NB):
                        for m, quarters in enumerate((middle, outer)):
                            act.wait_ge(y_read, 2 * k + m + 1)
                            if half_done(k):
                                keep_sums(k // (NB // 2), quarters)
                            if k + 2 < NB:
                                if m == 0:
                                    act.wait_ge(step_done, scanned(k, 3 * QT))
                                n = fill(k + 2, quarters, n)

                @block.vector
                def _(ve):
                    w = GB * B
                    with ve.Fori(0, NB // 2) as pair:
                        for m in range(2):
                            wait_apart(ve, filled_outer, pair * (2 * copies) + (m + 1) * copies, core.apart)
                            x = u[:, m].rearrange("p t r x -> p t (r x)")
                            for r in range(2):
                                first = x[:, 0, r * w:(r + 1) * w]
                                ve.tensor_scalar(first, first, 10.0, -10.0, ALU.min, ALU.max).then_inc(step_done, 1)
                            base = scanned(m, 0)
                            for t in range(1, L):
                                if t == QT:
                                    wait_apart(ve, filled_middle, pair * (2 * copies) + (m + 1) * copies, core.apart)
                                for r in range(2):
                                    prev, cur = (x[:, t - 1 + i, r * w:(r + 1) * w] for i in range(2))
                                    ve.wait_ge(step_done, pair * (2 * per_block) + (base + 4 * (t - 1) + r - 1))
                                    ve.scalar_tensor_tensor(cur, prev, a_col[:, :], cur, ALU.mult,
                                                            ALU.add).then_inc(step_done, 1)
                                for r in range(2):
                                    cur = x[:, t, r * w:(r + 1) * w]
                                    ve.wait_ge(step_done, pair * (2 * per_block) + (base + 4 * (t - 1) + r + 1))
                                    ve.tensor_scalar(cur, cur, 10.0, -10.0, ALU.min, ALU.max).then_inc(step_done, 1)

        with scope(core, "l0g") as (sb2, psum2):
            gate = sb2("gate", [P, 2, T])
            gT = sb2("gT", [P, 2, T])
            wout = sb2("wout", [P, 2, D])
            made, opened, wl = (core.sem(f"l0g_{s}") for s in ("made", "opened", "loads"))
            with scope(core, "l0gp") as (_, psum3), nc.Block() as block:
                pg = psum3("pg", [P, 8, 512])

                @block.sync
                def _(sp):
                    sp.dma_start(wout[:, :, :], d["L0_attn_out_proj_wT"].rearrange("(h p) d -> p h d", p=P)).then_inc(wl, 16)
                    sp.wait_ge(wl, 16)

                @block.tensor
                def _(pe):
                    for h in range(2):
                        for c in range(NC):
                            pe.matmul(pg[:, h * NC + c, 0:CH], win[:, INNER + h * P:INNER + (h + 1) * P],
                                      xnT[:, c * 14:(c + 1) * 14, :], start=True, stop=True).then_inc(made, 1)

                @block.scalar
                def _(act):
                    for k in range(2 * NC):
                        act.wait_ge(made, k + 1)
                        act.activation(gate[:, k // NC, (k % NC) * CH:(k % NC + 1) * CH], pg[:, k, 0:CH],
                                       ACT.Silu).then_inc(opened, 1)

                @block.vector
                def _(ve):
                    for k in range(2 * NC):
                        h, c = k // NC, k % NC
                        ve.wait_ge(opened, k + 1)
                        ve.tensor_tensor(gT[:, h, :].rearrange("p (b t) -> p t b", t=L)[:, c * 14:(c + 1) * 14, :],
                                         yT[:, h, c * 14:(c + 1) * 14, :],
                                         gate[:, h, c * CH:(c + 1) * CH].rearrange("p (t b) -> p t b", b=B), ALU.mult)

            def project(pe, n, out):
                for h in range(2):
                    last = pe.matmul(out, gT[:, h, n * T2:(n + 1) * T2], wout[:, h, :], start=(h == 0), stop=(h == 1))
                return last

            stage_norm(core, "l0p", project=project, outT=by_batch(core.xT))


HB, DH = 2, 64
QR = HB * L
QP = HB * DH
VW = DH + 1
HINV = 1.0 / D


def stage_attention(core):
    nc, d = core.nc, core.dram
    with scope(core, "b") as (sb, psum):
        mk = sb("mk", [D, D])
        mv_ext = sb("mv_ext", [D, HB, VW])
        qw = sb("qw", [D, B, QR])
        qblk = sb("qblk", [P, B, HB, L])
        klT = sb("klT", [P, T])
        vl = sb("vl", [L, B, HB, VW])
        aT = sb("aT", [HB * DH, T])
        wout = sb("wout", [HB * DH, D])
        bout = sb("bout", [T2, D])
        negmask = sb("negmask", [B, S2], BF16)
        onehot = sb("onehot", [B, B, QR], BF16)
        xc = sb("xc", [KP, NX, KT, D])
        loads = [core.sem(f"b_load{x}") for x in range(NX)]
        stage_latents(core, mk, mv_ext, qw, qblk, klT, vl, wout, bout, negmask, onehot, xc, loads)
        with scope(core, "bm") as (sb2, _):
            att = sb2("att", [P, B, DH])
            with scope(core, "bl") as (sb3, psum3):
                stage_context(core, sb3, psum3, mk, mv_ext, qw, qblk, klT, vl, att, negmask, onehot, xc, loads)
            heads_to_features(core, "bh", att, aT, None, bout)

        def project(pe, n, out):
            return pe.matmul(out, aT[:, n * T2:(n + 1) * T2], wout[:, :], start=True, stop=True)

        stage_norm(core, "bn", project=project, outT=by_batch(core.xT))


def context_in(core):
    return core.dram["ctx_1024"].rearrange("b (p k) f -> b p k f", k=KT)


def stage_latents(core, mk, mv_ext, qw, qblk, klT, vl, wout, bout, negmask, onehot, xc, ctx_loads):
    nc, d = core.nc, core.dram
    with scope(core, "bq") as (sb, psum):
        w = sb("w", [D, 3, D])
        lng = sb("lng", [D, 4])
        gam = sb("gam", [L, 2, DH])
        lT = sb("lT", [D, T])
        mask8 = sb("mask8", [B, S2], U8)
        loads, done = core.sem("bq_loads"), core.sem("bq_done")
        with nc.Block() as block:
            @block.sync
            def _(sp):
                sp.dma_start(w[:, 0, :], d["L0_xattn_W_q"]).then_inc(loads, 16)
                sp.dma_start(w[:, 1:3, :], d["L0_xattn_W_kv"].rearrange("i (k o) -> i k o", k=2)).then_inc(loads, 16)
                sp.dma_start(lng[:, :], d["L0_xattn_ln"]).then_inc(loads, 16)
                sp.dma_start(gam[:, 0, :], d["L0_xattn_q_gamma"].partition_broadcast(L)).then_inc(loads, 16)
                sp.dma_start(gam[:, 1, :], d["L0_xattn_k_gamma"].partition_broadcast(L)).then_inc(loads, 16)
                sp.dma_start(wout[:, :], d["L0_xattn_W_out"]).then_inc(loads, 16)
                sp.dma_start(bout[:, :], d["L0_xattn_b_out"].partition_broadcast(T2)).then_inc(loads, 16)
                sp.dma_start(mask8[:, :], d["mask_BxS2_bk0"]).then_inc(loads, 16)
                sp.wait_ge(loads, 8 * 16)

            @block.vector
            def _(ve):
                ve.memset(qblk[:, :, :, :], 0.0)
                ve.memset(vl[:, :, :, DH:VW], 1.0)
                ve.memset(mv_ext[:, :, DH:VW], HINV)
                ve.tensor_copy(onehot[:, :, :], over(core.ident[0:B, 0:B].unsqueeze(2), [B, B, QR]))
                ve.wait_ge(loads, 8 * 16)
                ve.tensor_scalar(negmask[:, :], mask8[:, :], 1.0, -NEG, ALU.subtract, ALU.mult)

        stage_norm(core, "bln", residual=False, gain=lng[:, 2:3], shift=lng[:, 3:4], outT=by_batch(lT))

        with scope(core, "bw") as (sb2, psum2):
            gw = sb2("gw", [D, 2, D])
            bias = sb2("bias", [D, D])
            negmean = sb2("negmean", [D, D])
            mkT = sb2("mkT", [P, HB, D])
            qk = sb2("qk", [L, B, 4, DH])
            sq = sb2("sq", [L, B, 4, DH])
            ss = sb2("ss", [L, B, 4])
            inv = sb2("inv", [L, B, 4])
            qT = sb2("qT", [P, T])
            ps = psum2("ps", [P, 8, 512])
            g = {s: core.sem(f"bw_{s}") for s in ("fold", "mean", "m", "qkv", "taken", "sq", "sq_last", "ss", "root", "inv", "unit",
                                                  "turned", "copied", "wide", "kept", "mkt", "mktc")}
            with nc.Block() as block:
                @block.sync
                def _(sp):
                    for n in range(NX):
                        sp.dma_start(xc[:, n, :, :], context_in(core)[n]).then_inc(ctx_loads[n], 16)

                @block.tensor
                def _(pe):
                    pe.wait_ge(g["fold"], 3)
                    out = ps[:, 0, 0:2 * D]
                    pe.matmul(out, negmean[:, :], gw[:, :, :], start=True, stop=False)
                    pe.matmul(out, bias[:, :], w[:, 1:3, :], start=False, stop=True).then_inc(g["mean"], 1)
                    for c in range(NC + 2):
                        if c < NC:
                            for b in range(c * BC, (c + 1) * BC):
                                if b >= 4:
                                    pe.wait_ge(g["taken"], 2 * (b - 3))
                                pe.matmul(ps[0:L, 1 + b % 4, 0:3 * D], lT[:, b * L:(b + 1) * L], w[:, :, :],
                                          start=True, stop=True).then_inc(g["qkv"], 1)
                        if c == 0:
                            pe.wait_ge(g["m"], 2)
                            pe.transpose(ps[:, 5, 0:D], mk[:, :], core.ident[:, :]).then_inc(g["mkt"], 1)
                        if c >= 2:
                            done = c - 2
                            pe.wait_ge(g["unit"], 2 * done + 3)
                            for which in range(2):
                                if done:
                                    pe.wait_ge(g["copied"], 2 * done - 1 + which)
                                for r in range(BC):
                                    last = pe.transpose(ps[:, 6 + which, r * L:(r + 1) * L],
                                                        qk[:, done * BC + r, 2 * which:2 * which + 2, :].rearrange("p h d -> p (h d)"),
                                                        core.ident[0:L, 0:L])
                                last.then_inc(g["turned"], 1)
                    pe.wait_ge(g["taken"], 2 * B)
                    pe.wait_ge(g["mktc"], HB + 1)
                    for n in range(HB * NC):
                        c, h = n // HB, n % HB
                        pe.wait_ge(g["copied"], 2 * c + 1)
                        if n >= 4:
                            pe.wait_ge(g["kept"], n - 3)
                        pe.matmul(ps[:, 1 + n % 4, 0:CH], mkT[:, h, :], qT[:, c * CH:(c + 1) * CH],
                                  start=True, stop=True).then_inc(g["wide"], 1)

                @block.gpsimd
                def _(pool):
                    pool.memset(mkT[:, :, :], 0.0).then_inc(g["mktc"], 1)
                    for c in range(NC - 1):
                        of = slice(c * BC, (c + 1) * BC)
                        pool.wait_ge(g["taken"], 2 * (c + 1) * BC)
                        pool.tensor_tensor(sq[:, of, :, :], qk[:, of, :, :], qk[:, of, :, :], ALU.mult).then_inc(g["sq"], 1)

                @block.scalar
                def _(act):
                    def root(c):
                        of = slice(c * BC, (c + 1) * BC)
                        act.wait_ge(g["ss"], c + 1)
                        act.activation(inv[:, of, :], ss[:, of, :], ACT.Sqrt, scale=1.0 / DH).then_inc(g["root"], 1)

                    for b in range(B):
                        act.wait_ge(g["qkv"], b + 1)
                        act.activation(qk[:, b, :, :], ps[0:L, 1 + b % 4, 0:2 * D].rearrange("p (k d) -> p k d", d=DH),
                                       ACT.Copy).then_inc(g["taken"], 1)
                        act.activation(vl[:, b, :, 0:DH], ps[0:L, 1 + b % 4, 2 * D:3 * D].rearrange("p (h d) -> p h d", d=DH),
                                       ACT.Copy).then_inc(g["taken"], 1)
                        if b == BC - 1:
                            act.wait_ge(g["mkt"], 1)
                            act.wait_ge(g["mktc"], 1)
                            for h in range(HB):
                                rows = slice(h * DH, (h + 1) * DH)
                                act.activation(mkT[rows, h, :], ps[rows, 5, 0:D], ACT.Copy).then_inc(g["mktc"], 1)
                        if b % BC == BC - 1 and b >= BC:
                            if b == B - 1:
                                act.wait_ge(g["taken"], 2 * B)
                                act.activation(sq[:, B - BC:B, :, :], qk[:, B - BC:B, :, :], ACT.Square).then_inc(g["sq_last"], 1)
                            root(b // BC - 1)
                    root(NC - 1)
                    for n in range(HB * NC):
                        c, h = n // HB, n % HB
                        act.wait_ge(g["wide"], n + 1)
                        act.activation(qw[:, c * BC:(c + 1) * BC, h * L:(h + 1) * L],
                                       ps[:, 1 + n % 4, 0:CH].rearrange("p (b t) -> p b t", t=L), ACT.Copy).then_inc(g["kept"], 1)

                @block.vector
                def _(ve):
                    ve.memset(negmean[:, :], -HINV).then_inc(g["fold"], 1)
                    ve.tensor_scalar(gw[:, :, :], w[:, 1:3, :], lng[:, 0:1], None, ALU.mult).then_inc(g["fold"], 1)
                    ve.tensor_scalar(bias[:, :], core.ones[:, :], lng[:, 1:2], HINV, ALU.mult, ALU.mult).then_inc(g["fold"], 1)
                    ve.wait_ge(g["mean"], 1)
                    ve.wait_ge(g["fold"], 3)
                    ve.tensor_tensor(mk[:, :], gw[:, 0, :], ps[:, 0, 0:D], ALU.add).then_inc(g["m"], 1)
                    ve.tensor_tensor(mv_ext[:, :, 0:DH], gw[:, 1, :].rearrange("p (h d) -> p h d", h=HB),
                                     ps[:, 0, D:2 * D].rearrange("p (h d) -> p h d", h=HB), ALU.add).then_inc(g["m"], 1)
                    ve.scalar_tensor_tensor(gam[:, 0, :], gam[:, 0, :], float(DH) ** -0.5, gam[:, 1, :],
                                            ALU.mult, ALU.mult).then_inc(g["unit"], 1)

                    def sums(c):
                        of = slice(c * BC, (c + 1) * BC)
                        if c < NC - 1:
                            ve.wait_ge(g["sq"], c + 1)
                        else:
                            ve.wait_ge(g["sq_last"], 1)
                        ve.tensor_reduce(ss[:, of, :], sq[:, of, :, :], AX, ALU.add).then_inc(g["ss"], 1)

                    def unit(c):
                        of = slice(c * BC, (c + 1) * BC)
                        ve.wait_ge(g["root"], c + 1)
                        ve.tensor_scalar(inv[:, of, :], inv[:, of, :], 1e-8, None, ALU.max).then_inc(g["inv"], 1)
                        ve.wait_ge(g["inv"], 2 * c + 1)
                        ve.reciprocal(inv[:, of, :], inv[:, of, :]).then_inc(g["inv"], 1)
                        ve.wait_ge(g["inv"], 2 * c + 2)
                        ve.tensor_tensor(qk[:, of, :, :], qk[:, of, :, :], over(inv[:, of, :].unsqueeze(3), [L, BC, 4, DH]),
                                         ALU.mult).then_inc(g["unit"], 1)
                        ve.wait_ge(g["unit"], 2 * c + 2)
                        ve.tensor_tensor(qk[:, of, 0:2, :], qk[:, of, 0:2, :],
                                         over(gam[:, 0, :].unsqueeze(1).unsqueeze(1), [L, BC, 2, DH]), ALU.mult).then_inc(g["unit"], 1)

                    def keep(c):
                        ve.wait_ge(g["turned"], 2 * c + 1)
                        src = ps[:, 6, 0:CH]
                        ve.tensor_copy(qT[:, c * CH:(c + 1) * CH], src)
                        for h in range(HB):
                            rows = slice(h * DH, (h + 1) * DH)
                            last = ve.tensor_copy(qblk[rows, c * BC:(c + 1) * BC, h, :],
                                                  src[rows, :].rearrange("p (b t) -> p b t", t=L))
                        last.then_inc(g["copied"], 1)
                        ve.wait_ge(g["turned"], 2 * c + 2)
                        ve.tensor_copy(klT[:, c * CH:(c + 1) * CH], ps[:, 7, 0:CH]).then_inc(g["copied"], 1)

                    sums(0)
                    for c in range(NC + 2):
                        if c + 1 < NC:
                            sums(c + 1)
                        if c < NC:
                            unit(c)
                        if c >= 2:
                            keep(c - 2)


def stage_context(core, sb, psum, mk, mv_ext, qw, qblk, klT, vl, att, negmask, onehot, xc, ctx_loads):
    nc = core.nc
    ctx_dram = context_in(core)
    SUB = 3
    KS = KT // SUB
    KA = 2
    stats = sb("stats", [KP, 2, KT, 6])
    moments = sb("moments", [KP, 2, KT, 2])
    rstd = sb("rstd", [KP, 2, KT])
    shift = sb("shift", [KP, 2, KT])
    xcT = sb("xcT", [D, 2, KT * KP])
    sq = sb("sq", [KP, 2, KS, HB, DH])
    ss = sb("ss", [KP, 2, KT, HB])
    inv = sb("inv", [KP, 2, KT, HB])
    sc = sb("sc", [P, 2, KT + 1, QR])
    top = sb("top", [P, 2, QR])
    topall = sb("topall", [P, 2, QR])
    plat = sb("plat", [L, QP])
    mixT = sb("mixT", [D, QP])
    rden = sb("rden", [P, HB])
    kl = sb("kl", [P, 2, L])
    pX = psum("pX", [P, 2, 512])
    pK = psum("pK", [P, 2, 512])
    pS = psum("pS", [P, SUB, 512])
    pO = psum("pO", [P, 512])
    lats_at, mix_at, val_at = slice(0, QR), slice(128, 128 + QR), slice(256, 256 + HB * VW)
    names = ("kl const stats moments lnv rstd shift xc xc_act turned xcT keys sq ss floor lninv inv raw lat scaled lats "
             "top topall subbed probs plat mix mixT val rden att").split()
    s = {n: core.sem(f"bl_{n}") for n in names}

    STEPS = B + 2
    PEEL, UN = 4, 4

    def run(eng, step, steps=STEPS):
        for n in range(PEEL):
            step(n, n)
        with eng.Fori(0, (B - PEEL) // UN) as i:
            for j in range(UN):
                step(i * UN + (PEEL + j), PEEL + j)
        for n in range(B, steps):
            step(n, n)

    def a_part(k):
        return k < B

    def b_part(k):
        return 1 <= k < B + 1

    def c_part(k):
        return 2 <= k < B + 2

    def d_part(k):
        return 3 <= k

    with nc.Block() as block:
        @block.sync
        def _(sp):
            def load(n, k):
                sp.wait_ge(s["mix"], n - NX + 1)
                sp.dma_start(xc[:, k % NX, :, :], ctx_dram[bass.ds(n, 1)].rearrange("a p k f -> p (a k) f")
                             if not isinstance(n, int) else ctx_dram[n]).then_inc(ctx_loads[k % NX], 16)
            with sp.Fori(0, (B - NX) // NX) as i:
                for j in range(NX):
                    load(i * NX + (NX + j), j)

        @block.gpsimd
        def _(pool):
            fills = ((sc[:, 0, KT, :], NEG), (top[96:P, 0, :], NEG), (sc[:, 1, KT, :], NEG),
                     (top[96:P, 1, :], NEG), (plat[:, :], 0.0), (mixT[:, :], 0.0), (att[:, :, :], 0.0))
            for m, (tile, value) in enumerate(fills):
                if m:
                    pool.wait_ge(s["const"], m)
                pool.memset(tile, value).then_inc(s["const"], 1)
            pool.wait_ge(s["const"], len(fills))

            def step(n, k):
                if c_part(k):
                    buf = k % 2
                    pool.wait_ge(s["topall"], n - 1)
                    pool.tensor_tensor(sc[0:KP, buf, :, :], sc[0:KP, buf, :, :],
                                       over(topall[0:KP, buf, :].unsqueeze(1), [KP, KT + 1, QR]),
                                       ALU.subtract).then_inc(s["subbed"], 1)
                if a_part(k):
                    wait_apart(pool, s["shift"], 2 * n + 2, core.apart)
                    for t in range(KT - KA):
                        last = pool.tensor_scalar(xc[:, k % NX, t, :], xc[:, k % NX, t, :],
                                                  rstd[:, k % 2, t:t + 1], shift[:, k % 2, t:t + 1], ALU.mult, ALU.add)
                    last.then_inc(s["xc"], 1)
                if b_part(k):
                    buf = (k - 1) % 2
                    if k > 2:
                        pool.wait_ge(s["subbed"], n - 2)
                    wait_apart(pool, s["top"], n, core.apart)
                    pool.partition_all_reduce(topall[:, buf, :], top[:, buf, :], P, RMAX).then_inc(s["topall"], 1)
            run(pool, step)

        @block.vector
        def _(ve):
            def shifts(n, buf):
                ve.wait_ge(s["rstd"], n + 1)
                ve.tensor_tensor(shift[:, buf, :], moments[:, buf, :, 0], rstd[:, buf, :], ALU.mult).then_inc(s["shift"], 1)
                ve.wait_ge(s["shift"], 2 * n + 1)
                ve.tensor_scalar(shift[:, buf, :], shift[:, buf, :], -1.0, 1.0, ALU.mult, ALU.add).then_inc(s["shift"], 1)

            def step(n, k):
                if a_part(k):
                    buf = k % 2
                    ve.wait_ge(ctx_loads[k % NX], (n - k % NX) * (16 // NX) + 16)
                    for t in range(KT):
                        last = ve.bn_stats(stats[:, buf, t, :], xc[:, k % NX, t, :])
                    last.then_inc(s["stats"], 1)
                if d_part(k):
                    ve.wait_ge(s["val"], n - 2)
                    val = pO[:, val_at].rearrange("p (h v) -> p h v", v=VW)
                    ve.reciprocal(rden[:, :], val[:, :, DH]).then_inc(s["rden"], 1)
                if a_part(k):
                    wait_apart(ve, s["stats"], n + 1, core.apart)
                    for t in range(KT):
                        last = ve.bn_aggr(moments[:, buf, t, :], stats[:, buf, t, :])
                    last.then_inc(s["moments"], 1)
                if d_part(k):
                    ve.wait_ge(s["rden"], n - 2)
                    for h in range(HB):
                        rows = slice(h * DH, h * DH + L)
                        last = ve.tensor_scalar(att[rows, bass.ds(n - 3, 1), :].rearrange("p a d -> p (a d)"),
                                                val[rows, h, 0:DH], rden[rows, h:h + 1], None, ALU.mult)
                    last.then_inc(s["att"], 1)
                if b_part(k):
                    buf = (k - 1) % 2
                    for u in range(SUB):
                        if u == 1 and a_part(k):
                            shifts(n, k % 2)
                        ve.wait_ge(s["sq"], n * SUB - SUB + u + 1)
                        ve.tensor_reduce(ss[:, buf, u * KS:(u + 1) * KS, :], sq[:, (k - 1 + u) % 2, :, :, :], AX,
                                         ALU.add).then_inc(s["ss"], 1)
                elif a_part(k):
                    shifts(n, k % 2)
                if b_part(k):
                    buf = (k - 1) % 2
                    if k == 1:
                        ve.wait_ge(s["const"], 7)
                    ve.wait_ge(s["ss"], SUB * n)
                    ve.tensor_scalar(ss[:, buf, :, :], ss[:, buf, :, :], 1e-16 * DH, None, ALU.max).then_inc(s["floor"], 1)
                    if k > 2:
                        ve.wait_ge(s["mix"], n - 2)
                    ve.wait_ge(s["lat"], n)
                    ve.tensor_copy(sc[0:L, buf, KT, :], pO[0:L, lats_at]).then_inc(s["lats"], 1)
                    ve.wait_ge(s["inv"], n)
                    for u in range(SUB):
                        tiles = slice(u * KS, (u + 1) * KS)
                        ve.wait_ge(s["raw"], n * SUB - SUB + u + 1)
                        ve.tensor_tensor(sc[0:KP, buf, tiles, :].rearrange("p k (h q) -> p k h q", h=HB),
                                         pS[0:KP, u, 0:KS * QR].rearrange("p (k h q) -> p k h q", k=KS, h=HB),
                                         over(inv[:, buf, tiles, :].unsqueeze(3), [KP, KS, HB, L]),
                                         ALU.mult).then_inc(s["scaled"], 1)
                    ve.wait_ge(s["scaled"], SUB * n)
                    ve.wait_ge(s["lats"], n)
                    if k > 2:
                        ve.wait_ge(s["topall"], n - 2)
                    ve.tensor_reduce(top[0:KP, buf, :], sc[0:KP, buf, :, :].rearrange("p k q -> p q k"), AX,
                                     ALU.max).then_inc(s["top"], 1)
            run(ve, step, STEPS + 1)

        @block.scalar
        def _(act):
            load_tables(nc, act, LN_EXP_TABLES)

            def roots(n, buf):
                act.wait_ge(s["moments"], n + 1)
                act.activation(rstd[:, buf, :], moments[:, buf, :, 1], ACT.Ln, bias=core.eps_ln[0:KP, :]).then_inc(s["lnv"], 1)
                act.wait_ge(s["lnv"], n + 1)
                act.activation(rstd[:, buf, :], rstd[:, buf, :], ACT.Exp, scale=-0.5).then_inc(s["rstd"], 1)

            def step(n, k):
                if a_part(k) and k == 0:
                    act.wait_ge(s["const"], 7)
                if b_part(k):
                    buf = (k - 1) % 2
                    act.activation(kl[:, buf, :], klT[:, bass.ds((n - 1) * L, L)], ACT.Copy).then_inc(s["kl"], 1)
                    for u in range(SUB + 1):
                        if u < SUB:
                            act.wait_ge(s["turned"], n * SUB - SUB + u + 1)
                            act.activation(xcT[:, buf, u * KS * KP:(u + 1) * KS * KP], pX[:, (k - 1 + u) % 2, 0:KS * KP],
                                           ACT.Copy).then_inc(s["xcT"], 1)
                        if u:
                            act.wait_ge(s["keys"], n * SUB - SUB + u)
                            if k > 1 or u > 2:
                                act.wait_ge(s["ss"], n * SUB - SUB + u - 2)
                            act.activation(sq[:, (k - 2 + u) % 2, :, :, :],
                                           pK[0:KP, (k - 2 + u) % 2, :].rearrange("p (k h d) -> p k h d", k=KS, h=HB),
                                           ACT.Square).then_inc(s["sq"], 1)
                        if u == 2 and a_part(k):
                            roots(n, k % 2)
                elif a_part(k):
                    roots(n, k % 2)
                if a_part(k):
                    wait_apart(act, s["shift"], 2 * n + 2, core.apart)
                    for t in range(KT - KA, KT):
                        last = act.activation(xc[:, k % NX, t, :], xc[:, k % NX, t, :], ACT.Identity,
                                              bias=shift[:, k % 2, t:t + 1], scale=rstd[:, k % 2, t:t + 1])
                    last.then_inc(s["xc_act"], 1)
                if c_part(k):
                    act.wait_ge(s["subbed"], n - 1)
                    act.activation(sc[0:KP, k % 2, 0:KT, :], sc[0:KP, k % 2, 0:KT, :], ACT.Exp).then_inc(s["probs"], 1)
                if b_part(k):
                    act.wait_ge(s["floor"], n)
                    act.activation(inv[:, buf, :, :], ss[:, buf, :, :], ACT.Ln, scale=1.0 / DH).then_inc(s["lninv"], 1)
                    act.wait_ge(s["lninv"], n)
                    act.activation(inv[:, buf, :, :], inv[:, buf, :, :], ACT.Exp, scale=-0.5).then_inc(s["inv"], 1)
                if c_part(k):
                    if k > 2:
                        act.wait_ge(s["val"], n - 2)
                    act.activation(plat[:, :].rearrange("p (h q) -> p h q", h=HB)[:, :, 0:L],
                                   sc[0:L, k % 2, KT, :].rearrange("p (h q) -> p h q", h=HB), ACT.Exp).then_inc(s["probs"], 1)
                    act.wait_ge(s["mix"], n - 1)
                    act.activation(mixT[:, :].rearrange("p (h q) -> p h q", h=HB)[:, :, 0:L],
                                   pO[:, mix_at].rearrange("p (h q) -> p h q", h=HB), ACT.Copy).then_inc(s["mixT"], 1)
            run(act, step)

        @block.tensor
        def _(pe):
            pe.wait_ge(s["const"], 7)

            def values(n, k):
                pe.wait_ge(s["mixT"], n - 2)
                pe.matmul(pO[:, val_at], mixT[:, :], mv_ext[:, :, :], start=True, stop=False)
                pe.matmul(pO[:, val_at], plat[:, :], vl[:, bass.ds(n - 3, 1), :, :], start=False,
                          stop=True).then_inc(s["val"], 1)

            def step(n, k):
                if b_part(k):
                    buf, x = (k - 1) % 2, (k - 1) % NX
                    bq = n - 1
                    pe.wait_ge(s["xc"], n)
                    pe.wait_ge(s["xc_act"], n)
                    def turn(u):
                        if k > 1 or u > 1:
                            pe.wait_ge(s["xcT"], n * SUB - SUB + u - 1)
                        for r in range(KS):
                            last = pe.transpose(pX[:, (k - 1 + u) % 2, r * KP:(r + 1) * KP], xc[:, x, u * KS + r, :],
                                                core.ident[0:KP, 0:KP])
                        last.then_inc(s["turned"], 1)

                    def keys(u):
                        pe.wait_ge(s["xcT"], n * SUB - SUB + u + 1)
                        if k > 1 or u > 1:
                            pe.wait_ge(s["sq"], n * SUB - SUB + u - 1)
                        for r in range(KS):
                            at = slice((u * KS + r) * KP, (u * KS + r + 1) * KP)
                            last = pe.matmul(pK[0:KP, (k - 1 + u) % 2, r * D:(r + 1) * D], xcT[:, buf, at], mk[:, :],
                                             start=True, stop=True)
                        last.then_inc(s["keys"], 1)

                    turn(0)
                    turn(1)
                    if d_part(k):
                        values(n, k)
                    keys(0)
                    turn(2)
                    keys(1)
                    keys(2)
                    if d_part(k):
                        pe.wait_ge(s["att"], n - 2)
                    elif k == 2:
                        pe.wait_ge(s["lats"], n - 1)
                    pe.wait_ge(s["kl"], n)
                    pe.matmul(pO[0:L, lats_at], kl[:, buf, :],
                              qblk[:, bass.ds(bq, 1), :, :], start=True, stop=True).then_inc(s["lat"], 1)
                    for u in range(SUB):
                        if k > 1:
                            pe.wait_ge(s["scaled"], n * SUB - 2 * SUB + u + 1)
                        for r in range(KS):
                            t = u * KS + r
                            out = pS[0:KP, u, r * QR:(r + 1) * QR]
                            pe.matmul(out, xcT[:, buf, t * KP:(t + 1) * KP], qw[:, bass.ds(bq, 1), :],
                                      start=True, stop=False)
                            last = pe.matmul(out, negmask[:, t:S2:KT], onehot[:, bass.ds(bq, 1), :], start=False, stop=True)
                        last.then_inc(s["raw"], 1)
                elif d_part(k):
                    values(n, k)
                if c_part(k):
                    buf, x = k % 2, (k - 2) % NX
                    pe.wait_ge(s["probs"], 2 * n - 2)
                    if b_part(k):
                        pe.wait_ge(s["lats"], n)
                    else:
                        pe.wait_ge(s["att"], n - 2)
                    for t in range(KT):
                        last = pe.matmul(pO[:, mix_at], xc[:, x, t, :], sc[0:KP, buf, t, :],
                                         start=(t == 0), stop=(t == KT - 1))
                    last.then_inc(s["mix"], 1)
            run(pe, step, STEPS + 1)


def rank_below(ve, s, values, earlier, lots, rank, n, limit, out):
    shape = [T2, NT, n, n]
    other, own = over(values.unsqueeze(2), shape), over(values.unsqueeze(3), shape)
    ve.tensor_tensor(lots[0], other, own, ALU.is_gt).then_inc(s.sem, 1)
    ve.tensor_tensor(lots[1], other, own, ALU.is_equal).then_inc(s.sem, 1)
    ve.wait_ge(s.sem, s(2))
    ve.tensor_tensor(lots[1], lots[1], over(earlier.unsqueeze(1), shape), ALU.mult).then_inc(s.sem, 1)
    ve.wait_ge(s.sem, s(3))
    ve.tensor_tensor(lots[0], lots[0], lots[1], ALU.add).then_inc(s.sem, 1)
    ve.wait_ge(s.sem, s(4))
    ve.tensor_reduce(rank, lots[0], AX, ALU.add).then_inc(s.sem, 1)
    ve.wait_ge(s.sem, s(5))
    ve.tensor_scalar(out, rank, limit - 0.5, None, ALU.is_lt).then_inc(s.sem, 1)
    ve.wait_ge(s.sem, s(6))
    s.base += 6


def stage_router(core, name, weights_T, bias, groups, parts, beside):
    nc = core.nc
    with scope(core, name) as (sb, psum):
        wr = sb("wr", [D, E])
        bias_row = sb("bias_row", [T2, E])
        prob = sb("prob", [T2, NT, E])
        choice = sb("choice", [T2, NT, E])
        pairs = sb("pairs", [T2, NT, E // 2])
        best = sb("best", [T2, NT, E // 2])
        lot0, lot1 = sb("lot0", [T2, NT, E, E]), sb("lot1", [T2, NT, E, E])
        earlier = sb("earlier", [T2, E, E])
        rank = sb("rank", [T2, NT, E])
        used = sb("used", [T2, NT, E])
        total = sb("total", [T2, NT])
        low = sb("low", [T2, NT, E], BF16)
        split = sb("split", [T2, NT, 96])
        ps = psum("ps", [P, 5, 512])
        loads, built, logits, probs, cut, turned = (core.sem(f"{name}_{x}") for x in ("loads", "built", "logits", "probs", "cut", "turned"))
        chain = core.shared("router_chain")
        with nc.Block() as block:
            @block.sync
            def _(sp):
                sp.dma_start(wr[:, :], weights_T).then_inc(loads, 16)
                if bias is not None:
                    sp.dma_start(bias_row[:, :], bias.partition_broadcast(T2)).then_inc(loads, 16)
                beside["sync"](sp)

            @block.gpsimd
            def _(pool):
                pool.memset(earlier[:, :, :], 1.0).then_inc(built, 1)
                pool.wait_ge(built, 1)
                pool.affine_select(out=earlier[:, :, :], in_=earlier[:, :, :], compare_op=ALU.is_ge, fill=0.0,
                                   base=-1, pattern=[[1, E], [-1, E]], channel_multiplier=0).then_inc(built, 1)
                pool.wait_ge(built, 2)
                pool.memset(split[:, :, :], 0.0).then_inc(built, 1)
                beside["gpsimd"](pool)

            @block.tensor
            def _(pe):
                pe.wait_ge(loads, 16 if bias is None else 32)
                for n in range(NT):
                    last = pe.matmul(ps[0:T2, 4, n * E:(n + 1) * E], core.xT[:, n * T2:(n + 1) * T2], wr[:, :],
                                     start=True, stop=True)
                last.then_inc(logits, 1)
                beside["tensor"](pe)
                pe.wait_ge(cut, 1)
                for c in range(NC):
                    for r in range(TPC):
                        last = pe.transpose(ps[0:96, c, r * T2:(r + 1) * T2], split[:, c * TPC + r, :],
                                            core.ident[0:T2, 0:T2])
                    last.then_inc(turned, 1)

            @block.scalar
            def _(act):
                act.wait_ge(logits, 1)
                act.activation(prob[:, :, :], ps[0:T2, 4, 0:NT * E].rearrange("p (n e) -> p n e", e=E),
                               ACT.Sigmoid).then_inc(probs, 1)
                beside["scalar"](act)
                for c in range(NC):
                    act.wait_ge(turned, c + 1)
                    act.activation(parts[:, c * CH:(c + 1) * CH], ps[0:96, c, 0:CH], ACT.Copy)

            @block.vector
            def _(ve):
                ve.wait_ge(probs, 1)
                ve.wait_ge(built, 3)
                ranked = prob[:, :, :]
                if bias is not None:
                    ranked = choice[:, :, :]
                    ve.tensor_tensor(ranked, prob[:, :, :], over(bias_row[:, :].unsqueeze(1), [T2, NT, E]),
                                     ALU.add).then_inc(chain.sem, 1)
                    ve.wait_ge(chain.sem, chain(1))
                    two = ranked.rearrange("p n (g k) -> p n g k", k=2)
                    ve.tensor_tensor(pairs[:, :, :], two[:, :, :, 0], two[:, :, :, 1], ALU.add).then_inc(chain.sem, 1)
                    ve.wait_ge(chain.sem, chain(2))
                    chain.base += 2
                    h = E // 2
                    rank_below(ve, chain, pairs[:, :, :], earlier[:, 0:h, 0:h],
                               [x[:, :, 0:h, 0:h] for x in (lot0, lot1)], rank[:, :, 0:h], h, 2, best[:, :, :])
                    ve.tensor_tensor(ranked.rearrange("p n (g k) -> p n g k", k=2), two,
                                     over(best[:, :, :].unsqueeze(3), [T2, NT, h, 2]), ALU.mult).then_inc(chain.sem, 1)
                    ve.wait_ge(chain.sem, chain(1))
                    ve.tensor_scalar(ranked, ranked, 0.0, None, ALU.add).then_inc(chain.sem, 1)
                    ve.wait_ge(chain.sem, chain(2))
                    chain.base += 2
                rank_below(ve, chain, ranked, earlier[:, :, :], [lot0[:, :, :, :], lot1[:, :, :, :]], rank[:, :, :],
                           E, 2, used[:, :, :])
                ve.tensor_tensor(used[:, :, :], used[:, :, :], prob[:, :, :], ALU.mult).then_inc(chain.sem, 1)
                ve.wait_ge(chain.sem, chain(1))
                ve.tensor_reduce(total[:, :], used[:, :, :], AX, ALU.add).then_inc(chain.sem, 1)
                ve.wait_ge(chain.sem, chain(2))
                ve.tensor_scalar(total[:, :], total[:, :], 1e-20, None, ALU.add).then_inc(chain.sem, 1)
                ve.wait_ge(chain.sem, chain(3))
                ve.reciprocal(total[:, :], total[:, :]).then_inc(chain.sem, 1)
                ve.wait_ge(chain.sem, chain(4))
                ve.tensor_tensor(used[:, :, :], used[:, :, :], over(total[:, :].unsqueeze(2), [T2, NT, E]),
                                 ALU.mult).then_inc(chain.sem, 1)
                ve.wait_ge(chain.sem, chain(5))
                chain.base += 5
                split_exactly(ve, chain, used[:, :, :], low[:, :, :], [split[:, :, 32 * p:32 * p + E] for p in range(3)])
                ve.tensor_scalar(total[:, :], total[:, :], 1.0, None, ALU.mult).then_inc(cut, 1)


def split_exactly(ve, s, value, low, parts):
    for p, part in enumerate(parts):
        ve.tensor_copy(low, value).then_inc(s.sem, 1)
        ve.wait_ge(s.sem, s(1))
        ve.tensor_copy(part, low).then_inc(s.sem, 1)
        if p < 2:
            ve.tensor_tensor(value, value, low, ALU.subtract).then_inc(s.sem, 1)
        ve.wait_ge(s.sem, s(3 if p < 2 else 2))
        s.base += 3 if p < 2 else 2


def stage_experts0(core):
    nc, d = core.nc, core.dram
    with scope(core, "f0") as (sb, psum):
        parts = sb("parts", [96, T], BF16)
        w1 = sb("w1", [D, E, P])
        w2 = sb("w2", [P, E, D])
        hidden = sb("hidden", [P, E, T])
        ph = psum("ph", [P, 3, 512])
        loads, up, rects, wide, weighted = (core.sem(f"f0_{x}") for x in ("loads", "up", "rects", "wide", "weighted"))

        def unit(n):
            c, e = n // E, n % E
            return c, e, hidden[:, e, c * CH:(c + 1) * CH]

        def load(sp):
            sp.dma_start(w1[:, :, :], d["L0_ffn_w1"].rearrange("i (e w) -> i e w", e=E)).then_inc(loads, 16)
            sp.dma_start(w2[:, :, :], d["L0_ffn_w2"].rearrange("(e w) o -> w e o", e=E)).then_inc(loads, 16)

        def products(pe):
            pe.wait_ge(loads, 32)
            for n in range(NC * E):
                c, e, _ = unit(n)
                if n >= 3:
                    pe.wait_ge(rects, n - 2)
                pe.matmul(ph[:, n % 3, 0:CH], w1[:, e, :], core.xT[:, c * CH:(c + 1) * CH], start=True,
                          stop=True).then_inc(up, 1)

        def squares(act):
            for n in range(NC * E + 1):
                if n < NC * E:
                    act.wait_ge(up, n + 1)
                    act.activation(unit(n)[2], ph[:, n % 3, 0:CH], ACT.Relu).then_inc(rects, 1)
                if n and n % 2:
                    act.wait_ge(rects, n)
                    act.activation(unit(n - 1)[2], unit(n - 1)[2], ACT.Square)

        def odd_squares(pool):
            for n in range(1, NC * E, 2):
                pool.wait_ge(rects, n + 1)
                pool.tensor_tensor(unit(n)[2], unit(n)[2], unit(n)[2], ALU.mult)

        stage_router(core, "f0r", d["L0_ffn_router_wT"], None, False, parts,
                     {"sync": load, "tensor": products, "scalar": squares, "gpsimd": odd_squares})
        with scope(core, "f0p") as (_, psum2), nc.Block() as block:
            pw = psum2("pw", [P, 4, 512])

            @block.tensor
            def _(pe):
                for n in range(NC * E):
                    c, e, _ = unit(n)
                    if n >= 4:
                        pe.wait_ge(weighted, n - 3)
                    pe.matmul(pw[:, n % 4, 0:CH], core.selector[:, e, :], parts[:, c * CH:(c + 1) * CH], start=True,
                              stop=True).then_inc(wide, 1)

            @block.vector
            def _(ve):
                for n in range(NC * E):
                    ve.wait_ge(wide, n + 1)
                    ve.tensor_tensor(unit(n)[2], unit(n)[2], pw[:, n % 4, 0:CH], ALU.mult).then_inc(weighted, 1)

        def project(pe, n, out):
            for e in range(E):
                last = pe.matmul(out, hidden[:, e, n * T2:(n + 1) * T2], w2[:, e, :], start=(e == 0), stop=(e == E - 1))
            return last

        stage_norm(core, "f0n", project=project, outT=None)


def stage_experts1(core):
    nc, d = core.nc, core.dram
    PR = E // 2
    half = P // 2

    def both(r):
        return core.selector[:, :, :].rearrange("k r m -> k (r m)")[:, r * P + half:(r + 1) * P + half]

    with scope(core, "f1") as (sb, psum):
        parts = sb("parts", [96, T], BF16)
        wg = sb("wg", [D, PR, P])
        wu = sb("wu", [D, PR, P])
        wd = sb("wd", [P, PR, D])
        hidden = sb("hidden", [P, PR, T])
        gate = sb("gate", [P, 2, CH])
        pg = psum("pg", [P, 2, 512])
        pu = psum("pu", [P, 1, 512])
        loads, gates, ups, opened, taken, mixed, wide, weighted = (
            core.sem(f"f1_{x}") for x in ("loads", "gates", "ups", "opened", "taken", "mixed", "wide", "weighted"))

        def unit(n):
            c, e = n // PR, n % PR
            return c, e, hidden[:, e, c * CH:(c + 1) * CH]

        def load(sp):
            sp.dma_start(wg[:, :, :], d["L1_ffn_gate_projT"].rearrange("i (e w) -> i e w", e=PR)).then_inc(loads, 16)
            sp.dma_start(wu[:, :, :], d["L1_ffn_up_projT"].rearrange("i (e w) -> i e w", e=PR)).then_inc(loads, 16)
            sp.dma_start(wd[:, :, :], d["L1_ffn_down_projT"].rearrange("(e w) o -> w e o", e=PR)).then_inc(loads, 16)

        def products(pe):
            pe.wait_ge(loads, 48)
            for n in range(NC * PR):
                c, e, _ = unit(n)
                cols = slice(c * CH, (c + 1) * CH)
                if n >= 2:
                    pe.wait_ge(opened, n - 1)
                pe.matmul(pg[:, n % 2, 0:CH], wg[:, e, :], core.xT[:, cols], start=True, stop=True).then_inc(gates, 1)
                if n:
                    pe.wait_ge(taken, n)
                pe.matmul(pu[:, 0, 0:CH], wu[:, e, :], core.xT[:, cols], start=True, stop=True).then_inc(ups, 1)

        def openings(act):
            for n in range(NC * PR):
                act.wait_ge(gates, n + 1)
                if n >= 2:
                    act.wait_ge(mixed, n - 1)
                act.activation(gate[:, n % 2, :], pg[:, n % 2, 0:CH], ACT.Silu).then_inc(opened, 1)
                act.wait_ge(ups, n + 1)
                act.activation(unit(n)[2], pu[:, 0, 0:CH], ACT.Copy).then_inc(taken, 1)

        def mixes(pool):
            for n in range(NC * PR):
                pool.wait_ge(opened, n + 1)
                pool.wait_ge(taken, n + 1)
                pool.tensor_tensor(unit(n)[2], unit(n)[2], gate[:, n % 2, :], ALU.mult).then_inc(mixed, 1)

        stage_router(core, "f1r", d["L1_ffn_gate_weightT"], d["L1_ffn_e_score_correction_bias"], True, parts,
                     {"sync": load, "tensor": products, "scalar": openings, "gpsimd": mixes})
        with scope(core, "f1p") as (_, psum2), nc.Block() as block:
            pw = psum2("pw", [P, 4, 512])

            @block.tensor
            def _(pe):
                for n in range(NC * PR):
                    c, e, _ = unit(n)
                    if n >= 4:
                        pe.wait_ge(weighted, n - 3)
                    pe.matmul(pw[:, n % 4, 0:CH], both(2 * e), parts[:, c * CH:(c + 1) * CH], start=True,
                              stop=True).then_inc(wide, 1)

            @block.vector
            def _(ve):
                for n in range(NC * PR):
                    ve.wait_ge(wide, n + 1)
                    ve.tensor_tensor(unit(n)[2], unit(n)[2], pw[:, n % 4, 0:CH], ALU.mult).then_inc(weighted, 1)

        def project(pe, n, out):
            for e in range(PR):
                last = pe.matmul(out, hidden[:, e, n * T2:(n + 1) * T2], wd[:, e, :], start=(e == 0), stop=(e == PR - 1))
            return last

        stage_norm(core, "f1n", project=project, final=True)


def stage_mamba(core):
    nc, d = core.nc, core.dram
    R = 64
    H2 = INNER // P
    with scope(core, "m") as (sb, psum):
        col = sb("col", [P, H2, 12])
        alog = sb("alog", [P, H2, DS])
        sz = sb("sz", [P, H2, T])
        u = sb("u", [P, H2, T])
        dt = sb("dt", [P, H2, T])
        bc3 = sb("bc3", [96, T], BF16)
        wout = sb("wout", [P, H2, D])
        bout = sb("bout", [T2, D])
        BIAS_U, BIAS_Z, CONV_B, DT_B, DT_B2, SKIP, TAP = 0, 1, 2, 3, 4, 5, 6
        with scope(core, "mi") as (sb2, _):
            xnT = sb2("xnT", [D, T])
            scale = sb2("scale", [D, 1])
            win = sb2("win", [D, 2 * INNER])
            wdt_in = sb2("wdt_in", [P, H2, R])
            wdt_out = sb2("wdt_out", [R, INNER])
            dtb = sb2("dtb", [R, 1])
            wbc = sb2("wbc", [P, H2, 96])
            bcb = sb2("bcb", [96, 1])
            loads = core.sem("mi_loads")
            with nc.Block() as block:
                @block.vector
                def _(ve):
                    ve.memset(wbc[:, :, :], 0.0)

                @block.sync
                def _(sp):
                    for dst, src in ((col[:, :, :], d["L1_attn_channels"].rearrange("(h p) k -> p h k", p=P)),
                                     (alog[:, :, :], d["L1_attn_a_log"].rearrange("(h p) s -> p h s", p=P)),
                                     (scale[:, :], d["L1_attn_norm_scale"].rearrange("(p a) -> p a", a=1)),
                                     (win[:, :], d["L1_attn_in_proj_w"]),
                                     (wdt_in[:, :, :], d["L1_attn_dt_in_w"].rearrange("(h p) r -> p h r", p=P)),
                                     (wdt_out[:, :], d["L1_attn_dt_out_w"]),
                                     (dtb[:, :], d["L1_attn_dt_in_b"].rearrange("(p a) -> p a", a=1)),
                                     (wout[:, :, :], d["L1_attn_out_proj_w"].rearrange("(h p) o -> p h o", p=P)),
                                     (bout[:, :], d["L1_attn_out_proj_b"].partition_broadcast(T2))):
                        sp.dma_start(dst, src).then_inc(loads, 16)
                    sp.wait_ge(loads, 9 * 16)
            with nc.Block() as block:
                @block.sync
                def _(sp):
                    for p in range(3):
                        for k, w in enumerate(("b", "c")):
                            at = slice(32 * p + DS * k, 32 * p + DS * (k + 1))
                            sp.dma_start(wbc[:, :, at], d[f"L1_attn_{w}_proj_w"].rearrange("(h p) s -> p h s", p=P)).then_inc(loads, 16)
                            sp.dma_start(bcb[at, :], d[f"L1_attn_{w}_proj_b"].rearrange("(p a) -> p a", a=1)).then_inc(loads, 16)
                    sp.wait_ge(loads, 21 * 16)
            stage_norm(core, "min", rms=True, residual=False, gain=scale[:, 0:1], outT=by_batch(xnT))
            TP = L + 3
            pre = sb2("pre", [P, H2, B, TP])
            dtr = sb2("dtr", [R, T])
            ubias = sb2("ubias", [P, H2])
            bc = sb2("bc", [96, T])
            low = sb2("low", [96, T], BF16)
            e1 = sb2("e1", [P, H2, T])
            names = "neg zero bias pu ur conv u pr r pd e low_e squares pbc bc".split()
            s = {n: core.sem(f"mi_{n}") for n in names}
            chain = core.shared("mi_chain")
            real_root, factors = log1p_factors(DT_TOP)
            roots = sb2("roots", [P, 2])
            squares = (pre[:, :, :, :].rearrange("p h b t -> p (h b t)")[:, 0:H2 * T].rearrange("p (h t) -> p h t", h=H2),
                       sb2("square", [P, H2, T]))
            quadratics = [(a, b, squares[m]) for m, (a, _, b) in enumerate(factors)]
            centres = [c for _, c, _ in factors]
            with scope(core, "mip") as (_, psum2), nc.Block() as block:
                ps = psum2("ps", [P, 8, 512])

                @block.gpsimd
                def _(pool):
                    pool.tensor_scalar(bout[:, :], bout[:, :], 0.5, None, ALU.mult).then_inc(s["bias"], 1)
                    pool.wait_ge(s["bias"], 1)
                    pool.tensor_tensor(core.x_tm[:, :, :], core.x_tm[:, :, :], over(bout[:, :].unsqueeze(1), [T2, NT, D]),
                                       ALU.add)

                @block.tensor
                def _(pe):
                    for k in range(2 * H2 * NC):
                        if k >= 8:
                            pe.wait_ge(s["ur"], k - 7)
                        pe.matmul(ps[:, k % 8, 0:CH], win[:, (k // NC) * P:(k // NC + 1) * P],
                                  xnT[:, (k % NC) * CH:(k % NC + 1) * CH], start=True, stop=True).then_inc(s["pu"], 1)
                    pe.wait_ge(s["ur"], 4 * NC)
                    for c in range(NC):
                        cols = slice(c * CH, (c + 1) * CH)
                        pe.wait_ge(s["u"], 2)
                        for h in range(H2):
                            last = pe.matmul(ps[0:R, c, 0:CH], wdt_in[:, h, :], u[:, h, cols], start=(h == 0), stop=(h == 1))
                        last.then_inc(s["pr"], 1)
                    for k in range(H2 * NC):
                        h, c = k // NC, k % NC
                        pe.wait_ge(s["r"], NC)
                        pe.matmul(ps[:, k, 0:CH], wdt_out[:, h * P:(h + 1) * P], dtr[:, c * CH:(c + 1) * CH],
                                  start=True, stop=True).then_inc(s["pd"], 1)
                    for c in range(NC):
                        pe.wait_ge(s["neg"], NC + c + 1)
                        for h in range(H2):
                            last = pe.matmul(ps[0:96, 4 + c, 0:CH], wbc[:, h, :], u[:, h, c * CH:(c + 1) * CH],
                                             start=(h == 0), stop=(h == 1))
                        last.then_inc(s["pbc"], 1)

                @block.scalar
                def _(act):
                    act.wait_ge(s["zero"], 3)
                    for k in range(4 * NC):
                        h, c = (k // NC) % H2, k % NC
                        cols = slice(c * CH, (c + 1) * CH)
                        act.wait_ge(s["pu"], k + 1)
                        if k < 2 * NC:
                            act.activation(pre[:, h, c * BC:(c + 1) * BC, 3:TP],
                                           ps[:, k % 8, 0:CH].rearrange("p (b t) -> p b t", t=L), ACT.Identity,
                                           bias=col[:, h, BIAS_U:BIAS_U + 1]).then_inc(s["ur"], 1)
                        else:
                            act.activation(sz[:, h, cols], ps[:, k % 8, 0:CH], ACT.Silu,
                                           bias=col[:, h, BIAS_Z:BIAS_Z + 1]).then_inc(s["ur"], 1)
                    for h in range(H2):
                        act.wait_ge(s["conv"], 4 * (h + 1))
                        act.activation(u[:, h, :], e1[:, h, :], ACT.Silu, bias=col[:, h, CONV_B:CONV_B + 1]).then_inc(s["u"], 1)
                    for c in range(NC):
                        act.wait_ge(s["pr"], c + 1)
                        act.activation(dtr[:, c * CH:(c + 1) * CH], ps[0:R, c, 0:CH], ACT.Identity, bias=dtb[:, :]).then_inc(s["r"], 1)
                    for k in range(H2 * NC):
                        h, c = k // NC, k % NC
                        act.wait_ge(s["neg"], k + 1)
                        act.activation(e1[:, h, c * CH:(c + 1) * CH], e1[:, h, c * CH:(c + 1) * CH],
                                       ACT.Exp).then_inc(s["e"], 1)
                    act.activation(alog[:, :, :], alog[:, :, :], ACT.Exp)
                    for h in range(H2):
                        act.wait_ge(s["low_e"], h + 1)
                        for m, (scale_of, _, out) in enumerate(quadratics):
                            act.activation(out[:, h, :], e1[:, h, :], ACT.Square, bias=roots[:, m:m + 1],
                                           scale=scale_of).then_inc(s["squares"], 1)
                    for c in range(NC):
                        act.wait_ge(s["pbc"], c + 1)
                        act.activation(bc[:, c * CH:(c + 1) * CH], ps[0:96, 4 + c, 0:CH], ACT.Tanh, bias=bcb[:, :]).then_inc(s["bc"], 1)

                @block.vector
                def _(ve):
                    ve.memset(pre[:, :, :, 0:3], 0.0).then_inc(s["zero"], 1)
                    for m in range(2):
                        ve.memset(roots[:, m:m + 1], centres[m]).then_inc(s["zero"], 1)
                    ve.tensor_tensor(ubias[:, :], col[:, :, DT_B], col[:, :, DT_B2], ALU.add).then_inc(s["zero"], 1)
                    for h in range(H2):
                        out = e1[:, h, :].rearrange("p (b t) -> p b t", t=L)
                        ve.wait_ge(s["ur"], (h + 1) * NC)
                        ve.tensor_scalar(out, pre[:, h, :, 0:L], col[:, h, TAP:TAP + 1], None, ALU.mult).then_inc(s["conv"], 1)
                        for k in range(1, 4):
                            ve.wait_ge(s["conv"], 4 * h + k)
                            ve.scalar_tensor_tensor(out, pre[:, h, :, k:k + L], col[:, h, TAP + k:TAP + k + 1], out,
                                                    ALU.mult, ALU.add).then_inc(s["conv"], 1)
                    ve.wait_ge(s["zero"], 4)
                    ve.wait_ge(s["u"], 2)
                    for k in range(H2 * NC):
                        h, c = k // NC, k % NC
                        ve.wait_ge(s["pd"], k + 1)
                        ve.tensor_scalar(e1[:, h, c * CH:(c + 1) * CH], ps[:, k, 0:CH], ubias[:, h:h + 1], 0.0,
                                         ALU.add, ALU.min).then_inc(s["neg"], 1)
                    for h in range(H2):
                        ve.wait_ge(s["e"], (h + 1) * NC)
                        ve.tensor_scalar(e1[:, h, :], e1[:, h, :], DT_TOP, None, ALU.min).then_inc(s["low_e"], 1)
                    for h in range(H2):
                        ve.wait_ge(s["low_e"], h + 1)
                        ve.scalar_tensor_tensor(dt[:, h, :], e1[:, h, :], real_root, e1[:, h, :], ALU.subtract,
                                                ALU.mult).then_inc(chain.sem, 1)
                    for m, (_, rest, square) in enumerate(quadratics):
                        for h in range(H2):
                            ve.wait_ge(s["squares"], 2 * h + m + 1)
                            ve.wait_ge(chain.sem, chain(2 * m + h + 1))
                            ve.scalar_tensor_tensor(dt[:, h, :], square[:, h, :], rest, dt[:, h, :], ALU.add,
                                                    ALU.mult).then_inc(chain.sem, 1)
                    for h in range(H2):
                        ve.wait_ge(chain.sem, chain(5 + h))
                        ve.tensor_scalar(dt[:, h, :], dt[:, h, :], -0.001, -0.1, ALU.min, ALU.max)
                    chain.base += 6
                    ve.wait_ge(s["bc"], NC)
                    for p in range(3):
                        ve.tensor_copy(low[:, :], bc[:, :]).then_inc(chain.sem, 1)
                        ve.wait_ge(chain.sem, chain(1))
                        ve.tensor_copy(bc3[32 * p:32 * p + 32, :], low[32 * p:32 * p + 32, :])
                        chain.base += 1
                        if p < 2:
                            for q in range(p + 1, 3):
                                one = slice(32 * q, 32 * q + 32)
                                ve.tensor_tensor(bc[one, :], bc[one, :], low[one, :], ALU.subtract).then_inc(chain.sem, 1)
                            chain.base += 2 - p
                            ve.wait_ge(chain.sem, chain(0))

        gT = sb("gT", [P, H2, T])
        dtu = sb("dtu", [P, H2, T])
        NU = 4
        da = sb("da", [P, NU, CH])
        h_in = sb("h_in", [P, NU, CH])
        hs = sb("hs", [P, NU, CH])
        hc = sb("hc", [P, NU, CH])
        bs = sb("bs", [P, 2, CH])
        names = "bcopied dtu decay zeroed wideb widec db scan hc summed out".split()
        s = {n: core.sem(f"ms_{n}") for n in names}
        with scope(core, "msp") as (_, psum2), nc.Block() as block:
            pb, pc = psum2("pb", [P, 2, 512]), psum2("pc", [P, 2, 512])
            py = psum2("py", [P, NC, 512])

            def over_states(eng, step):
                for half in range(H2):
                    n0 = half * DS * NC
                    step(half, 0, n0, 0)
                    with eng.Fori(1, DS - 1) as st:
                        step(half, st, st * NC + n0, None)
                    step(half, DS - 1, n0 + (DS - 1) * NC, DS - 1)

            @block.tensor
            def _(pe):
                def row(st):
                    if isinstance(st, int):
                        return core.selector[:, st, :]
                    return core.selector[:, bass.ds(st, 1), :].rearrange("p a m -> p (a m)")

                def wide_b(st, n, k, first=False):
                    if not first:
                        pe.wait_ge(s["bcopied"], n + k - 1)
                    pe.matmul(pb[:, k % 2, 0:CH], row(st), bc3[:, k * CH:(k + 1) * CH],
                              start=True, stop=True).then_inc(s["wideb"], 1)

                def wide_c(st, n, k, first=False):
                    if not first:
                        pe.wait_ge(s["hc"], n + k - 1)
                    pe.matmul(pc[:, k % 2, 0:CH], row(st + DS), bc3[:, k * CH:(k + 1) * CH],
                              start=True, stop=True).then_inc(s["widec"], 1)

                def add(half, n, k, known):
                    pe.wait_ge(s["hc"], n + k + 1)
                    if known == 0 and half:
                        pe.wait_ge(s["out"], half * NC)
                    pe.matmul(py[:, k, 0:CH], core.ident[:, :], hc[:, k, :], start=(known == 0),
                              stop=(known == DS - 1)).then_inc(s["summed"], 1)

                pe.sem_inc(s["summed"])
                for k in range(NC):
                    wide_b(0, 0, k, first=(k < 2))
                wide_c(0, 0, 0, first=True)
                wide_c(0, 0, 1, first=True)

                def step(half, st, n, known):
                    after = None if (half == H2 - 1 and known == DS - 1) else (
                        (0, n + NC) if known == DS - 1 else (st + 1, n + NC))
                    for k in range(NC):
                        if after:
                            wide_b(*after, k)
                        if k < 2:
                            wide_c(st, n, k + 2)
                        elif after:
                            wide_c(*after, k - 2)
                        add(half, n, k, known)
                over_states(pe, step)

            @block.gpsimd
            def _(pool):
                pool.wait_ge(s["dtu"], 1)

                def step(half, st, n, known):
                    if half and known == 0:
                        pool.wait_ge(s["dtu"], 2)
                    for k in range(NC):
                        if not (half == 0 and known == 0):
                            wait_apart(pool, s["scan"], n + k - NC + 1, core.apart)
                        pool.wait_ge(s["bcopied"], n + k + 1)
                        pool.tensor_tensor(h_in[:, k, :], dtu[:, half, k * CH:(k + 1) * CH], bs[:, k % 2, :],
                                           ALU.mult).then_inc(s["db"], 1)
                over_states(pool, step)

            @block.scalar
            def _(act):
                act.wait_ge(s["zeroed"], 1)

                def copy_b(unit, buf, first):
                    if not first:
                        wait_apart(act, s["db"], unit - 1, core.apart)
                    act.wait_ge(s["wideb"], unit + 1)
                    act.activation(bs[:, buf, :], pb[:, buf, 0:CH], ACT.Copy).then_inc(s["bcopied"], 1)

                copy_b(0, 0, first=True)
                copy_b(1, 1, first=True)

                def step(half, st, n, known):
                    for k in range(NC):
                        if not (half == 0 and known == 0):
                            wait_apart(act, s["scan"], n + k - NC + 1, core.apart)
                        a = alog[:, half, st:st + 1] if isinstance(st, int) else alog[:, half, bass.ds(st, 1)]
                        act.activation(da[:, k, :].rearrange("p (b t) -> p b t", t=L)[:, :, 1:L],
                                       dt[:, half, k * CH:(k + 1) * CH].rearrange("p (b t) -> p b t", t=L)[:, :, 1:L],
                                       ACT.Exp, scale=a).then_inc(s["decay"], 1)
                        if not (half == H2 - 1 and known == DS - 1 and k >= 2):
                            copy_b(n + k + 2, k % 2, first=False)
                over_states(act, step)

            @block.vector
            def _(ve):
                ve.memset(da[:, :, 0:CH:L], 0.0).then_inc(s["zeroed"], 1)
                for half in range(H2):
                    ve.scalar_tensor_tensor(dtu[:, half, :], dt[:, half, :], -1.0, u[:, half, :], ALU.mult,
                                            ALU.mult).then_inc(s["dtu"], 1)

                def readout(n, k, known, half):
                    ve.wait_ge(s["scan"], n + 1)
                    if not (known == 0 and half == 0):
                        ve.wait_ge(s["summed"], n - NC + 2)
                    ve.tensor_tensor(hc[:, k, :], hs[:, k, :], pc[:, k % 2, 0:CH], ALU.mult).then_inc(s["hc"], 1)

                def step(half, st, n, known):
                    for k in range(NC):
                        ve.wait_ge(s["decay"], n + k + 1)
                        ve.wait_ge(s["db"], n + k + 1)
                        ve.tensor_tensor_scan(hs[:, k, :], da[:, k, :], h_in[:, k, :], 0.0, ALU.mult,
                                              ALU.add).then_inc(s["scan"], 1)
                        if k:
                            ve.wait_ge(s["widec"], n + k)
                            readout(n + k - 1, k - 1, known, half)
                        elif known != 0:
                            ve.wait_ge(s["widec"], n)
                            readout(n - 1, NC - 1, None, half)
                    if known == DS - 1:
                        ve.wait_ge(s["widec"], n + NC)
                        readout(n + NC - 1, NC - 1, known, half)
                        for k in range(NC):
                            cols = slice(k * CH, (k + 1) * CH)
                            ve.wait_ge(s["summed"], n + k + 2)
                            ve.scalar_tensor_tensor(gT[:, half, cols], u[:, half, cols], col[:, half, SKIP:SKIP + 1],
                                                    py[:, k, 0:CH], ALU.mult, ALU.add).then_inc(s["out"], 1)
                            ve.wait_ge(s["out"], half * NC + k + 1)
                            ve.tensor_tensor(gT[:, half, cols], gT[:, half, cols], sz[:, half, cols], ALU.mult)
                over_states(ve, step)

        def project(pe, n, out):
            for h in range(H2):
                last = pe.matmul(out, gT[:, h, n * T2:(n + 1) * T2], wout[:, h, :], start=(h == 0), stop=(h == H2 - 1))
            return last

        stage_norm(core, "mn", project=project, factor=2.0, outT=by_batch(core.xT))


def log1p_factors(top):
    e = top * (0.5 - 0.5 * np.cos(np.pi * (np.arange(400) + 0.5) / 400))
    poly = np.polynomial.polynomial.polyfit(e, np.log1p(e) / e, 5)
    roots = np.polynomial.polynomial.polyroots(poly)
    real = [float(x.real) for x in roots if abs(x.imag) < 1e-9]
    pairs = [x for x in roots if x.imag > 1e-9]
    assert len(real) == 1 and len(pairs) == 2 and poly[-1] < 0
    a = float(-poly[-1]) ** 0.25
    return real[0], [(a, float(-x.real) * a, float(x.imag * a) ** 2) for x in pairs]


H1, DH1 = 16, 8
HP = H1 // 2
LP = 64


def heads_to_features(core, name, att, aT, bias, out_bias):
    nc = core.nc
    moved, took = core.sem(f"{name}_moved"), core.sem(f"{name}_took")
    with scope(core, name) as (_, psum), nc.Block() as block:
        ps = psum("ps", [P, 2, 512])

        @block.tensor
        def _(pe):
            for b in range(B):
                g, r = b // 4, b % 4
                if g >= 2 and r == 0:
                    pe.wait_ge(took, 2 * (g - 1))
                last = pe.transpose(ps[0:64, g % 2, r * P:(r + 1) * P], att[:, b, :], core.ident[:, :])
                if r == 3:
                    last.then_inc(moved, 1)

        @block.gpsimd
        def _(pool):
            pool.tensor_tensor(core.x_tm[:, :, :], core.x_tm[:, :, :], over(out_bias[:, :].unsqueeze(1), [T2, NT, D]), ALU.add)

        @block.vector
        def _(ve):
            for g in range(B // 4):
                ve.wait_ge(moved, g + 1)
                for h in range(2):
                    dst = aT[h * 64:(h + 1) * 64, g * 4 * L:(g + 1) * 4 * L].rearrange("p (b t) -> p b t", t=L)
                    src = ps[0:64, g % 2, :].rearrange("p (b h t) -> p h b t", b=4, h=2)[:, h, :, 0:L]
                    if bias is None:
                        ve.tensor_copy(dst, src).then_inc(took, 1)
                    else:
                        ve.tensor_scalar(dst, src, bias[:, h:h + 1], None, ALU.add).then_inc(took, 1)


def stage_causal(core):
    nc, d = core.nc, core.dram
    with scope(core, "c") as (sb, psum):
        wp = sb("wp", [P, D])
        bp = sb("bp", [T2, D])
        bv = sb("bv", [64, 2])
        att = sb("att", [P, B, 64])
        aT = sb("aT", [P, T])
        with scope(core, "cl") as (sb2, psum2):
            wqkv = sb2("wqkv", [D, 3, D])
            bqk = sb2("bqk", [D, 2])
            cT = sb2("cT", [D, T])
            qT, kT = sb2("qT", [D, T]), sb2("kT", [D, T])
            v1 = sb2("v1", [P, B, H1, DH1 + 1])
            head = sb2("head", [D, H1])
            causal = sb2("causal", [P, L])
            qblk = sb2("qblk", [D, 2, H1, LP])
            sc = sb2("sc", [P, 2, HP, L])
            top = sb2("top", [P, 2, HP])
            pT = sb2("pT", [P, HP, P])
            rden = sb2("rden", [P, HP, 2])
            own = sb2("own", [P, HP, 2, DH1 + 1])
            loads, built, pre, got = (core.sem(f"cl_{x}") for x in ("loads", "built", "pre", "got"))
            with scope(core, "cq") as (_, psum3), nc.Block() as block:
                ps = psum3("ps", [P, 8, 512])

                @block.sync
                def _(sp):
                    for dst, src in ((wqkv[:, 0, :], d["L1_xattn_Wq"]), (wqkv[:, 1:3, :], d["L1_xattn_Wkv"].rearrange("i (k o) -> i k o", k=2)),
                                     (bqk[:, :], d["L1_xattn_bqk"]), (cT[:, :], d["ctx_headT"]),
                                     (wp[:, :], d["L1_xattn_Wp_split"]), (bv[:, :], d["L1_xattn_bv_split"]),
                                     (bp[:, :], d["L1_xattn_bp"].partition_broadcast(T2))):
                        sp.dma_start(dst, src).then_inc(loads, 16)
                    sp.wait_ge(loads, 7 * 16)

                @block.gpsimd
                def _(pool):
                    cz = causal[:, :]
                    steps = (lambda: pool.memset(head[:, :], 1.0),
                             lambda: pool.affine_select(out=head[:, :], in_=head[:, :], compare_op=ALU.is_ge, fill=0.0, base=0,
                                                        pattern=[[-DH1, H1]], channel_multiplier=1),
                             lambda: pool.affine_select(out=head[:, :], in_=head[:, :], compare_op=ALU.is_ge, fill=0.0, base=DH1 - 1,
                                                        pattern=[[DH1, H1]], channel_multiplier=-1),
                             lambda: pool.memset(qblk[:, :, :, :], 0.0),
                             lambda: pool.memset(att[:, :, :], 0.0),
                             lambda: pool.memset(v1[:, :, :, :], 0.0),
                             lambda: pool.memset(v1[0:L, :, :, DH1:DH1 + 1], 1.0),
                             lambda: pool.memset(pT[:, :, :], 0.0),
                             lambda: pool.memset(cz, 0.0),
                             lambda: pool.affine_select(out=causal[0:LP, :], in_=causal[0:LP, :], compare_op=ALU.is_ge, fill=NEG,
                                                        base=0, pattern=[[-1, L]], channel_multiplier=1),
                             lambda: pool.affine_select(out=causal[LP:P, :], in_=causal[LP:P, :], compare_op=ALU.is_ge, fill=NEG,
                                                        base=0, pattern=[[-1, L]], channel_multiplier=1))
                    for n, make in enumerate(steps):
                        make().then_inc(built, 1)
                        pool.wait_ge(built, n + 1)

                @block.tensor
                def _(pe):
                    pe.wait_ge(loads, 7 * 16)
                    for k in range(2 * NC):
                        c = k % NC
                        if k >= 4:
                            pe.wait_ge(got, k - 3)
                        pe.matmul(ps[:, k % 4, 0:CH], wqkv[:, k // NC, :], (core.xT, cT)[k // NC][:, c * CH:(c + 1) * CH],
                                  start=True, stop=True).then_inc(pre, 1)
                    for g in range(B // 4):
                        if g >= 4:
                            pe.wait_ge(got, 2 * NC + g - 3)
                        for r in range(4):
                            b = 4 * g + r
                            last = pe.matmul(ps[0:L, 4 + g % 4, r * D:(r + 1) * D], cT[:, b * L:(b + 1) * L], wqkv[:, 2, :],
                                             start=True, stop=True)
                        last.then_inc(pre, 1)

                @block.vector
                def _(ve):
                    ve.wait_ge(loads, 7 * 16)
                    ve.wait_ge(built, 8)
                    for k in range(2 * NC):
                        ve.wait_ge(pre, k + 1)
                        dst = (qT, kT)[k // NC][:, (k % NC) * CH:(k % NC + 1) * CH]
                        ve.tensor_scalar(dst, ps[:, k % 4, 0:CH], bqk[:, k // NC:k // NC + 1], None, ALU.add).then_inc(got, 1)
                    for g in range(B // 4):
                        ve.wait_ge(pre, 2 * NC + g + 1)
                        ve.tensor_copy(v1[0:L, 4 * g:4 * g + 4, :, 0:DH1],
                                       ps[0:L, 4 + g % 4, :].rearrange("p (b h e) -> p b h e", b=4, h=H1)).then_inc(got, 1)

            names = "q raw masked top less probs turned pT val own rden att".split()
            s = {n: core.sem(f"cl_{n}") for n in names}
            SCALE = 1.0 / float(np.sqrt(DH1))
            with scope(core, "clp") as (_, psum3), nc.Block() as block:
                pA, pT2 = psum3("pA", [P, 2, 512]), psum3("pT2", [P, 2, 512])
                VA = H1 * (DH1 + 1)
                pV = psum3("pV", [P, 3, 512])

                def values_at(hp):
                    return hp // 3, slice((hp % 3) * VA, (hp % 3 + 1) * VA)

                def run(eng, step):
                    for n in range(4):
                        step(n, n, n // 2)
                    with eng.Fori(2, B // 2) as i:
                        for j in range(2):
                            step(i * 2 + j, 4 + j, i)
                    for n in range(B, B + 2):
                        step(n, n, n // 2)

                @block.gpsimd
                def _(pool):
                    def step(n, k, pair):
                        if k < B:
                            if k > 1:
                                pool.wait_ge(s["raw"], n - 1)
                            pool.tensor_tensor(qblk[:, k % 2, :, 0:L], over(qT[:, bass.ds(n * L, L)].unsqueeze(1), [D, H1, L]),
                                               over(head[:, :].unsqueeze(2), [D, H1, L]), ALU.mult).then_inc(s["q"], 1)
                    run(pool, step)

                @block.tensor
                def _(pe):
                    def step(n, k, pair):
                        if k < B:
                            pe.wait_ge(s["q"], n + 1)
                            if k:
                                pe.wait_ge(s["masked"], n)
                            for hp in range(HP):
                                last = pe.matmul(pA[:, hp // 4, (hp % 4) * T2:(hp % 4 + 1) * T2],
                                                 qblk[:, k % 2, 2 * hp:2 * hp + 2, :], kT[:, bass.ds(pair * T2, T2)],
                                                 start=True, stop=True)
                            last.then_inc(s["raw"], 1)
                        if k > 1:
                            pe.wait_ge(s["pT"], n - 1)
                            if k > 2:
                                pe.wait_ge(s["att"], n - 2)
                            for hp in range(HP):
                                bank, cols = values_at(hp)
                                last = pe.matmul(pV[:, bank, cols], pT[:, hp, :], v1[:, bass.ds(n - 2, 1), :, :],
                                                 start=True, stop=True)
                            last.then_inc(s["val"], 1)
                        if 1 <= k < B + 1:
                            wait_apart(pe, s["probs"], n, core.apart)
                            for hp in range(HP):
                                last = pe.transpose(pT2[0:L, hp // 4, (hp % 4) * P:(hp % 4 + 1) * P], sc[:, (k - 1) % 2, hp, :],
                                                    core.ident[:, :])
                            last.then_inc(s["turned"], 1)
                    run(pe, step)

                @block.scalar
                def _(act):
                    def step(n, k, pair):
                        if 1 <= k < B + 1:
                            act.wait_ge(s["turned"], n)
                            if k > 1:
                                act.wait_ge(s["val"], n - 1)
                            act.activation(pT[0:L, :, :].rearrange("p (g h) q -> p g (h q)", g=2), pT2[0:L, :, :],
                                           ACT.Copy).then_inc(s["pT"], 1)
                        if k < B:
                            act.wait_ge(s["less"], n + 1)
                            act.activation(sc[:, k % 2, :, :], sc[:, k % 2, :, :], ACT.Exp, scale=SCALE).then_inc(s["probs"], 1)
                    run(act, step)

                @block.vector
                def _(ve):
                    def step(n, k, pair):
                        if k < B:
                            buf = k % 2
                            ve.wait_ge(s["raw"], n + 1)
                            if k > 1:
                                ve.wait_ge(s["turned"], n - 1)
                            for g in range(2):
                                last = ve.tensor_tensor(sc[:, buf, 4 * g:4 * g + 4, :],
                                                        pA[:, g, 0:4 * T2].rearrange("p (h j t) -> p h j t", h=4, j=2)[:, :, k % 2, :],
                                                        over(causal[:, :].unsqueeze(1), [P, 4, L]), ALU.add)
                            last.then_inc(s["masked"], 1)
                            ve.wait_ge(s["masked"], n + 1)
                            ve.tensor_reduce(top[:, buf, :], sc[:, buf, :, :], AX, ALU.max).then_inc(s["top"], 1)
                        if k > 1:
                            ve.wait_ge(s["val"], n - 1)
                            for hp in range(HP):
                                bank, cols = values_at(hp)
                                pair_of = pV[:, bank, cols].rearrange("p (h k e) -> p h k e", k=2, e=DH1 + 1)[:, hp]
                                last = ve.tensor_copy(own[:, hp, :, :], pair_of)
                            last.then_inc(s["own"], 1)
                            ve.wait_ge(s["own"], n - 1)
                            ve.reciprocal(rden[:, :, :], own[:, :, :, DH1]).then_inc(s["rden"], 1)
                        if k < B:
                            ve.wait_ge(s["top"], n + 1)
                            ve.tensor_tensor(sc[:, buf, :, :], sc[:, buf, :, :], over(top[:, buf, :].unsqueeze(2), [P, HP, L]),
                                             ALU.subtract).then_inc(s["less"], 1)
                        if k > 1:
                            ve.wait_ge(s["rden"], n - 1)
                            for par in range(2):
                                rows = slice(par * LP, par * LP + L)
                                last = ve.tensor_tensor(att[rows, bass.ds(n - 2, 1), :].rearrange("p a (h e) -> p (a h) e", e=DH1),
                                                        own[rows, :, par, 0:DH1], over(rden[rows, :, par].unsqueeze(2), [L, HP, DH1]),
                                                        ALU.mult)
                            last.then_inc(s["att"], 1)
                    run(ve, step)

        heads_to_features(core, "ch", att, aT, bv, bp)

        def project(pe, n, out):
            return pe.matmul(out, aT[:, n * T2:(n + 1) * T2], wp[:, :], start=True, stop=True)

        stage_norm(core, "cn", project=project, outT=by_batch(core.xT))



def program(nc, dram, out):
    with ExitStack() as ctx:
        core = Core(nc, dram, out, ctx)
        stage_constants(core)
        for stage in (stage_scan, stage_attention, stage_experts0, stage_mamba, stage_causal, stage_experts1):
            stage(core)


_HOST = {
    "L0_ffn_router_wT": lambda i: i["L0_ffn_router_w"].T,
    "L1_ffn_gate_weightT": lambda i: i["L1_ffn_gate_weight"].T,
    "L1_ffn_gate_projT": lambda i: i["L1_ffn_gate_proj"].reshape(-1, D).T,
    "L1_ffn_up_projT": lambda i: i["L1_ffn_up_proj"].reshape(-1, D).T,
    "L1_ffn_down_projT": lambda i: i["L1_ffn_down_proj"].transpose(0, 2, 1).reshape(-1, D),
    "L1_attn_channels": lambda i: np.concatenate([_channels(i), i["L1_attn_conv_kernel"].T,
                                                  np.zeros((INNER, 2), np.float32)], axis=1),
    "L1_xattn_bqk": lambda i: np.stack([i["L1_xattn_bq"], i["L1_xattn_bkv"][:D]], axis=1),
    "L1_xattn_Wp_split": lambda i: i["L1_xattn_Wp"].reshape(8, 2, 8, D).transpose(1, 0, 2, 3).reshape(P, D),
    "L1_xattn_bv_split": lambda i: i["L1_xattn_bkv"][D:].reshape(8, 2, 8).transpose(0, 2, 1).reshape(64, 2),
    "ctx_headT": lambda i: i["ctx_1024"][:, :L].transpose(2, 0, 1).reshape(D, T),
    "L0_xattn_ln": lambda i: _stack(i, "L0_xattn_ln_x_g", "L0_xattn_ln_x_b", "L0_xattn_ln_l_g", "L0_xattn_ln_l_b"),
    "L0_attn_in_proj_wT": lambda i: i["L0_attn_in_proj_w"].T,
    "L0_attn_ln": lambda i: _stack(i, "L0_attn_ln_w", "L0_attn_ln_b"),
    "L0_attn_out_proj_wT": lambda i: i["L0_attn_out_proj_w"].T,
}
_PLAIN = ["mask_BxS2_bk0", "L0_ffn_w1", "L0_ffn_w2", "L1_ffn_e_score_correction_bias", "L1_attn_a_log", "L1_attn_norm_scale",
          "L1_attn_in_proj_w", "L1_attn_dt_in_w", "L1_attn_dt_out_w", "L1_attn_dt_in_b", "L1_attn_out_proj_w",
          "L1_attn_out_proj_b", "L1_attn_b_proj_w", "L1_attn_c_proj_w", "L1_attn_b_proj_b", "L1_attn_c_proj_b",
          "L1_xattn_Wq", "L1_xattn_Wkv", "L1_xattn_bp",
          "ctx_1024", "L0_xattn_q_gamma", "L0_xattn_k_gamma", "L0_xattn_W_q", "L0_xattn_W_kv", "L0_xattn_W_out",
          "L0_xattn_b_out",
          "x", "L0_attn_A_log", "L0_attn_B_mat", "L0_attn_C_mat"]


def _channels(i):
    b = i["L1_attn_in_proj_b"]
    return np.stack([b[:INNER], b[INNER:], i["L1_attn_conv_bias"], i["L1_attn_dt_out_b"], i["L1_attn_dt_bias"],
                     i["L1_attn_d"]], axis=1)


def _stack(i, *names):
    return np.stack([np.asarray(i[n]) for n in names], axis=1)


def kernel(**inputs):
    import concourse.bacc as _bacc
    from concourse.bass_utils import run_bass_kernel_spmd as _run

    inputs = {k: np.asarray(v) for k, v in inputs.items()}
    laid = {n: inputs[n] for n in _PLAIN} | {n: f(inputs) for n, f in _HOST.items()}
    nc = _bacc.Bacc("TRN2", target_bir_lowering=False, num_devices=1)
    arrays, dram = {}, {}
    for name, a in laid.items():
        a = np.ascontiguousarray(a)
        arrays[f"in_{name}"] = a
        dram[name] = nc.dram_tensor(f"in_{name}", a.shape, mybir.dt.from_np(a.dtype), kind="ExternalInput").ap()
    out = nc.dram_tensor("out_dram", (B, L, D), F32, kind="ExternalOutput").ap()
    program(nc, dram, out)
    r = _run(nc, [arrays], core_ids=[0])
    return r.results[0]["out_dram"]
```
